# Optimizing a Trainium2 kernel written in Bass

```python
import numpy as np
import jax
import jax.numpy as jnp

def _softmax(x, axis=-1):
    return jax.nn.softmax(x, axis=axis)

def _gelu(x):
    return jax.nn.gelu(x, approximate=True)

def _silu(x):
    return jax.nn.silu(x)

def _sigmoid(x):
    return jax.nn.sigmoid(x)

def _layernorm(x, axis=-1, eps=1e-05):
    m = jnp.mean(x, axis=axis, keepdims=True)
    v = jnp.var(x, axis=axis, keepdims=True)
    return (x - m) / jnp.sqrt(v + eps)

def _scatter_add(tgt, idx, src, axis=0):
    return tgt.at[idx].add(src)

def _segment_sum(src, seg, n):
    return jax.ops.segment_sum(src, seg, n)
kernel_name = 'mk_gnn_ffn_d1_gnn_r8_7e8b4e'

def setup_inputs(seed: int=0):
    np.random.seed(seed)
    _w = jnp.asarray

    def _rec_inputs():
        import jax
        import jax.numpy as jnp
        _gk = jax.random.key(seed)
        x = -0.0002117 + 1 * jax.random.normal(jax.random.fold_in(_gk, 1), (6250, 256), jnp.float32)
        src = jax.random.randint(jax.random.fold_in(_gk, 2), (200000,), 0, 6250, jnp.int32)
        dst = jnp.minimum((6250 * jax.random.uniform(jax.random.fold_in(_gk, 3), (200000,)) ** 2.0).astype(jnp.int32), 49999)
        _o = jnp.argsort(dst, stable=True)
        src = src[_o]
        dst = dst[_o]
        return (x, src, dst)
    x, src, dst = _rec_inputs()

    def _L0_gnn_setup():
        import jax, jax.numpy as jnp
        import numpy as np
        N_NODES = 12500
        N_EDGES = 40000
        D_IN = 256
        D_H = 256
        D_OUT = 256

        def gcn_layer(x, W, b, src, dst, num_nodes):
            ones = jnp.ones(src.shape[0], dtype=x.dtype)
            deg = jax.ops.segment_sum(ones, dst, num_segments=num_nodes)
            dinv = jnp.where(deg > 0, jax.lax.rsqrt(deg), 0.0)
            norm = dinv[src] * dinv[dst]
            h = x @ W
            msg = h[src] * norm[:, None]
            out = jax.ops.segment_sum(msg, dst, num_segments=num_nodes)
            return out + b
        key = jax.random.key(seed)
        ks = jax.random.split(key, 8)
        x = jax.random.normal(ks[0], (N_NODES, D_IN), dtype=jnp.float32)
        edge_index = jax.random.randint(ks[1], (2, N_EDGES), 0, N_NODES, dtype=jnp.int64)

        def glorot(k, fan_in, fan_out):
            s = jnp.sqrt(6.0 / (fan_in + fan_out)).astype(jnp.float32)
            return jax.random.uniform(k, (fan_in, fan_out), jnp.float32, -s, s)
        return {'x': x, 'edge_index': edge_index, 'W1': glorot(ks[2], D_IN, D_H), 'b1': jnp.zeros((D_H,), jnp.float32), 'W2': glorot(ks[3], D_H, D_H), 'b2': jnp.zeros((D_H,), jnp.float32), 'W3': glorot(ks[4], D_H, D_OUT), 'b3': jnp.zeros((D_OUT,), jnp.float32)}
    _L0_gnn_all = _L0_gnn_setup()
    _L0_gnn_in = {k: v for k, v in _L0_gnn_all.items() if k in ('W1', 'b1', 'W2', 'b2', 'W3', 'b3')}
    del _L0_gnn_all

    def _L0_ffn_setup():
        import jax, jax.numpy as jnp
        import numpy as np
        B, N, D = (16, 512, 256)
        NUM_EXPERTS, TOP_K, HEADS = (4, 2, 4)
        N_EDGES = 131072
        LN_EPS = 1e-05

        def _layernorm(x, g, b):
            mu = x.mean(-1, keepdims=True)
            var = ((x - mu) ** 2).mean(-1, keepdims=True)
            return (x - mu) * jax.lax.rsqrt(var + LN_EPS) * g + b

        def _forward(x, edge_index, W_gat, att_src, att_dst, b_gat, ln_gamma, ln_beta, W1, b1, W2, b2):
            Bc, Nc, Dc = x.shape
            M = Bc * Nc
            x_flat = x.reshape(M, Dc)
            h = (x_flat @ W_gat).reshape(M, HEADS, NUM_EXPERTS)
            loops = jnp.arange(M, dtype=edge_index.dtype)
            src = jnp.concatenate([edge_index[0], loops])
            dst = jnp.concatenate([edge_index[1], loops])
            a_src = (h * att_src).sum(-1)
            a_dst = (h * att_dst).sum(-1)
            e = jax.nn.leaky_relu(a_src[src] + a_dst[dst], negative_slope=0.2)
            e_max = jax.ops.segment_max(e, dst, num_segments=M)
            ee = jnp.exp(e - e_max[dst])
            denom = jax.ops.segment_sum(ee, dst, num_segments=M)
            alpha = ee / (denom[dst] + 1e-16)
            msg = h[src] * alpha[:, :, None]
            agg = jax.ops.segment_sum(msg, dst, num_segments=M).reshape(M, HEADS * NUM_EXPERTS) + b_gat
            scores = _layernorm(agg, ln_gamma, ln_beta).reshape(M, HEADS, NUM_EXPERTS).mean(1)
            scores = scores.reshape(Bc, Nc, NUM_EXPERTS)
            topk_s, topk_i = jax.lax.top_k(scores, TOP_K)
            w = jax.nn.softmax(topk_s, axis=-1)
            out = jnp.zeros_like(x)
            for ei in range(NUM_EXPERTS):
                g = jnp.where(topk_i == ei, w, 0.0).sum(-1)
                hh = jax.nn.gelu(x @ W1[ei] + b1[ei], approximate=False)
                out = out + g[..., None] * (hh @ W2[ei] + b2[ei])
            return out
        key = jax.random.key(seed)
        ks = jax.random.split(key, 8)
        s = 0.05
        return {'x': jax.random.normal(ks[0], (B, N, D), jnp.float32), 'W_gat': jax.random.normal(ks[1], (D, HEADS * NUM_EXPERTS), jnp.float32) * s, 'att_src': jax.random.normal(ks[2], (HEADS, NUM_EXPERTS), jnp.float32) * s, 'att_dst': jax.random.normal(ks[3], (HEADS, NUM_EXPERTS), jnp.float32) * s, 'b_gat': jnp.zeros((HEADS * NUM_EXPERTS,), jnp.float32), 'ln_gamma': jnp.ones((HEADS * NUM_EXPERTS,), jnp.float32), 'ln_beta': jnp.zeros((HEADS * NUM_EXPERTS,), jnp.float32), 'W1': jax.random.normal(ks[4], (NUM_EXPERTS, D, 2 * D), jnp.float32) * s, 'b1': jnp.zeros((NUM_EXPERTS, 2 * D), jnp.float32), 'W2': jax.random.normal(ks[5], (NUM_EXPERTS, 2 * D, D), jnp.float32) * s, 'b2': jnp.zeros((NUM_EXPERTS, D), jnp.float32), 'edge_index': jax.random.randint(ks[6], (2, N_EDGES), 0, B * N, jnp.int32)}
    _L0_ffn_all = _L0_ffn_setup()
    _L0_ffn_in = {k: v for k, v in _L0_ffn_all.items() if k in ('W_gat', 'att_src', 'att_dst', 'b_gat', 'ln_gamma', 'ln_beta', 'W1', 'b1', 'W2', 'b2', 'edge_index')}
    del _L0_ffn_all
    return {'x': x, 'src': src, 'dst': dst, 'L0_gnn_W1': _L0_gnn_in['W1'], 'L0_gnn_b1': _L0_gnn_in['b1'], 'L0_gnn_W2': _L0_gnn_in['W2'], 'L0_gnn_b2': _L0_gnn_in['b2'], 'L0_gnn_W3': _L0_gnn_in['W3'], 'L0_gnn_b3': _L0_gnn_in['b3'], 'L0_ffn_W_gat': _L0_ffn_in['W_gat'], 'L0_ffn_att_src': _L0_ffn_in['att_src'], 'L0_ffn_att_dst': _L0_ffn_in['att_dst'], 'L0_ffn_b_gat': _L0_ffn_in['b_gat'], 'L0_ffn_ln_gamma': _L0_ffn_in['ln_gamma'], 'L0_ffn_ln_beta': _L0_ffn_in['ln_beta'], 'L0_ffn_W1': _L0_ffn_in['W1'], 'L0_ffn_b1': _L0_ffn_in['b1'], 'L0_ffn_W2': _L0_ffn_in['W2'], 'L0_ffn_b2': _L0_ffn_in['b2'], 'L0_ffn_edge_index': _L0_ffn_in['edge_index']}

def reference(x, src, dst, L0_gnn_W1, L0_gnn_b1, L0_gnn_W2, L0_gnn_b2, L0_gnn_W3, L0_gnn_b3, L0_ffn_W_gat, L0_ffn_att_src, L0_ffn_att_dst, L0_ffn_b_gat, L0_ffn_ln_gamma, L0_ffn_ln_beta, L0_ffn_W1, L0_ffn_b1, L0_ffn_W2, L0_ffn_b2, L0_ffn_edge_index):
    import jax
    import jax.numpy as jnp

    def _L0_gnn_ref(x, edge_index, W1, b1, W2, b2, W3, b3):
        import jax, jax.numpy as jnp
        import numpy as np
        N_NODES = 12500
        N_EDGES = 40000
        D_IN = 256
        D_H = 256
        D_OUT = 256

        def gcn_layer(x, W, b, src, dst, num_nodes):
            ones = jnp.ones(src.shape[0], dtype=x.dtype)
            deg = jax.ops.segment_sum(ones, dst, num_segments=num_nodes)
            dinv = jnp.where(deg > 0, jax.lax.rsqrt(deg), 0.0)
            norm = dinv[src] * dinv[dst]
            h = x @ W
            msg = h[src] * norm[:, None]
            out = jax.ops.segment_sum(msg, dst, num_segments=num_nodes)
            return out + b
        num_nodes = x.shape[0]
        loop = jnp.arange(num_nodes, dtype=edge_index.dtype)
        src = jnp.concatenate([edge_index[0], loop])
        dst = jnp.concatenate([edge_index[1], loop])
        h = gcn_layer(x, W1, b1, src, dst, num_nodes)
        h = gcn_layer(h, W2, b2, src, dst, num_nodes)
        h = gcn_layer(h, W3, b3, src, dst, num_nodes)
        return h

    def _L0_ffn_ref(x, W_gat, att_src, att_dst, b_gat, ln_gamma, ln_beta, W1, b1, W2, b2, edge_index):
        import jax, jax.numpy as jnp
        import numpy as np
        B, N, D = (16, 512, 256)
        NUM_EXPERTS, TOP_K, HEADS = (4, 2, 4)
        N_EDGES = 131072
        LN_EPS = 1e-05

        def _layernorm(x, g, b):
            mu = x.mean(-1, keepdims=True)
            var = ((x - mu) ** 2).mean(-1, keepdims=True)
            return (x - mu) * jax.lax.rsqrt(var + LN_EPS) * g + b

        def _forward(x, edge_index, W_gat, att_src, att_dst, b_gat, ln_gamma, ln_beta, W1, b1, W2, b2):
            Bc, Nc, Dc = x.shape
            M = Bc * Nc
            x_flat = x.reshape(M, Dc)
            h = (x_flat @ W_gat).reshape(M, HEADS, NUM_EXPERTS)
            loops = jnp.arange(M, dtype=edge_index.dtype)
            src = jnp.concatenate([edge_index[0], loops])
            dst = jnp.concatenate([edge_index[1], loops])
            a_src = (h * att_src).sum(-1)
            a_dst = (h * att_dst).sum(-1)
            e = jax.nn.leaky_relu(a_src[src] + a_dst[dst], negative_slope=0.2)
            e_max = jax.ops.segment_max(e, dst, num_segments=M)
            ee = jnp.exp(e - e_max[dst])
            denom = jax.ops.segment_sum(ee, dst, num_segments=M)
            alpha = ee / (denom[dst] + 1e-16)
            msg = h[src] * alpha[:, :, None]
            agg = jax.ops.segment_sum(msg, dst, num_segments=M).reshape(M, HEADS * NUM_EXPERTS) + b_gat
            scores = _layernorm(agg, ln_gamma, ln_beta).reshape(M, HEADS, NUM_EXPERTS).mean(1)
            scores = scores.reshape(Bc, Nc, NUM_EXPERTS)
            topk_s, topk_i = jax.lax.top_k(scores, TOP_K)
            w = jax.nn.softmax(topk_s, axis=-1)
            out = jnp.zeros_like(x)
            for ei in range(NUM_EXPERTS):
                g = jnp.where(topk_i == ei, w, 0.0).sum(-1)
                hh = jax.nn.gelu(x @ W1[ei] + b1[ei], approximate=False)
                out = out + g[..., None] * (hh @ W2[ei] + b2[ei])
            return out
        return _forward(x, edge_index, W_gat, att_src, att_dst, b_gat, ln_gamma, ln_beta, W1, b1, W2, b2)
    edge_index = jnp.stack([src, dst])
    x = x + _L0_gnn_ref(_layernorm(x, axis=-1), edge_index, L0_gnn_W1, L0_gnn_b1, L0_gnn_W2, L0_gnn_b2, L0_gnn_W3, L0_gnn_b3)
    x = x + _L0_ffn_ref(_layernorm(x, axis=-1)[None], L0_ffn_W_gat, L0_ffn_att_src, L0_ffn_att_dst, L0_ffn_b_gat, L0_ffn_ln_gamma, L0_ffn_ln_beta, L0_ffn_W1, L0_ffn_b1, L0_ffn_W2, L0_ffn_b2, L0_ffn_edge_index)[0]
    return x

_drawn_inputs = setup_inputs


def setup_inputs(seed=0):
    import zlib

    import numpy as np

    out = dict(_drawn_inputs(seed))
    spreads = {'L0_gnn_b1': (0.0, 0.1),
     'L0_gnn_b2': (0.0, 0.1),
     'L0_gnn_b3': (0.0, 0.1),
     'L0_ffn_b_gat': (0.0, 0.1),
     'L0_ffn_ln_gamma': (1.0, 0.2),
     'L0_ffn_ln_beta': (0.0, 0.1),
     'L0_ffn_b1': (0.0, 0.1),
     'L0_ffn_b2': (0.0, 0.1)}
    factors = {}
    for name, (base, spread) in spreads.items():
        noise = np.random.default_rng([zlib.crc32(name.encode()), seed]).standard_normal(out[name].shape)
        drawn = base * np.exp(spread * noise) if base else spread * noise
        out[name] = jnp.asarray(drawn.astype(out[name].dtype))
    for name, factor in factors.items():
        out[name] = (out[name] * factor).astype(out[name].dtype)
    return out
```

```python
import concourse.bass as bass
from concourse import mybir
from contextlib import ExitStack, contextmanager


class Steps:

    def __init__(self, sem):
        self.sem, self.n, self.base, self.k, self.per = sem, 0, 0, None, 0

    def enter(self, k, per):
        if isinstance(k, int):
            self.k = None
            return
        self.k, self.per, self.i = k, per, 0

    def leave(self, turns):
        if self.k is not None:
            assert self.i == self.per, (self.i, self.per)
            self.n += turns * self.per
            self.k = None

    def done(self, ins, eng):
        ins.then_inc(self.sem, 1)
        if self.k is None:
            self.n += 1
            eng.wait_ge(self.sem, self.n)
        else:
            self.i += 1
            eng.wait_ge(self.sem, (self.k - 1) * self.per + (self.n + self.i))


def wait(eng, sem, value):
    if isinstance(value, int) and value <= 0:
        return
    eng.wait_ge(sem, value)


def turns(eng, count, body, steps=(), per=()):
    body(0)
    if count > 1:
        with eng.Fori(1, count) as k:
            for s, p in zip(steps, per):
                s.enter(k, p)
            body(k)
        for s in steps:
            s.leave(count - 1)


def gnn_moe_kernel(nc, x, src, dst, gW, gb, W_gat, att_src, att_dst, b_gat, ln_g, ln_b,
                   W1, b1, W2, b2, edges, out):
    f32, bf16 = mybir.dt.float32, mybir.dt.bfloat16
    i32, u32 = mybir.dt.int32, mybir.dt.uint32
    ALU, ACT, AX = mybir.AluOpType, mybir.ActivationFunctionType, mybir.AxisListType
    P = 128

    N, D = x.shape
    NB = -(-N // P)
    NP = NB * P
    E1, E2 = src.shape[0], edges.shape[1]
    NE, _, F = W1.shape
    H = att_src.shape[0]
    HE = H * NE
    KD, FC = D // P, F // P
    EPS = 1e-5
    U = 8
    RING = 2 * U
    C1 = -(-(-(-E1 // P)) // RING) * RING
    C2 = -(-(-(-E2 // P)) // RING) * RING
    S1 = -(-((E1 + NB * (P - 1)) // P) // RING) * RING
    S2 = C2
    assert E2 == P * C2 and NB % 7 == 0
    INVALID = 8192
    SKIP = float(1 << 20)
    BIG = 1e30
    G7 = NB // 7

    sorted1 = nc.dram_tensor("sorted1", (P * S1, 4), f32).ap()
    sorted2 = nc.dram_tensor("sorted2", (P * S2 + 1, 4), f32).ap()
    chunk_dram = nc.dram_tensor("chunk_block", (-(-S1 // P) * P,), i32).ap()
    table = nc.dram_tensor("table", (NP, D), f32).ap()
    x1_dram = nc.dram_tensor("x1_dram", (NP, D), f32).ap()
    xT_dram = nc.dram_tensor("xT_dram", (P, KD, NP), f32).ap()
    TW = 32
    table2 = nc.dram_tensor("table2", (NP, TW), f32).ap()
    maxes = nc.dram_tensor("maxes", (P * S2, H), f32).ap()
    spread = nc.dram_tensor("spread", (P * S2, 2 * H), f32).ap()
    sums = nc.dram_tensor("sums", (P * S2, HE + H), f32).ap()

    ctx = ExitStack()
    with ctx:
        def sb(name, shape, dt=f32):
            return ctx.enter_context(nc.sbuf_tensor(name, shape, dt))

        def kept_sem(name):
            return ctx.enter_context(nc.semaphore(name))

        scope, names_made = [], []

        def sem(name):
            names_made.append(name)
            scope[-1].append(nc.alloc_semaphore(name=f"{name}_{names_made.count(name)}"))
            return scope[-1][-1]

        @contextmanager
        def stage_of():
            scope.append([])
            with nc.Block() as block:
                yield block
            nc.clear_and_free_semaphores(scope.pop())
            nc.all_engine_barrier()

        iota_row = sb("iota_row", [P, P])
        iota_col = sb("iota_col", [P, 1])
        iota_bf = sb("iota_bf", [P, P], bf16)
        ident = sb("ident", [P, P])
        ident_bf = sb("ident_bf", [P, P], bf16)
        before = sb("before", [P, P])
        after = sb("after", [P, P])
        ones = sb("ones", [P, P])
        iota_i = sb("iota_i", [P, P], i32)
        iota_pi = sb("iota_pi", [P, 1], i32)
        counts = [sb(f"counts{g}", [P, NB]) for g in range(2)]
        starts = [sb(f"starts{g}", [P, NB]) for g in range(2)]
        dinv = sb("dinv", [P, NB])
        small = sb("small", [P, 8, NB])
        small_i = sb("small_i", [P, 2, NB], i32)
        node_feat = sb("node_feat", [P, NB, 24])
        gates = sb("gates", [P, NB, NE])
        ARENA = 45 * 1024
        arena = sb("arena", [P, ARENA])
        psum = ctx.enter_context(nc.psum_tensor("psum", [P, 8, 512], f32))

        class Place:

            def __init__(self):
                self.at = 0

            def __call__(self, shape, dt=f32):
                n = 1
                for s in shape:
                    n *= s
                words = n if dt != bf16 else -(-n // 2)
                words = -(-words // 8) * 8
                v = arena[:, self.at:self.at + words]
                self.at += words
                assert self.at <= ARENA, self.at
                if dt != f32:
                    v = v.bitcast(dt)
                v = v[:, 0:n]
                if len(shape) == 2:
                    v = v.rearrange("p (a b) -> p a b", b=shape[1])
                elif len(shape) == 3:
                    v = v.rearrange("p (a b c) -> p a b c", b=shape[1], c=shape[2])
                return v

        dve_step = Steps(kept_sem("dve_step"))
        loads = kept_sem("loads")
        loaded = [0]

        def load(eng, to, of):
            eng.dma_start(to, of).then_inc(loads, 16)
            loaded[0] += 16

        with stage_of() as block:
            iotas = sem("iotas")

            @block.gpsimd
            def _(pool):
                pool.iota(iota_i[:, :], pattern=[[1, P]], base=0, channel_multiplier=0).then_inc(iotas, 1)
                pool.iota(iota_pi[:, :], pattern=[[0, 1]], base=0, channel_multiplier=1).then_inc(iotas, 1)

            @block.vector
            def _(dve):
                dve.memset(ones[:, :], 1.0)
                dve.wait_ge(iotas, 2)
                dve.tensor_copy(iota_col[:, :], iota_pi[:, :])
                dve_step.done(dve.tensor_copy(iota_row[:, :], iota_i[:, :]), dve)
                dve.tensor_copy(iota_bf[:, :], iota_row[:, :])
                dve.tensor_scalar(ident[:, :], iota_row[:, :], iota_col[:, :], None, ALU.is_equal)
                dve.tensor_scalar(ident_bf[:, :], iota_row[:, :], iota_col[:, :], None, ALU.is_equal)
                dve.tensor_scalar(before[:, :], iota_row[:, :], iota_col[:, :], None, ALU.is_lt)
                dve_step.done(dve.tensor_scalar(after[:, :], iota_row[:, :], iota_col[:, :], None, ALU.is_gt), dve)

        def sort_edges(g, src_ap, dst_ap, E, C, rows, padded):
            place = Place()
            src_i, dst_i = place([C], i32), place([C], i32)
            key_i, part_i = place([C], i32), place([C], i32)
            cols = place([C, 4])
            stage = place([RING, 4])
            stage_bf = place([RING, 2], bf16)
            hot_lo = place([RING, P], bf16)
            hot_hi = place([RING, NB], bf16)
            hot_loT = place([RING, P])
            place_of = place([2, NB])
            scrap, picked = place([U, P]), place([U, NB])
            rank, looked = place([RING]), place([RING])
            row_f, row_skip = place([RING]), place([RING])
            pos_i, lo_i, hi_i = place([RING], i32), place([RING], i32), place([RING], i32)
            row_u = place([RING], u32)
            FILL = 512
            fill = place([FILL, 4])
            turns_ = C // RING

            hist = psum[:, 0, 0:NB]
            total = psum[:, 1, 0:NB]
            within = psum[:, 2, 0:NB]
            heap = psum[:, 0, 0:NB]
            look = [psum[:, 1 + b, 0:U * NB].rearrange("p (u c) -> p u c", c=NB) for b in range(2)]
            rows_of = psum[:, 3:7, :].rearrange("p b (u t c) -> p (b u) t c", u=2, t=2)

            full = E // C

            with stage_of() as block:
                clean, s_fill, s_filled = sem(f"clean{g}"), sem(f"fill_made{g}"), sem(f"filled{g}")

                @block.sync
                def _(sp):
                    sp.wait_ge(clean, 1)
                    for to, of in ((src_i, src_ap), (dst_i, dst_ap)):
                        load(sp, to[0:full, :], of[0:full * C].rearrange("(p c) -> p c", c=C))
                        if E > full * C:
                            load(sp, to[full:full + 1, 0:E - full * C],
                                 of[full * C:E].rearrange("(a c) -> a c", a=1))
                    sp.wait_ge(s_fill, 1)
                    nrow = rows.shape[0]
                    if nrow % P:
                        sp.dma_start(rows[0:1, :], fill[0:1, 0, :]).then_inc(s_filled, 16)
                    body = rows[nrow % P:nrow, :].rearrange("(p c) f -> p c f", p=P)
                    n = nrow // P
                    at, made = 0, 16 * (nrow % P > 0)
                    while at < n:
                        m = min(FILL, n - at)
                        sp.dma_start(body[:, at:at + m, :], fill[:, 0:m, :]).then_inc(s_filled, 16)
                        at, made = at + m, made + 16
                    sp.wait_ge(s_filled, made)

                want = loaded[0]

                @block.vector
                def _(dve):
                    dve.memset(src_i, 0)
                    dve.memset(dst_i, INVALID - 1).then_inc(clean, 1)
                    dve.memset(fill[:, :, 0:1], 0.0)
                    dve.memset(fill[:, :, 1:2], 2.0 * INVALID)
                    dve.memset(fill[:, :, 2:4], 2.0 * P).then_inc(s_fill, 1)
                    dve.wait_ge(loads, want)
                    dve_step.done(dve.tensor_scalar(key_i, dst_i, float(N), float(INVALID), ALU.is_ge, ALU.mult), dve)
                    dve_step.done(dve.tensor_tensor(key_i, key_i, dst_i, ALU.add), dve)
                    dve.tensor_scalar(cols[:, :, 0:1].rearrange("p c a -> p (c a)"), src_i, float(N - 1), None, ALU.min)
                    dve.tensor_copy(cols[:, :, 1:2].rearrange("p c a -> p (c a)"), key_i)
                    dve_step.done(dve.tensor_scalar(part_i, key_i, P - 1, None, ALU.bitwise_and), dve)
                    dve_step.done(dve.tensor_copy(cols[:, :, 2:3].rearrange("p c a -> p (c a)"), part_i), dve)
                    dve_step.done(dve.tensor_scalar(part_i, key_i, 7, None, ALU.logical_shift_right), dve)
                    dve_step.done(dve.tensor_copy(cols[:, :, 3:4].rearrange("p c a -> p (c a)"), part_i), dve)

            with stage_of() as block:
                staged, hot, counted = sem(f"h_staged{g}"), sem(f"h_hot{g}"), sem(f"h_counted{g}")
                summed = sem(f"h_summed{g}")

                @block.scalar
                def _(act):
                    def body(k):
                        for b in range(2):
                            wait(act, hot, (2 * k + b - 1) * U)
                            act.copy(stage[:, b * U:b * U + U, :], cols[:, bass.ds(k * RING + b * U, U), :]).then_inc(staged, 1)
                    turns(act, turns_, body)

                @block.vector
                def _(dve):
                    def body(k):
                        for b in range(2):
                            dve.wait_ge(staged, 2 * k + b + 1)
                            wait(dve, counted, (2 * k + b - 1) * U)
                            for u in range(b * U, b * U + U):
                                dve.tensor_scalar(hot_lo[:, u, :], iota_bf[:, :], stage[:, u, 2:3], None, ALU.is_equal)
                                dve.tensor_scalar(hot_hi[:, u, :], iota_bf[:, 0:NB], stage[:, u, 3:4], None, ALU.is_equal).then_inc(hot, 1)
                    turns(dve, turns_, body)
                    dve.wait_ge(counted, C)
                    dve.tensor_copy(counts[g][:, :], hist).then_inc(summed, 1)

                @block.tensor
                def _(pe):
                    def body(k):
                        for u in range(RING):
                            pe.wait_ge(hot, k * RING + u + 1)
                            first = isinstance(k, int) and u == 0
                            pe.matmul(hist, hot_lo[:, u, :], hot_hi[:, u, :], start=first, stop=True,
                                      skip_group_check=True).then_inc(counted, 1)
                    turns(pe, turns_, body)
                    pe.wait_ge(summed, 1)
                    pe.matmul(total, ones[:, :], counts[g][:, :], start=True, stop=True)
                    pe.matmul(within, after[:, :], counts[g][:, :], start=True, stop=True).then_inc(summed, 1)

            with stage_of() as block:
                chunks_made, copied = sem(f"chunks{g}"), sem(f"chunk_copied{g}")
                rooted, padded_i = sem(f"rooted{g}"), small_i[:, 0, :]
                CC = -(-S1 // P)

                @block.vector
                def _(dve):
                    size, ends = small[:, 0, :], small[:, 1, :]
                    if padded:
                        dve_step.done(dve.tensor_scalar(padded_i, total, float(P - 1), None, ALU.add), dve)
                        dve_step.done(dve.tensor_scalar(small_i[:, 1, :], padded_i, 7, None, ALU.logical_shift_right), dve)
                        dve_step.done(dve.tensor_scalar(size, small_i[:, 1, :], float(P), None, ALU.mult), dve)
                    else:
                        dve_step.done(dve.tensor_copy(size, total), dve)
                    dve_step.done(dve.tensor_tensor_scan(ends, ones[:, 0:NB], size, 0.0, ALU.mult, ALU.add), dve)
                    dve_step.done(dve.tensor_tensor(small[:, 2, :], ends, size, ALU.subtract), dve)
                    dve_step.done(dve.tensor_tensor(starts[g][:, :], small[:, 2, :], within, ALU.add), dve)
                    if padded:
                        first_of, blocks = scrap[:, 0, 0:CC], scrap[:, 1, 0:CC]
                        dve_step.done(dve.tensor_scalar(first_of, iota_row[:, 0:CC], float(P), iota_col[:, :], ALU.mult, ALU.add), dve)
                        dve_step.done(dve.tensor_scalar(first_of, first_of, float(P), None, ALU.mult), dve)
                        for c in range(CC):
                            dve_step.done(dve.tensor_scalar(small[:, 3, :], ends, first_of[:, c:c + 1], 0.0, ALU.is_le, ALU.add,
                                                            accum_out=blocks[:, c:c + 1]), dve)
                        dve_step.done(dve.tensor_scalar(blocks, blocks, float(NB - 1), None, ALU.min), dve)
                        dve.tensor_copy(pos_i[:, 0:CC], blocks).then_inc(chunks_made, 1)
                        dve_step.done(dve.tensor_scalar(dinv[:, :], counts[g][:, :], 1.0, None, ALU.add), dve)
                        dve.tensor_copy(small[:, 4, :], dinv[:, :]).then_inc(rooted, 1)
                        dve.wait_ge(rooted, 2)
                        dve_step.done(dve.reciprocal(dinv[:, :], small[:, 5, :]), dve)

                if padded:
                    @block.scalar
                    def _(act):
                        act.wait_ge(rooted, 1)
                        act.activation(small[:, 5, :], small[:, 4, :], ACT.Sqrt).then_inc(rooted, 1)

                    @block.sync
                    def _(sp):
                        sp.wait_ge(chunks_made, 1)
                        with nc.allow_non_contiguous_dma("a few words"):
                            sp.dma_start(chunk_dram.rearrange("(c p) -> p c", p=P), pos_i[:, 0:CC]).then_inc(copied, 16)
                        sp.wait_ge(copied, 16)

            with stage_of() as block:
                names = ("staged", "heap_set", "free_set", "rows_made", "hot_made", "rows_used", "looked", "moved", "ranked")
                staged, heap_set, free_set, rows_made, hot_made, rows_used, looked_up, moved, ranked = (
                    sem(f"r_{n}{g}") for n in names)
                scattered = [sem(f"scattered{g}_{b}") for b in range(2)]

                @block.scalar
                def _(act):
                    act.wait_ge(heap_set, 1)
                    act.copy(place_of[:, 0, :], heap).then_inc(free_set, 1)

                    def body(k):
                        for b in range(2):
                            j = 2 * k + b
                            wait(act, scattered[b], k * (16 * U))
                            wait(act, ranked, j - 1)
                            half = slice(b * U, b * U + U)
                            act.copy(stage[:, half, :], cols[:, bass.ds(k * RING + b * U, U), :])
                            act.copy(stage_bf[:, half, 0:1], cols[:, bass.ds(k * RING + b * U, U), 2:3])
                            act.mul(stage_bf[:, half, 1:2], cols[:, bass.ds(k * RING + b * U, U), 3:4], float(P)).then_inc(staged, 1)
                            for u in range(b * U, b * U + U):
                                act.wait_ge(moved, k * RING + u + 1)
                                act.copy(place_of[:, (u + 1) % 2, :], heap).then_inc(free_set, 1)
                    turns(act, turns_, body)

                @block.tensor
                def _(pe):
                    pe.matmul(heap, ident[:, :], starts[g][:, :], start=True, stop=True).then_inc(heap_set, 1)

                    def body(k):
                        for b in range(2):
                            j = 2 * k + b
                            pe.wait_ge(staged, j + 1)
                            wait(pe, rows_used, j)
                            for u in range(U):
                                lo = stage_bf[:, b * U + u, 0:1].to_broadcast([P, P])
                                hi = stage_bf[:, b * U + u, 1:2].to_broadcast([P, P])
                                pe.matmul(rows_of[:, u, 0, :], lo, ident_bf[:, :], start=True, stop=True)
                                pe.matmul(rows_of[:, u, 1, :], hi, ident_bf[:, :], start=True, stop=False)
                                last = pe.matmul(rows_of[:, u, 1, :], lo, ident_bf[:, :], start=False, stop=True)
                                if u % 2:
                                    last.then_inc(rows_made, 1)
                            wait(pe, ranked, j - 1)
                            for u in range(U):
                                n = k * RING + (b * U + u + 1)
                                r = b * U + u
                                pe.wait_ge(hot_made, n)
                                pe.wait_ge(free_set, n)
                                pe.matmul(look[b][:, u, :], hot_loT[:, r, :], place_of[:, r % 2, :], start=True, stop=True).then_inc(looked_up, 1)
                                pe.matmul(heap, hot_lo[:, r, :], hot_hi[:, r, :], start=False, stop=True,
                                          skip_group_check=True).then_inc(moved, 1)
                    turns(pe, turns_, body)

                @block.vector
                def _(dve):
                    def body(k):
                        for b in range(2):
                            j = 2 * k + b
                            half = slice(b * U, b * U + U)
                            dve.wait_ge(staged, j + 1)
                            for u in range(U):
                                r = b * U + u
                                dve.tensor_scalar(hot_lo[:, r, :], iota_bf[:, :], stage[:, r, 2:3], None, ALU.is_equal)
                                dve.tensor_scalar(hot_hi[:, r, :], iota_bf[:, 0:NB], stage[:, r, 3:4], None, ALU.is_equal)
                                if u % 2 == 0:
                                    dve.wait_ge(rows_made, (2 * k + b) * (U // 2) + (u // 2 + 1))
                                dve.tensor_scalar(hot_loT[:, r, :], rows_of[:, u, 0, :], iota_col[:, :], None, ALU.is_equal).then_inc(hot_made, 1)
                                last = dve.scalar_tensor_tensor(scrap[:, u, :], rows_of[:, u, 1, :], stage[:, r, 1:2], before[:, :],
                                                                ALU.is_equal, ALU.mult, accum_out=rank[:, r:r + 1])
                            last.then_inc(rows_used, 1)
                            dve.wait_ge(looked_up, (j + 1) * U)
                            dve_step.done(dve.tensor_tensor(picked, look[b], hot_hi[:, half, :], ALU.mult), dve)
                            dve_step.done(dve.tensor_reduce(looked[:, half], picked, AX.X, ALU.add), dve)
                            dve.tensor_scalar(row_skip[:, half], stage[:, half, 1:2].rearrange("p u a -> p (u a)"), float(INVALID), SKIP,
                                              ALU.is_ge, ALU.mult)
                            if padded:
                                dve_step.done(dve.tensor_tensor(pos_i[:, half], rank[:, half], looked[:, half], ALU.add), dve)
                                dve.tensor_scalar(lo_i[:, half], pos_i[:, half], P - 1, None, ALU.bitwise_and)
                                dve_step.done(dve.tensor_scalar(hi_i[:, half], pos_i[:, half], 7, None, ALU.logical_shift_right), dve)
                                dve_step.done(dve.scalar_tensor_tensor(row_f[:, half], lo_i[:, half], float(S1), hi_i[:, half], ALU.mult, ALU.add), dve)
                            else:
                                dve_step.done(dve.scalar_tensor_tensor(row_f[:, half], rank[:, half], 1.0, looked[:, half], ALU.add, ALU.add), dve)
                            dve.tensor_tensor(row_u[:, half], row_f[:, half], row_skip[:, half], ALU.add).then_inc(ranked, 1)
                    turns(dve, turns_, body, [dve_step], [2 * (5 if padded else 3)])

                @block.gpsimd
                def _(pool):
                    paced = sem("paced")
                    bound = pool.to_reg(rows.shape[0] - 1)

                    def body(k):
                        for b in range(2):
                            pool.wait_ge(ranked, 2 * k + b + 1)
                            pool.sem_inc(paced, 1)
                            for r in range(b * U, b * U + U):
                                pool.indirect_dma_start(
                                    out=rows[:, :], out_offset=bass.IndirectOffsetOnAxis(ap=row_u[:, r:r + 1], axis=0),
                                    in_=stage[:, r, :], in_offset=None,
                                    bounds_check=bound, oob_is_err=False).then_inc(scattered[b], 16)
                    turns(pool, turns_, body)
                    for b in range(2):
                        pool.wait_ge(scattered[b], 16 * U * turns_)

        sort_edges(0, src, dst, E1, C1, sorted1, True)
        sort_edges(1, edges[0], edges[1], E2, C2, sorted2, False)

        place = Place()
        x_sb = place([NB, D])
        acc = place([NB, D])
        src_u = place([S1], u32)
        dst_lo = place([S1])
        fetched = place([RING, D])
        hot = place([RING, P])
        idx = place([RING], u32)
        lo_stage = place([RING])
        chunk_row = place([S1], i32)
        W_sb = place([KD, D])
        bias = place([D])
        SO = 7
        flat = fetched.rearrange("p r d -> p (r d)")
        o_ring = flat[:, 0:SO * D].rearrange("p (u d) -> p u d", d=D)
        oT_ring = flat[:, SO * D:2 * SO * D].rearrange("p (u k c) -> p u k c", k=KD, c=P)
        stats = place([NB, 6])
        mv = place([NB, 2])
        rstd = place([NB])
        record = flat[:, 0:S1].rearrange("p (c f) -> p c f", f=4)
        table_v = table.rearrange("(b p) f -> p b f", p=P)
        psum_T = psum[:, 0:4, 0:D].rearrange("p b (k c) -> p b k c", k=KD)
        psum_M = psum[:, 4:8, 0:D]

        def norm_stats(tag, before_it=None):
            with stage_of() as block:
                var_ready, root_ready = sem(f"var_ready{tag}"), sem(f"root_ready{tag}")

                @block.vector
                def _(dve):
                    if before_it:
                        before_it(dve)
                    for n in range(NB):
                        last = dve.bn_stats(stats[:, n, :], x_sb[:, n, :])
                    dve_step.done(last, dve)
                    for n in range(NB):
                        last = dve.bn_aggr(mv[:, n, :], stats[:, n, :])
                    dve_step.done(last, dve)
                    dve.tensor_scalar(rstd, mv[:, :, 1:2].rearrange("p n a -> p (n a)"), EPS, None, ALU.add).then_inc(var_ready, 1)
                    dve.wait_ge(root_ready, 1)
                    dve_step.done(dve.reciprocal(rstd, rstd), dve)

                @block.scalar
                def _(act):
                    act.wait_ge(var_ready, 1)
                    act.activation(rstd, rstd, ACT.Sqrt).then_inc(root_ready, 1)

        def project(tag, rows_of_block, width, finish, transposed_too=None, weights=None):
            with stage_of() as block:
                rows_ready, turned, T_ready, multiplied, ended, left, sent = (
                    sem(f"{n}{tag}") for n in ("rows_ready", "turned", "T_ready", "multiplied", "ended", "left", "sent"))
                t_out = sem(f"t_out{tag}")

                @block.vector
                def _(dve):
                    def body(k):
                        for u in range(SO):
                            wait(dve, turned, k * SO + (u + 1 - SO))
                            rows_of_block(dve, k * SO + u, o_ring[:, u, :]).then_inc(rows_ready, 1)
                    turns(dve, G7, body)

                @block.tensor
                def _(pe):
                    pe.wait_ge(loads, loaded[0])

                    def body(k):
                        for u in range(SO):
                            pe.wait_ge(rows_ready, k * SO + (u + 1))
                            wait(pe, T_ready, k * SO + max(u - 3, 0))
                            for c in range(KD):
                                last = pe.transpose(psum_T[:, u % 4, c, :], o_ring[:, u, c * P:(c + 1) * P], ident[:, :])
                            last.then_inc(turned, 1)
                        for u in range(SO):
                            pe.wait_ge(T_ready, k * SO + (u + 1))
                            wait(pe, ended, k * SO + max(u - 3, 0))
                            for c in range(KD):
                                last = pe.matmul(psum_M[:, u % 4, 0:width], oT_ring[:, u, c, :], weights[:, c, 0:width],
                                                 start=c == 0, stop=c == KD - 1)
                            last.then_inc(multiplied, 1)
                    turns(pe, G7, body)

                @block.scalar
                def _(act):
                    def body(k):
                        for u in range(SO):
                            act.wait_ge(turned, k * SO + (u + 1))
                            wait(act, multiplied, k * SO + (u + 1 - SO))
                            if transposed_too is not None:
                                wait(act, t_out, k * 16)
                            act.copy(oT_ring[:, u, :, :], psum_T[:, u % 4, :, :]).then_inc(T_ready, 1)
                        for u in range(SO):
                            act.wait_ge(multiplied, k * SO + (u + 1))
                            finish(act, k * SO + u, psum_M[:, u % 4, 0:width]).then_inc(ended, 1)
                    turns(act, G7, body)

                @block.sync
                def _(sp):
                    paced = sem(f"paced{tag}")

                    def body(k):
                        if transposed_too is None:
                            sp.wait_ge(ended, k * SO + SO)
                            sp.sem_inc(paced, 1)
                            sp.dma_start(table_v[:, bass.ds(k * SO, SO), :], acc[:, bass.ds(k * SO, SO), :]).then_inc(left, 16)
                        else:
                            sp.wait_ge(T_ready, k * SO + SO)
                            sp.sem_inc(paced, 1)
                            view = transposed_too[:, :, bass.ds(k * (SO * P), SO * P)]
                            for c in range(KD):
                                sp.dma_start(view[:, c, :].rearrange("p (u n) -> p u n", n=P), oT_ring[:, :, c, :]).then_inc(
                                    t_out if c == KD - 1 else left, 16)
                            sp.wait_ge(left, 16 * (k + 1))
                            sp.wait_ge(t_out, 16 * (k + 1))
                            sp.sem_inc(paced, 1)
                    turns(sp, G7, body)
                    sp.wait_ge(left, 16 * G7)

        with stage_of() as block:
            zeroed, rec_in, rec_used = sem("zeroed"), sem("rec_in"), sem("rec_used")
            part = S1 // 4
            assert S1 % 4 == 0
            sv = sorted1.rearrange("(p c) f -> p c f", c=S1)

            @block.sync
            def _(sp):
                load(sp, chunk_row[0:1, :], chunk_dram[0:S1].rearrange("(a c) -> a c", a=1))
                sp.wait_ge(zeroed, 1)
                nf = N // P
                load(sp, x_sb[:, 0:nf, :], x[0:nf * P, :].rearrange("(b p) f -> p b f", p=P))
                load(sp, x_sb[0:N - nf * P, nf, :], x[nf * P:N, :])
                for q in range(4):
                    wait(sp, rec_used, q)
                    sp.dma_start(record[:, 0:part, :], sv[:, q * part:(q + 1) * part, :]).then_inc(rec_in, 16)

            want = loaded[0]

            @block.vector
            def _(dve):
                dve.memset(x_sb[:, NB - 1, :], 0.0).then_inc(zeroed, 1)
                for q in range(4):
                    dve.wait_ge(rec_in, 16 * (q + 1))
                    cut = slice(q * part, (q + 1) * part)
                    dve.tensor_copy(src_u[:, cut], record[:, 0:part, 0:1].rearrange("p c a -> p (c a)"))
                    dve.tensor_copy(dst_lo[:, cut], record[:, 0:part, 2:3].rearrange("p c a -> p (c a)")).then_inc(rec_used, 1)
                dve.wait_ge(loads, want)

        norm_stats("a")

        def normed(dve, n, to):
            return dve.tensor_scalar(to, x_sb[:, bass.ds(n, 1), :].rearrange("p a f -> p (a f)"),
                                     mv[:, bass.ds(n, 1), 0:1].rearrange("p a f -> p (a f)"), rstd[:, bass.ds(n, 1)],
                                     ALU.subtract, ALU.mult)

        def conv_out(dve, n, to):
            return dve.scalar_tensor_tensor(to, acc[:, bass.ds(n, 1), :].rearrange("p a f -> p (a f)"),
                                            dinv[:, bass.ds(n, 1)], bias, ALU.mult, ALU.add)

        def scaled(act, n, got):
            return act.activation(acc[:, bass.ds(n, 1), :].rearrange("p a f -> p (a f)"), got, ACT.Copy,
                                  scale=dinv[:, bass.ds(n, 1)])

        def load_layer(layer):
            with stage_of() as block:
                @block.sync
                def _(sp):
                    load(sp, W_sb, gW[layer].rearrange("(k p) n -> p k n", p=P))
                    if layer:
                        load(sp, bias, gb[layer - 1].partition_broadcast(P))
                    sp.wait_ge(loads, loaded[0])

        def add_neighbours(layer):
            with stage_of() as block:
                names = ("idx_ready", "lo_ready", "hot_ready", "multiplied", "added")
                idx_ready, lo_ready, hot_ready, multiplied, added = (sem(f"c{layer}_{n}") for n in names)
                arrived = [sem(f"c{layer}_arrived{b}") for b in range(2)]
                slots = psum[:, :, 0:D]
                TURNS = S1 // RING

                @block.scalar
                def _(act):
                    def body(k):
                        for b in range(2):
                            half = slice(b * U, b * U + U)
                            wait(act, arrived[b], k * (16 * U))
                            act.copy(idx[:, half], src_u[:, bass.ds(k * RING + b * U, U)]).then_inc(idx_ready, 1)
                            wait(act, hot_ready, (2 * k + b - 1) * U)
                            act.copy(lo_stage[:, half], dst_lo[:, bass.ds(k * RING + b * U, U)]).then_inc(lo_ready, 1)
                    turns(act, TURNS, body)

                @block.gpsimd
                def _(pool):
                    paced = sem("paced")
                    bound = pool.to_reg(NP - 1)

                    def body(k):
                        for b in range(2):
                            pool.wait_ge(idx_ready, 2 * k + b + 1)
                            wait(pool, multiplied, (2 * k + b - 1) * U)
                            pool.sem_inc(paced, 1)
                            for r in range(b * U, b * U + U):
                                pool.indirect_dma_start(
                                    out=fetched[:, r, :], out_offset=None, in_=table[:, :],
                                    in_offset=bass.IndirectOffsetOnAxis(ap=idx[:, r:r + 1], axis=0),
                                    bounds_check=bound, oob_is_err=False).then_inc(arrived[b], 16)
                    turns(pool, TURNS, body)

                @block.vector
                def _(dve):
                    reg = [dve.alloc_register(f"blk{layer}_{u}") for u in range(U)]

                    def body(k):
                        for b in range(2):
                            dve.wait_ge(lo_ready, 2 * k + b + 1)
                            wait(dve, multiplied, (2 * k + b - 1) * U)
                            for r in range(b * U, b * U + U):
                                dve.tensor_scalar(hot[:, r, :], iota_row[:, :], lo_stage[:, r:r + 1], None, ALU.is_equal).then_inc(hot_ready, 1)
                            dve.load(reg, chunk_row[0:1, bass.ds(k * RING + b * U, U)])
                            for u in range(U):
                                n = k * RING + (b * U + u)
                                where = bass.ds(dve.snap(reg[u], min_val=0, max_val=NB - 1), 1)
                                to = acc[:, where, :].rearrange("p a f -> p (a f)")
                                dve.wait_ge(multiplied, n + 1)
                                wait(dve, added, n)
                                dve.tensor_tensor(to, to, slots[:, u, :], ALU.add).then_inc(added, 1)
                    turns(dve, TURNS, body)
                    dve.wait_ge(added, S1)

                @block.tensor
                def _(pe):
                    def body(k):
                        for b in range(2):
                            pe.wait_ge(arrived[b], (k + 1) * (16 * U))
                            for u in range(U):
                                n = k * RING + (b * U + u)
                                pe.wait_ge(hot_ready, n + 1)
                                wait(pe, added, n - U + 1)
                                pe.matmul(slots[:, u, :], hot[:, b * U + u, :], fetched[:, b * U + u, :], start=True, stop=True).then_inc(multiplied, 1)
                    turns(pe, TURNS, body)

        for layer in range(3):
            load_layer(layer)
            project(f"_l{layer}", conv_out if layer else normed, D, scaled, weights=W_sb)
            add_neighbours(layer)

        Wg = place([KD, HE])
        att = place([2, HE])
        last_bias = place([D])
        with stage_of() as block:
            stored = sem("x1_stored")
            x1_ready = sem("x1_ready")

            @block.sync
            def _(sp):
                load(sp, last_bias, gb[2].partition_broadcast(P))
                load(sp, Wg, W_gat.rearrange("(k p) n -> p k n", p=P))
                load(sp, att[:, 0, :], att_src.rearrange("h e -> (h e)").partition_broadcast(P))
                load(sp, att[:, 1, :], att_dst.rearrange("h e -> (h e)").partition_broadcast(P))
                sp.wait_ge(x1_ready, 1)
                sp.dma_start(x1_dram.rearrange("(b p) f -> p b f", p=P), x_sb).then_inc(stored, 16)
                sp.wait_ge(stored, 16)
                sp.wait_ge(loads, loaded[0])

            want = loaded[0]

            @block.vector
            def _(dve):
                dve.wait_ge(loads, want)
                for n in range(NB):
                    last = dve.scalar_tensor_tensor(acc[:, n, :], acc[:, n, :], dinv[:, n:n + 1], last_bias, ALU.mult, ALU.add)
                dve_step.done(last, dve)
                dve.tensor_tensor(x_sb, x_sb, acc, ALU.add).then_inc(x1_ready, 1)
                dve.wait_ge(x1_ready, 1)

        norm_stats("b")

        def features(act, n, got):
            return act.copy(node_feat[:, bass.ds(n, 1), 0:HE].rearrange("p a f -> p (a f)"), got)

        project("_gat", normed, HE, features, transposed_too=xT_dram, weights=Wg)

        attw = sb("attw", [P, 2, HE])
        place = Place()
        packed = place([NB, TW])
        prod = place([NB, HE])
        with stage_of() as block:
            stored, packed_ready = sem("table2_stored"), sem("packed_ready")

            @block.vector
            def _(dve):
                dve.memset(packed, 0.0)
                dve_step.done(dve.tensor_copy(attw[:, :, :], att), dve)
                for s in range(2):
                    dve_step.done(dve.tensor_tensor(prod, node_feat[:, :, 0:HE],
                                                    attw[:, s:s + 1, :].to_broadcast([P, NB, HE]), ALU.mult), dve)
                    dve_step.done(dve.tensor_reduce(node_feat[:, :, HE + H * s:HE + H * s + H],
                                                    prod.rearrange("p n (h e) -> p n h e", h=H), AX.X, ALU.add), dve)
                dve.tensor_copy(packed[:, :, 0:24], node_feat[:, :, :]).then_inc(packed_ready, 1)

            @block.sync
            def _(sp):
                sp.wait_ge(packed_ready, 1)
                sp.dma_start(table2.rearrange("(b p) f -> p b f", p=P), packed).then_inc(stored, 16)
                sp.wait_ge(stored, 16)

        place = Place()
        EW = HE + H
        edge = place([S2, EW])
        far = place([S2, 2 * H])
        score = place([S2, H])
        maxed = place([S2, H])
        same = place([S2])
        apart = place([S2])
        key_now, key_prev, src_f = same, apart, score[:, 0:S2 // 4, :].rearrange("p a b -> p (a b)")
        idx2_all = maxed[:, 0:S2 // 4, :].rearrange("p a b -> p (a b)").bitcast(u32)
        rec = far
        fetched2 = place([RING, TW])
        idx2 = place([RING], u32)
        node_max = place([NB, H])
        node_pay = place([NB, 2 * H])
        node_sum = place([NB, EW])
        first_row, last_row = place([NB], u32), place([NB], u32)
        node_tmp = place([NB, H])
        node_tmp2 = place([NB, H])
        node_big = place([NB, HE])
        carry_rows = place([4, P])
        end_cols = place([2, 24])
        nt1, nt2 = place([NB]), place([NB])
        vecs = place([3, HE])
        all_same = place([1])

        with stage_of() as block:
            rec_in, rec_used, vec_in = sem("rec2_in"), sem("rec2_used"), sem("vec_in")
            spread0 = sem("spread_zeroed")
            rv = sorted2[1:P * S2 + 1, :].rearrange("(p c) f -> p c f", c=S2)
            rprev = sorted2[0:P * S2, :].rearrange("(p c) f -> p c f", c=S2)
            recv = far.rearrange("p c f -> p (c f)")[:, 0:S2 * 4].rearrange("p (c f) -> p c f", f=4)

            @block.sync
            def _(sp):
                sp.dma_start(recv, rv).then_inc(rec_in, 16)
                sp.wait_ge(rec_used, 1)
                sp.dma_start(recv, rprev).then_inc(rec_in, 16)
                for i, v in enumerate((b_gat, ln_g, ln_b)):
                    sp.dma_start(vecs[:, i, :], v.partition_broadcast(P)).then_inc(vec_in, 16)
                sp.wait_ge(vec_in, 48)
                sp.wait_ge(rec_used, 2)
                sp.dma_start(spread.rearrange("(p c) f -> p c f", c=S2), far).then_inc(spread0, 16)
                sp.wait_ge(spread0, 16)

            @block.vector
            def _(dve):
                dve.memset(node_max, -BIG)
                dve.memset(node_sum, 0.0)
                dve.wait_ge(rec_in, 16)
                dve.tensor_copy(idx2_all, recv[:, :, 0:1].rearrange("p c a -> p (c a)"))
                dve.tensor_copy(same, recv[:, :, 1:2].rearrange("p c a -> p (c a)")).then_inc(rec_used, 1)
                dve.wait_ge(rec_in, 32)
                dve_step.done(dve.tensor_tensor(same, same, recv[:, :, 1:2].rearrange("p c a -> p (c a)"), ALU.is_equal), dve)
                dve.memset(far, 0.0).then_inc(rec_used, 1)
                dve_step.done(dve.tensor_scalar(apart, same, 1.0, BIG, ALU.subtract, ALU.mult), dve)
                dve_step.done(dve.tensor_reduce(all_same, same, AX.X, ALU.min), dve)
                dve_step.done(dve.tensor_scalar(nt1, counts[1][:, :], 0.0, SKIP, ALU.is_equal, ALU.mult), dve)
                dve_step.done(dve.tensor_tensor(nt2, nt1, starts[1][:, :], ALU.add), dve)
                dve.tensor_copy(first_row, nt2)
                dve_step.done(dve.tensor_tensor(nt1, nt2, counts[1][:, :], ALU.add), dve)
                dve_step.done(dve.tensor_scalar(last_row, nt1, 1.0, None, ALU.subtract), dve)

        with stage_of() as block:
            idx_ready, copied2 = sem("g_idx_ready"), sem("g_copied")
            arrived2 = [sem(f"g_arrived{b}") for b in range(2)]

            @block.scalar
            def _(act):
                def body(k):
                    for b in range(2):
                        half = slice(b * U, b * U + U)
                        wait(act, arrived2[b], k * (16 * U))
                        act.copy(idx2[:, half], idx2_all[:, bass.ds(k * RING + b * U, U)]).then_inc(idx_ready, 1)
                turns(act, S2 // RING, body)

            @block.gpsimd
            def _(pool):
                paced = sem("paced")
                bound = pool.to_reg(NP - 1)

                def body(k):
                    for b in range(2):
                        pool.wait_ge(idx_ready, 2 * k + b + 1)
                        wait(pool, copied2, 2 * k + b - 1)
                        pool.sem_inc(paced, 1)
                        for r in range(b * U, b * U + U):
                            pool.indirect_dma_start(
                                out=fetched2[:, r, :], out_offset=None, in_=table2[:, :],
                                in_offset=bass.IndirectOffsetOnAxis(ap=idx2[:, r:r + 1], axis=0),
                                bounds_check=bound, oob_is_err=False).then_inc(arrived2[b], 16)
                turns(pool, S2 // RING, body)

            @block.vector
            def _(dve):
                def body(k):
                    for b in range(2):
                        dve.wait_ge(arrived2[b], (k + 1) * (16 * U))
                        dve.tensor_copy(edge[:, bass.ds(k * RING + b * U, U), :],
                                        fetched2[:, b * U:b * U + U, 0:EW]).then_inc(copied2, 1)
                turns(dve, S2 // RING, body)
                dve.wait_ge(copied2, 2 * (S2 // RING))

        def segment_scan(tag, width, data, result, gate, op0, neutral):
            with stage_of() as block:
                scanned, turned, combined, back = (sem(f"{n}{tag}") for n in ("scanned", "turned", "combined", "back"))
                ends, gates_ = end_cols[:, 0, 0:width], end_cols[:, 1, 0:width]
                T1, T2 = psum[0:width, 0, 0:P], psum[0:width, 1, 0:P]
                R1, R2, R3, R4 = (carry_rows[0:width, i, :] for i in range(4))
                TB = psum[:, 2, 0:width]

                @block.vector
                def _(dve):
                    for f in range(width):
                        last = dve.tensor_tensor_scan(result(f), gate, data(f), neutral, op0[0], op0[1])
                    dve_step.done(last, dve)
                    for f in range(width):
                        dve.tensor_copy(ends[:, f:f + 1], result(f)[:, S2 - 1:S2])
                        if neutral == 0.0:
                            last = dve.tensor_copy(gates_[:, f:f + 1], all_same)
                        else:
                            last = dve.tensor_scalar(gates_[:, f:f + 1], all_same, 1.0, BIG, ALU.subtract, ALU.mult)
                    last.then_inc(scanned, 1)
                    dve.wait_ge(turned, 1)
                    dve.tensor_copy(R1, T1)
                    dve_step.done(dve.tensor_copy(R2, T2), dve)
                    dve_step.done(dve.tensor_tensor_scan(R3, R2, R1, neutral, op0[0], op0[1]), dve)
                    dve_step.done(dve.memset(R4, neutral), dve)
                    dve.tensor_copy(R4[:, 1:P], R3[:, 0:P - 1]).then_inc(combined, 1)
                    dve.wait_ge(back, 1)
                    dve_step.done(dve.tensor_copy(ends, TB), dve)
                    for f in range(width):
                        last = dve.tensor_tensor_scan(result(f), gate, data(f), ends[:, f:f + 1], op0[0], op0[1])
                    dve_step.done(last, dve)

                @block.tensor
                def _(pe):
                    pe.wait_ge(scanned, 1)
                    pe.transpose(T1, ends, ident[:, :])
                    pe.transpose(T2, gates_, ident[:, :]).then_inc(turned, 1)
                    pe.wait_ge(combined, 1)
                    pe.transpose(TB, R4, ident[0:width, 0:width]).then_inc(back, 1)

        def column(t, f):
            return t[:, :, f:f + 1].rearrange("p c a -> p (c a)")

        def node_rows(tag, tensor, to, rows, scatter):
            with stage_of() as block:
                moved = sem(f"node_moved{tag}")

                @block.gpsimd
                def _(pool):
                    bound = pool.to_reg(P * S2 - 1)
                    for n in range(NB):
                        off = bass.IndirectOffsetOnAxis(ap=rows[:, n:n + 1], axis=0)
                        if scatter:
                            pool.indirect_dma_start(out=tensor[:, :], out_offset=off, in_=to[:, n, :], in_offset=None,
                                                    bounds_check=bound, oob_is_err=False).then_inc(moved, 16)
                        else:
                            pool.indirect_dma_start(out=to[:, n, :], out_offset=None, in_=tensor[:, :], in_offset=off,
                                                    bounds_check=bound, oob_is_err=False).then_inc(moved, 16)
                    pool.wait_ge(moved, 16 * NB)

        def move(tag, to, of):
            with stage_of() as block:
                moved = sem(f"moved{tag}")

                @block.sync
                def _(sp):
                    sp.dma_start(to, of).then_inc(moved, 16)
                    sp.wait_ge(moved, 16)

        segment_scan("_max", H, lambda f: column(edge, HE + f), lambda f: column(maxed, f), apart, (ALU.add, ALU.max), -BIG)
        move("_max", maxes.rearrange("(p c) f -> p c f", c=S2), maxed)
        node_rows("_max", maxes, node_max, last_row, False)

        with stage_of() as block:
            @block.vector
            def _(dve):
                a_src, a_dst = node_feat[:, :, HE:HE + H], node_feat[:, :, HE + H:HE + 2 * H]
                dve.tensor_copy(node_pay[:, :, 0:H], a_dst)
                dve_step.done(dve.tensor_tensor(node_max, node_max, a_src, ALU.max), dve)
                dve_step.done(dve.tensor_tensor(node_tmp, node_max, a_dst, ALU.add), dve)
                dve_step.done(dve.scalar_tensor_tensor(node_pay[:, :, H:2 * H], node_tmp, 0.2, node_tmp, ALU.mult, ALU.max), dve)
        node_rows("_pay", spread, node_pay, first_row, True)
        move("_pay", far, spread.rearrange("(p c) f -> p c f", c=S2))

        segment_scan("_far0", H, lambda f: column(far, f), lambda f: column(score, f), same, (ALU.mult, ALU.add), 0.0)
        segment_scan("_far1", H, lambda f: column(far, H + f), lambda f: column(maxed, f), same, (ALU.mult, ALU.add), 0.0)

        with stage_of() as block:
            raw_ready, exp_ready = sem("raw_ready"), sem("exp_ready")

            @block.vector
            def _(dve):
                a_src = edge[:, :, HE:HE + H]
                dve_step.done(dve.tensor_tensor(score, score, a_src, ALU.add), dve)
                dve_step.done(dve.scalar_tensor_tensor(far[:, :, 0:H], score, 0.2, score, ALU.mult, ALU.max), dve)
                dve.tensor_tensor(score, far[:, :, 0:H], maxed, ALU.subtract).then_inc(raw_ready, 1)
                dve.wait_ge(exp_ready, 1)
                for h in range(H):
                    part_ = edge[:, :, h * NE:(h + 1) * NE]
                    dve.tensor_tensor(part_, part_, score[:, :, h:h + 1].to_broadcast([P, S2, NE]), ALU.mult)
                dve_step.done(dve.tensor_copy(edge[:, :, HE:HE + H], score), dve)

            @block.scalar
            def _(act):
                act.wait_ge(raw_ready, 1)
                act.activation(score, score, ACT.Exp).then_inc(exp_ready, 1)


        for part_no, (f0, f1) in enumerate(((0, 8), (8, 16), (16, 20))):
            w = f1 - f0
            tgt = far if w == 8 else score
            segment_scan(f"_sum{part_no}", w, lambda f, f0=f0: column(edge, f0 + f), lambda f, tgt=tgt: column(tgt, f),
                         same, (ALU.mult, ALU.add), 0.0)
            with stage_of() as block:
                @block.vector
                def _(dve, f0=f0, f1=f1, tgt=tgt, w=w):
                    dve_step.done(dve.tensor_copy(edge[:, :, f0:f1], tgt[:, :, 0:w]), dve)
        move("_sum", sums.rearrange("(p c) f -> p c f", c=S2), edge)
        node_rows("_sum", sums, node_sum, last_row, False)

        with stage_of() as block:
            s_raw, s_exp, s_var, s_root = sem("s_raw"), sem("s_exp"), sem("s_var"), sem("s_root")
            a_src, a_dst = node_feat[:, :, HE:HE + H], node_feat[:, :, HE + H:HE + 2 * H]
            agg = node_sum[:, :, 0:HE]
            sc = node_tmp2

            @block.vector
            def _(dve):
                def do(ins):
                    dve_step.done(ins, dve)

                do(dve.tensor_tensor(node_tmp, a_src, a_dst, ALU.add))
                do(dve.scalar_tensor_tensor(node_tmp2, node_tmp, 0.2, node_tmp, ALU.mult, ALU.max))
                dve.tensor_tensor(node_tmp, node_tmp2, node_pay[:, :, H:2 * H], ALU.subtract).then_inc(s_raw, 1)
                dve.wait_ge(s_exp, 1)
                for h in range(H):
                    last = dve.tensor_tensor(node_big[:, :, h * NE:(h + 1) * NE], node_feat[:, :, h * NE:(h + 1) * NE],
                                             node_tmp[:, :, h:h + 1].to_broadcast([P, NB, NE]), ALU.mult)
                do(last)
                do(dve.tensor_tensor(agg, agg, node_big, ALU.add))
                do(dve.tensor_tensor(node_tmp2, node_sum[:, :, HE:EW], node_tmp, ALU.add))
                do(dve.tensor_scalar(node_tmp2, node_tmp2, 1e-16, None, ALU.add))
                do(dve.reciprocal(node_tmp, node_tmp2))
                for h in range(H):
                    last = dve.tensor_tensor(agg[:, :, h * NE:(h + 1) * NE], agg[:, :, h * NE:(h + 1) * NE],
                                             node_tmp[:, :, h:h + 1].to_broadcast([P, NB, NE]), ALU.mult)
                do(last)
                do(dve.tensor_tensor(agg, agg, vecs[:, 0:1, :].to_broadcast([P, NB, HE]), ALU.add))
                do(dve.tensor_reduce(nt1, agg, AX.X, ALU.add))
                do(dve.tensor_scalar(nt1, nt1, 1.0 / HE, None, ALU.mult))
                do(dve.tensor_tensor(agg, agg, nt1.rearrange("p (n a) -> p n a", a=1).to_broadcast([P, NB, HE]), ALU.subtract))
                do(dve.tensor_tensor(node_big, agg, agg, ALU.mult))
                do(dve.tensor_reduce(nt1, node_big, AX.X, ALU.add))
                dve.tensor_scalar(nt1, nt1, 1.0 / HE, EPS, ALU.mult, ALU.add).then_inc(s_var, 1)
                dve.wait_ge(s_root, 1)
                do(dve.reciprocal(nt2, nt1))
                do(dve.tensor_tensor(agg, agg, nt2.rearrange("p (n a) -> p n a", a=1).to_broadcast([P, NB, HE]), ALU.mult))
                do(dve.tensor_tensor(agg, agg, vecs[:, 1:2, :].to_broadcast([P, NB, HE]), ALU.mult))
                do(dve.tensor_tensor(agg, agg, vecs[:, 2:3, :].to_broadcast([P, NB, HE]), ALU.add))
                do(dve.tensor_reduce(sc, agg.rearrange("p n (h e) -> p n e h", h=H), AX.X, ALU.add))
                do(dve.tensor_scalar(sc, sc, 1.0 / H, None, ALU.mult))
                place_ = node_pay[:, :, 0:NE]
                do(dve.memset(place_, 0.0))
                for e in range(NE):
                    for o in range(NE):
                        if o != e:
                            do(dve.tensor_tensor(node_tmp[:, :, 0:1], sc[:, :, o:o + 1], sc[:, :, e:e + 1],
                                                 ALU.is_ge if o < e else ALU.is_gt))
                            do(dve.tensor_tensor(place_[:, :, e:e + 1], place_[:, :, e:e + 1], node_tmp[:, :, 0:1], ALU.add))
                do(dve.tensor_scalar(place_, place_, 1.5, None, ALU.is_lt))
                do(dve.tensor_reduce(nt1, sc, AX.X, ALU.max))
                dve.tensor_tensor(sc, sc, nt1.rearrange("p (n a) -> p n a", a=1).to_broadcast([P, NB, NE]), ALU.subtract).then_inc(s_raw, 1)
                dve.wait_ge(s_exp, 2)
                do(dve.tensor_tensor(gates[:, :, :], sc, place_, ALU.mult))
                do(dve.tensor_reduce(nt1, gates[:, :, :], AX.X, ALU.add))
                do(dve.reciprocal(nt2, nt1))
                do(dve.tensor_tensor(gates[:, :, :], gates[:, :, :], nt2.rearrange("p (n a) -> p n a", a=1).to_broadcast([P, NB, NE]), ALU.mult))

            @block.scalar
            def _(act):
                act.wait_ge(s_raw, 1)
                act.activation(node_tmp, node_tmp, ACT.Exp).then_inc(s_exp, 1)
                act.wait_ge(s_var, 1)
                act.activation(nt1, nt1, ACT.Sqrt).then_inc(s_root, 1)
                act.wait_ge(s_raw, 2)
                act.activation(sc, sc, ACT.Exp).then_inc(s_exp, 1)

        place = Place()
        GN = SO * P
        HN = GN // 2
        W1_sb = place([NE * KD, F])
        W2_sb = place([NE * FC, D])
        b1_sb = place([NE, FC])
        b2_sb = place([NE, D])
        xT = place([2 * KD, GN])
        ya = place([2 * SO, D])
        hh = place([2 * FC, GN])
        gate_ring = place([2 * SO, NE])
        psum_H = psum[:, 0:4, 0:HN]
        psum_Y = psum[:, 4:8, 0:D]
        out_v = out[0:(NB - 1) * P, :].rearrange("(b p) f -> p b f", p=P)
        x1_v = x1_dram.rearrange("(b p) f -> p b f", p=P)
        assert G7 % 2 == 1
        PAIRS = G7 // 2
        HT, YT = 2 * FC, SO
        with stage_of() as block:
            w_in, hid, gelud, y_made, y_added, gate_ready = (sem(n) for n in ("w_in", "hid", "gelud", "y_made", "y_added", "gate_ready"))
            x_in, y_in, y_out = ([sem(f"{n}{i}") for i in range(2)] for n in ("x_in", "y_in", "y_out"))

            def groups(eng, one, steps=(), per=()):
                def body(k):
                    for s in range(2):
                        one(2 * k + s, s, k)
                turns(eng, PAIRS, body, steps, per)
                one(G7 - 1, 0, PAIRS)

            @block.sync
            def _(sp):
                paced = sem("paced")
                sp.dma_start(W1_sb, W1.rearrange("e (k p) f -> p (e k) f", p=P)).then_inc(w_in, 16)
                sp.dma_start(W2_sb, W2.rearrange("e (c p) d -> p (e c) d", p=P)).then_inc(w_in, 16)
                with nc.allow_non_contiguous_dma("biases, one word a row"):
                    for e in range(NE):
                        sp.dma_start(b1_sb[:, e, :], b1[e].rearrange("(c p) -> p c", p=P)).then_inc(w_in, 16)
                sp.dma_start(b2_sb[0:1, :, :], b2.rearrange("(a e) d -> a e d", a=1)).then_inc(w_in, 16)

                def fetch(t, s, k):
                    wait(sp, y_made, (t - 1) * (NE * YT))
                    wait(sp, y_out[s], k * 16)
                    sp.sem_inc(paced, 1)
                    sp.dma_start(xT[:, s * KD:(s + 1) * KD, :], xT_dram[:, :, bass.ds(t * GN, GN)]).then_inc(x_in[s], 16)
                    sp.dma_start(ya[:, s * SO:(s + 1) * SO, :], x1_v[:, bass.ds(t * SO, SO), :]).then_inc(y_in[s], 16)

                def store(t, s, k):
                    sp.wait_ge(y_added, (t + 1) * (NE * YT))
                    sp.sem_inc(paced, 1)
                    sp.dma_start(out_v[:, bass.ds(t * SO, SO), :], ya[:, s * SO:(s + 1) * SO, :]).then_inc(y_out[s], 16)

                fetch(0, 0, 0)
                fetch(1, 1, 0)

                def body(k):
                    store(2 * k, 0, k)
                    fetch(2 * k + 2, 0, k + 1)
                    store(2 * k + 1, 1, k)
                    if not (isinstance(k, int) and k == PAIRS - 1):
                        fetch(2 * k + 3, 1, k + 1)
                body(0)
                if PAIRS > 2:
                    with sp.Fori(1, PAIRS - 1) as k:
                        body(k)
                body(PAIRS - 1)
                sp.wait_ge(y_added, G7 * NE * YT)
                sp.dma_start(out_v[:, (G7 - 1) * SO:NB - 1, :], ya[:, 0:SO - 1, :]).then_inc(y_out[0], 16)
                sp.dma_start(out[(NB - 1) * P:N, :], ya[0:N - (NB - 1) * P, SO - 1, :]).then_inc(y_out[1], 16)
                for s in range(2):
                    sp.wait_ge(y_out[s], 16 * (PAIRS + 1))

            @block.tensor
            def _(pe):
                pe.wait_ge(w_in, 16 * (3 + NE))

                def up(t, s, k, e):
                    if e == 0:
                        pe.wait_ge(x_in[s], (k + 1) * 16)
                    for i in range(HT):
                        fc, half = i // 2, i % 2
                        wait(pe, gelud, t * (NE * HT) + (e * HT + i - 3))
                        for c in range(KD):
                            last = pe.matmul(psum_H[:, i % 4, :], W1_sb[:, e * KD + c, fc * P:(fc + 1) * P],
                                             xT[:, s * KD + c, half * HN:(half + 1) * HN], start=c == 0, stop=c == KD - 1)
                        last.then_inc(hid, 1)

                def down(t, s, k, e):
                    pe.wait_ge(gelud, t * (NE * HT) + (e + 1) * HT)
                    for u in range(YT):
                        wait(pe, y_added, t * (NE * YT) + (e * YT + max(u - 3, 0)))
                        for fc in range(FC):
                            pe.matmul(psum_Y[:, u % 4, :], hh[:, (e % 2) * FC + fc, u * P:(u + 1) * P], W2_sb[:, e * FC + fc, :],
                                      start=fc == 0, stop=False)
                        pe.matmul(psum_Y[:, u % 4, :], ones[0:1, :], b2_sb[0:1, e, :], start=False, stop=True).then_inc(y_made, 1)

                def one(t, s, k):
                    up(t, s, k, 0)
                    for e in range(NE):
                        if e + 1 < NE:
                            up(t, s, k, e + 1)
                        down(t, s, k, e)
                groups(pe, one)

            @block.scalar
            def _(act):
                act.wait_ge(w_in, 16 * (3 + NE))

                def one(t, s, k):
                    for e in range(NE):
                        wait(act, y_made, t * (NE * YT) + (e - 1) * YT)
                        for i in range(HT):
                            fc, half = i // 2, i % 2
                            act.wait_ge(hid, t * (NE * HT) + (e * HT + i + 1))
                            act.activation(hh[:, (e % 2) * FC + fc, half * HN:(half + 1) * HN], psum_H[:, i % 4, :], ACT.Gelu,
                                           bias=b1_sb[:, e, fc:fc + 1]).then_inc(gelud, 1)
                groups(act, one)

            @block.vector
            def _(dve):
                def one(t, s, k):
                    dve.wait_ge(y_in[s], (k + 1) * 16)
                    cut = slice(s * SO, (s + 1) * SO)
                    dve_step.done(dve.tensor_copy(gate_ring[:, cut, :], gates[:, bass.ds(t * SO, SO), :]), dve)
                    for e in range(NE):
                        for u in range(YT):
                            n = t * (NE * YT) + (e * YT + u)
                            dve.wait_ge(y_made, n + 1)
                            wait(dve, y_added, n - (YT - 1))
                            to = ya[:, s * SO + u, :]
                            dve.scalar_tensor_tensor(to, psum_Y[:, u % 4, :], gate_ring[:, s * SO + u, e:e + 1], to,
                                                     ALU.mult, ALU.add).then_inc(y_added, 1)
                groups(dve, one, [dve_step], [2])


_INS = ['x', 'src', 'dst', 'L0_gnn_W1', 'L0_gnn_b1', 'L0_gnn_W2', 'L0_gnn_b2', 'L0_gnn_W3', 'L0_gnn_b3',
        'L0_ffn_W_gat', 'L0_ffn_att_src', 'L0_ffn_att_dst', 'L0_ffn_b_gat', 'L0_ffn_ln_gamma', 'L0_ffn_ln_beta',
        'L0_ffn_W1', 'L0_ffn_b1', 'L0_ffn_W2', 'L0_ffn_b2', 'L0_ffn_edge_index']


def build(nc, a, out):
    gnn_moe_kernel(nc, a['x'], a['src'], a['dst'],
                   [a[f'L0_gnn_W{i}'] for i in (1, 2, 3)], [a[f'L0_gnn_b{i}'] for i in (1, 2, 3)],
                   a['L0_ffn_W_gat'], a['L0_ffn_att_src'], a['L0_ffn_att_dst'], a['L0_ffn_b_gat'],
                   a['L0_ffn_ln_gamma'], a['L0_ffn_ln_beta'], a['L0_ffn_W1'], a['L0_ffn_b1'],
                   a['L0_ffn_W2'], a['L0_ffn_b2'], a['L0_ffn_edge_index'], out)


def kernel(**inputs):
    import numpy as _np
    import concourse.bacc as _bacc
    from concourse import mybir as _mybir
    from concourse.bass_utils import run_bass_kernel_spmd as _run

    nc = _bacc.Bacc("TRN2", target_bir_lowering=False, num_devices=1)
    arrays, args = {}, {}
    for name in _INS:
        a = _np.ascontiguousarray(inputs[name])
        arrays[f"in_{name}_dram"] = a
        args[name] = nc.dram_tensor(f"in_{name}_dram", a.shape, _mybir.dt.from_np(a.dtype), kind="ExternalInput").ap()
    out = nc.dram_tensor("out_0_dram", inputs['x'].shape, _mybir.dt.float32, kind="ExternalOutput").ap()
    build(nc, args, out)
    r = _run(nc, [arrays], core_ids=[0])
    return r.results[0]["out_0_dram"]
```

```python
import concourse.bass as bass
from concourse import mybir
from contextlib import ExitStack, contextmanager


class Steps:

    def __init__(self, sem):
        self.sem, self.n, self.base, self.k, self.per = sem, 0, 0, None, 0

    def enter(self, k, per):
        if isinstance(k, int):
            self.k = None
            return
        self.k, self.per, self.i = k, per, 0

    def leave(self, turns):
        if self.k is not None:
            assert self.i == self.per, (self.i, self.per)
            self.n += turns * self.per
            self.k = None

    def done(self, ins, eng):
        ins.then_inc(self.sem, 1)
        if self.k is None:
            self.n += 1
            eng.wait_ge(self.sem, self.n)
        else:
            self.i += 1
            eng.wait_ge(self.sem, (self.k - 1) * self.per + (self.n + self.i))


def wait(eng, sem, value):
    if isinstance(value, int) and value <= 0:
        return
    eng.wait_ge(sem, value)


def turns(eng, count, body, steps=(), per=()):
    body(0)
    if count > 1:
        with eng.Fori(1, count) as k:
            for s, p in zip(steps, per):
                s.enter(k, p)
            body(k)
        for s in steps:
            s.leave(count - 1)


def turns_ahead(eng, count, body, steps=(), per=()):
    body(0, count == 1)
    if count > 2:
        with eng.Fori(1, count - 1) as k:
            for s, p in zip(steps, per):
                s.enter(k, p)
            body(k, False)
        for s in steps:
            s.leave(count - 2)
    if count > 1:
        body(count - 1, True)


def gnn_moe_kernel(nc, x, src, dst, gW, gb, W_gat, att_src, att_dst, b_gat, ln_g, ln_b,
                   W1, b1, W2, b2, edges, out):
    f32, bf16 = mybir.dt.float32, mybir.dt.bfloat16
    i32, u32 = mybir.dt.int32, mybir.dt.uint32
    ALU, ACT, AX = mybir.AluOpType, mybir.ActivationFunctionType, mybir.AxisListType
    P = 128

    N, D = x.shape
    NB = -(-N // P)
    NP = NB * P
    E1, E2 = src.shape[0], edges.shape[1]
    NE, _, F = W1.shape
    H = att_src.shape[0]
    HE = H * NE
    KD, FC = D // P, F // P
    EPS = 1e-5
    U = 8
    RING = 2 * U
    C1 = -(-(-(-E1 // P)) // (4 * U)) * (4 * U)
    C2 = -(-(-(-E2 // P)) // (4 * U)) * (4 * U)
    S1 = -(-(-(-E1 // P) + NB) // RING) * RING
    S2 = C2
    assert E2 == P * C2 and NB % 7 == 0
    INVALID = 8192
    SKIP = float(1 << 20)
    BIG = 1e30
    G7 = NB // 7
    FILL = 512

    sorted1 = nc.dram_tensor("sorted1", (P * C1 + 1, 4), f32).ap()
    src_rows = nc.dram_tensor("src_rows", (C1, P), f32).ap()
    key_rows_dram = nc.dram_tensor("key_rows_dram", (C1, P), f32).ap()
    sorted2 = nc.dram_tensor("sorted2", (P * S2 + 1, 4), f32).ap()
    chunk_dram = nc.dram_tensor("chunk_block", (-(-S1 // P) * P,), i32).ap()
    table = nc.dram_tensor("table", (NP, D), f32).ap()
    x1_dram = nc.dram_tensor("x1_dram", (NP, D), f32).ap()
    xT_dram = nc.dram_tensor("xT_dram", (P, KD, NP), f32).ap()
    y_dram = nc.dram_tensor("y_dram", (NE, NP, D), f32).ap()
    TW = 32
    table2 = nc.dram_tensor("table2", (NP, TW), f32).ap()
    maxes = nc.dram_tensor("maxes", (P * S2, H), f32).ap()
    spread = nc.dram_tensor("spread", (P * S2, 2 * H), f32).ap()
    sums = nc.dram_tensor("sums", (P * S2, HE + H), f32).ap()

    ctx = ExitStack()
    with ctx:
        def sb(name, shape, dt=f32):
            return ctx.enter_context(nc.sbuf_tensor(name, shape, dt))

        def kept_sem(name):
            return ctx.enter_context(nc.semaphore(name))

        scope, names_made = [], []

        def sem(name):
            names_made.append(name)
            scope[-1].append(nc.alloc_semaphore(name=f"{name}_{names_made.count(name)}"))
            return scope[-1][-1]

        @contextmanager
        def stage_of():
            scope.append([])
            with nc.Block() as block:
                yield block
            nc.clear_and_free_semaphores(scope.pop())
            nc.all_engine_barrier()

        iota_row = sb("iota_row", [P, P])
        iota_col = sb("iota_col", [P, 1])
        iota_bf3 = sb("iota_bf3", [P, 1, P], bf16)
        iota_bf = iota_bf3[:, 0, :]
        ident = sb("ident", [P, P])
        ident_bf = sb("ident_bf", [P, P], bf16)
        before = sb("before", [P, 2 * P])
        after = sb("after", [P, P])
        ones = sb("ones", [P, P])
        iota_i = sb("iota_i", [P, P], i32)
        iota_pi = sb("iota_pi", [P, 1], i32)
        counts = [sb(f"counts{g}", [P, NB]) for g in range(2)]
        starts = [sb(f"starts{g}", [P, NB]) for g in range(2)]
        block_start = [sb(f"block_start{g}", [P, NB]) for g in range(2)]
        dinv = sb("dinv", [P, NB])
        small = sb("small", [P, 8, NB])
        small_i = sb("small_i", [P, 2, NB], i32)
        node_feat = sb("node_feat", [P, NB, 24])
        gates = sb("gates", [P, NB, NE])
        ARENA = 49600
        arena = sb("arena", [P, ARENA])
        psum = ctx.enter_context(nc.psum_tensor("psum", [P, 8, 512], f32))

        class Place:

            def __init__(self):
                self.at = 0

            def __call__(self, shape, dt=f32):
                n = 1
                for s in shape:
                    n *= s
                words = n if dt != bf16 else -(-n // 2)
                words = -(-words // 8) * 8
                v = arena[:, self.at:self.at + words]
                self.at += words
                assert self.at <= ARENA, self.at
                if dt != f32:
                    v = v.bitcast(dt)
                v = v[:, 0:n]
                if len(shape) == 2:
                    v = v.rearrange("p (a b) -> p a b", b=shape[1])
                elif len(shape) == 3:
                    v = v.rearrange("p (a b c) -> p a b c", b=shape[1], c=shape[2])
                return v

        dve_step = Steps(kept_sem("dve_step"))
        loads = kept_sem("loads")
        loaded = [0]

        def load(eng, to, of):
            eng.dma_start(to, of).then_inc(loads, 16)
            loaded[0] += 16

        with stage_of() as block:
            iotas = sem("iotas")

            @block.gpsimd
            def _(pool):
                pool.iota(iota_i[:, :], pattern=[[1, P]], base=0, channel_multiplier=0).then_inc(iotas, 1)
                pool.iota(iota_pi[:, :], pattern=[[0, 1]], base=0, channel_multiplier=1).then_inc(iotas, 1)

            @block.vector
            def _(dve):
                dve.memset(ones[:, :], 1.0)
                dve.wait_ge(iotas, 2)
                dve.tensor_copy(iota_col[:, :], iota_pi[:, :])
                dve_step.done(dve.tensor_copy(iota_row[:, :], iota_i[:, :]), dve)
                dve.tensor_copy(iota_bf[:, :], iota_row[:, :])
                dve.tensor_scalar(ident[:, :], iota_row[:, :], iota_col[:, :], None, ALU.is_equal)
                dve.tensor_scalar(ident_bf[:, :], iota_row[:, :], iota_col[:, :], None, ALU.is_equal)
                dve.memset(before[:, 0:P], 1.0)
                dve.tensor_scalar(before[:, P:2 * P], iota_row[:, :], iota_col[:, :], None, ALU.is_lt)
                dve_step.done(dve.tensor_scalar(after[:, :], iota_row[:, :], iota_col[:, :], None, ALU.is_gt), dve)

        class Sort:
            pass

        def start_sort(g, src_ap, dst_ap, E, C, may_be_sorted):
            q = Sort()
            q.g, q.C = g, C
            q.rows = (sorted1, sorted2)[g]
            place = q.place = Place()
            q.cols = place([C, 4])
            q.fill = place([FILL, 4])
            q.flag = place([8], i32)
            kept = place.at
            src_i, dst_i, next_i = place([C], i32), place([C], i32), place([C], i32)
            key_i, part_i = place([C], i32), place([C], i32)
            worst = place([1])
            cols, fill = q.cols, q.fill
            full = E // C

            def spread_out(to, of, n):
                f = n // C
                load(nc.sync, to[0:f, :], of[0:f * C].rearrange("(p c) -> p c", c=C))
                if n > f * C:
                    load(nc.sync, to[f:f + 1, 0:n - f * C], of[f * C:n].rearrange("(a c) -> a c", a=1))

            with stage_of() as block:
                clean, disorder, judged = sem("clean"), sem("disorder"), sem("judged")

                @block.sync
                def _(sp):
                    sp.wait_ge(clean, 1)
                    spread_out(src_i, src_ap, E)
                    spread_out(dst_i, dst_ap, E)
                    if may_be_sorted:
                        spread_out(next_i, dst_ap[1:E], E - 1)

                want = loaded[0]

                @block.vector
                def _(dve):
                    dve.memset(src_i, 0)
                    if may_be_sorted:
                        dve.memset(next_i, INVALID - 1)
                    dve.memset(dst_i, INVALID - 1).then_inc(clean, 1)
                    dve.memset(fill[:, :, 0:1], 0.0)
                    dve.memset(fill[:, :, 1:2], 2.0 * INVALID)
                    dve.memset(fill[:, :, 2:4], 2.0 * P)
                    dve.wait_ge(loads, want)
                    if may_be_sorted:
                        dve_step.done(dve.tensor_tensor(part_i, dst_i, next_i, ALU.is_gt), dve)
                        dve.tensor_reduce(worst, part_i, AX.X, ALU.max).then_inc(disorder, 1)
                    dve_step.done(dve.tensor_scalar(key_i, dst_i, float(N), float(INVALID), ALU.is_ge, ALU.mult), dve)
                    dve_step.done(dve.tensor_tensor(key_i, key_i, dst_i, ALU.add), dve)
                    dve.tensor_scalar(cols[:, :, 0:1].rearrange("p c a -> p (c a)"), src_i, float(N - 1), None, ALU.min)
                    dve.tensor_copy(cols[:, :, 1:2].rearrange("p c a -> p (c a)"), key_i)
                    dve_step.done(dve.tensor_scalar(part_i, key_i, P - 1, None, ALU.bitwise_and), dve)
                    dve_step.done(dve.tensor_copy(cols[:, :, 2:3].rearrange("p c a -> p (c a)"), part_i), dve)
                    dve_step.done(dve.tensor_scalar(part_i, key_i, 7, None, ALU.logical_shift_right), dve)
                    dve_step.done(dve.tensor_copy(cols[:, :, 3:4].rearrange("p c a -> p (c a)"), part_i), dve)
                    if may_be_sorted:
                        dve.wait_ge(judged, 1)
                        dve_step.done(dve.tensor_scalar(q.flag[:, 0:1], psum[:, 0, 0:1], 0.0, None, ALU.is_equal), dve)

                if may_be_sorted:
                    @block.tensor
                    def _(pe):
                        pe.wait_ge(disorder, 1)
                        pe.matmul(psum[:, 0, 0:1], ones[:, :], worst, start=True, stop=True).then_inc(judged, 1)

            place.at = kept
            stage = place([RING, 4])
            hot_lo = place([RING, P], bf16)
            hot_hi = place([RING, NB], bf16)
            ends = place([NB])
            hist, total, within = psum[:, 0, 0:NB], psum[:, 1, 0:NB], psum[:, 2, 0:NB]

            with stage_of() as block:
                staged, hot, counted, summed = sem("staged"), sem("hot"), sem("counted"), sem("summed")

                @block.scalar
                def _(act):
                    def body(k):
                        for b in range(2):
                            wait(act, hot, 2 * k + b - 1)
                            act.copy(stage[:, b * U:b * U + U, :], cols[:, bass.ds(k * RING + b * U, U), :]).then_inc(staged, 1)
                    turns(act, C // RING, body)

                @block.vector
                def _(dve):
                    def body(k):
                        for b in range(2):
                            dve.wait_ge(staged, 2 * k + b + 1)
                            wait(dve, counted, (2 * k + b - 1) * U)
                            one_hots(dve, hot_lo, hot_hi, stage, b * U, b * U).then_inc(hot, 1)
                    turns(dve, C // RING, body)
                    dve.wait_ge(counted, C)
                    dve.tensor_copy(counts[g][:, :], hist).then_inc(summed, 1)
                    dve.wait_ge(summed, 2)
                    dve_step.done(dve.tensor_tensor_scan(ends, ones[:, 0:NB], total, 0.0, ALU.mult, ALU.add), dve)
                    dve_step.done(dve.tensor_tensor(block_start[g][:, :], ends, total, ALU.subtract), dve)
                    dve_step.done(dve.tensor_tensor(starts[g][:, :], block_start[g][:, :], within, ALU.add), dve)

                @block.tensor
                def _(pe):
                    def body(k):
                        for b in range(2):
                            pe.wait_ge(hot, 2 * k + b + 1)
                            for u in range(b * U, b * U + U):
                                first = isinstance(k, int) and u == 0
                                pe.matmul(hist, hot_lo[:, u, :], hot_hi[:, u, :], start=first, stop=True,
                                          skip_group_check=True).then_inc(counted, 1)
                    turns(pe, C // RING, body)
                    pe.wait_ge(summed, 1)
                    pe.matmul(total, ones[:, :], counts[g][:, :], start=True, stop=True)
                    pe.matmul(within, after[:, :], counts[g][:, :], start=True, stop=True).then_inc(summed, 1)
            place.at = kept
            return q

        def one_hots(dve, hot_lo, hot_hi, stage, to, of):
            for u in range(U):
                dve.tensor_scalar(hot_lo[:, to + u, :], iota_bf[:, :], stage[:, of + u, 2:3], None, ALU.is_equal)
            return dve.tensor_tensor(hot_hi[:, to:to + U, :], iota_bf3[:, :, 0:NB].to_broadcast([P, U, NB]),
                                     stage[:, of:of + U, 3:4].to_broadcast([P, U, NB]), ALU.is_equal)

        def scatter_sorted(q, only_unsorted):
            g, C, rows, cols, fill, place = q.g, q.C, q.rows, q.cols, q.fill, q.place
            SR = 4 * U
            stage = place([SR, 4])
            stage_bf = place([SR, 2], bf16)
            hot_lo = place([RING, P], bf16)
            hot_hi = place([RING, NB], bf16)
            hot_loT = place([U, P])
            place_of = place([2, NB])
            scrap, picked = place([U, 2 * P]), place([U, NB])
            rank, looked = place([RING]), place([RING])
            skip = place([RING])
            row_u = place([SR], u32)
            heap = psum[:, 0, 0:NB]
            look = [psum[:, 1 + b, 0:U * NB].rearrange("p (u c) -> p u c", c=NB) for b in range(2)]
            key_rows = psum[:, 3:5, :].rearrange("p b c -> p (b c)")
            turned = psum[:, 5, :].bitcast(bf16).rearrange("p (u c) -> p u c", c=P)
            TURNS = C // SR
            assert C % SR == 0

            with stage_of() as block:
                names = ("staged", "heap_set", "place_set", "keys_made", "hot_made", "keys_used", "hot_turned",
                         "hotT_made", "looked", "moved", "ranked", "list_done", "list_back", "filled", "paced")
                (staged, heap_set, place_set, keys_made, hot_made, keys_used, hot_turned,
                 hotT_made, looked_up, moved, ranked, list_done, list_back, filled, paced) = (sem(n) for n in names)
                scattered = [sem(f"scattered{b}") for b in range(4)]
                rank_step = Steps(sem("rank_step"))

                def unless_sorted(eng, program):
                    if only_unsorted:
                        with eng.If(eng.value_load(q.flag[0:1, 0:1], min_val=0, max_val=1) == 0):
                            program(eng)
                    else:
                        program(eng)

                @block.sync
                def _(sp):
                    def program(sp):
                        nrow = rows.shape[0]
                        sp.dma_start(rows[0:1, :], fill[0:1, 0, :]).then_inc(filled, 16)
                        body = rows[1:nrow, :].rearrange("(p c) f -> p c f", p=P)
                        at, made = 0, 16
                        while at < C:
                            m = min(FILL, C - at)
                            sp.dma_start(body[:, at:at + m, :], fill[:, 0:m, :]).then_inc(filled, 16)
                            at, made = at + m, made + 16
                        sp.wait_ge(filled, made)
                        sp.sem_inc(paced, 1)
                        if only_unsorted:
                            sp.wait_ge(list_done, 1)
                            sp.dma_start(cols, body).then_inc(list_back, 16)
                            sp.wait_ge(list_back, 16)
                    unless_sorted(sp, program)

                @block.scalar
                def _(act):
                    def stage_half(k, b):
                        wait(act, scattered[b], k * (16 * U))
                        half = slice(b * U, b * U + U)
                        act.copy(stage[:, half, :], cols[:, bass.ds(k * SR + b * U, U), :])
                        act.copy(stage_bf[:, half, 0:1], cols[:, bass.ds(k * SR + b * U, U), 2:3])
                        act.mul(stage_bf[:, half, 1:2], cols[:, bass.ds(k * SR + b * U, U), 3:4], float(P)).then_inc(staged, 1)

                    def program(act):
                        act.wait_ge(heap_set, 1)
                        act.copy(place_of[:, 0, :], heap).then_inc(place_set, 1)
                        stage_half(0, 0)

                        def body(k, last):
                            for b in range(4):
                                act.wait_ge(hot_turned, 4 * k + b + 1)
                                act.copy(hot_loT, turned).then_inc(hotT_made, 1)
                                if b < 3:
                                    stage_half(k, b + 1)
                                elif not last:
                                    stage_half(k + 1, 0)
                                for v in range(U // 2):
                                    act.wait_ge(moved, k * (SR // 2) + (b * (U // 2) + v + 1))
                                    act.copy(place_of[:, (v + 1) % 2, :], heap).then_inc(place_set, 1)
                        turns_ahead(act, TURNS, body)
                    unless_sorted(act, program)

                @block.tensor
                def _(pe):
                    def program(pe):
                        pe.matmul(heap, ident[:, :], starts[g][:, :], start=True, stop=True).then_inc(heap_set, 1)

                        def body(k):
                            for b in range(4):
                                j = 4 * k + b
                                pe.wait_ge(staged, j + 1)
                                wait(pe, keys_used, j)
                                for u in range(U):
                                    lo = stage_bf[:, b * U + u, 0:1].to_broadcast([P, P])
                                    hi = stage_bf[:, b * U + u, 1:2].to_broadcast([P, P])
                                    pe.matmul(key_rows[:, u * P:(u + 1) * P], hi, ident_bf[:, :], start=True, stop=False)
                                    last = pe.matmul(key_rows[:, u * P:(u + 1) * P], lo, ident_bf[:, :], start=False, stop=True)
                                last.then_inc(keys_made, 1)
                                pe.wait_ge(hot_made, j + 1)
                                for u in range(U):
                                    last = pe.transpose(turned[:, u, :], hot_lo[:, (b % 2) * U + u, :], ident_bf[:, :])
                                last.then_inc(hot_turned, 1)
                                pe.wait_ge(hotT_made, j + 1)
                                wait(pe, ranked, j - 1)
                                for v in range(U // 2):
                                    pe.wait_ge(place_set, k * (SR // 2) + (b * (U // 2) + v + 1))
                                    for u in (2 * v, 2 * v + 1):
                                        r = (b % 2) * U + u
                                        last = pe.matmul(heap, hot_lo[:, r, :], hot_hi[:, r, :], start=False, stop=True,
                                                         skip_group_check=True)
                                    last.then_inc(moved, 1)
                                    for u in (2 * v, 2 * v + 1):
                                        last = pe.matmul(look[b % 2][:, u, :], hot_loT[:, u, :], place_of[:, v % 2, :], start=True, stop=True)
                                last.then_inc(looked_up, 1)
                        turns(pe, TURNS, body)
                    unless_sorted(pe, program)

                @block.vector
                def _(dve):
                    def program(dve):
                        dve.wait_ge(staged, 1)
                        one_hots(dve, hot_lo, hot_hi, stage, 0, 0).then_inc(hot_made, 1)

                        def body(k, last):
                            for b in range(4):
                                j = 4 * k + b
                                half = slice((b % 2) * U, (b % 2) * U + U)
                                out_half = slice(b * U, b * U + U)
                                dve.wait_ge(keys_made, j + 1)
                                for u in range(U):
                                    r, w = b * U + u, P * (1 + u % 2)
                                    done = dve.scalar_tensor_tensor(scrap[:, u, 0:w], key_rows[:, (u - u % 2) * P:(u + 1) * P],
                                                                    stage[:, r, 1:2], before[:, 2 * P - w:2 * P],
                                                                    ALU.is_equal, ALU.mult, accum_out=rank[:, (b % 2) * U + u:(b % 2) * U + u + 1])
                                done.then_inc(keys_used, 1)
                                dve.tensor_scalar(skip[:, half], stage[:, out_half, 1:2].rearrange("p u a -> p (u a)"), float(INVALID), SKIP,
                                                  ALU.is_ge, ALU.mult)
                                if not (last and b == 3):
                                    dve.wait_ge(staged, j + 2)
                                    one_hots(dve, hot_lo, hot_hi, stage, ((b + 1) % 2) * U, ((b + 1) % 4) * U).then_inc(hot_made, 1)
                                dve.wait_ge(looked_up, j + 1)
                                rank_step.done(dve.tensor_tensor(picked, look[b % 2], hot_hi[:, half, :], ALU.mult), dve)
                                rank_step.done(dve.tensor_reduce(looked[:, half], picked, AX.X, ALU.add), dve)
                                rank_step.done(dve.scalar_tensor_tensor(rank[:, half], rank[:, half], 1.0, looked[:, half], ALU.add, ALU.add), dve)
                                dve.tensor_tensor(row_u[:, out_half], rank[:, half], skip[:, half], ALU.add).then_inc(ranked, 1)
                        turns_ahead(dve, TURNS, body, [rank_step], [12])
                    unless_sorted(dve, program)

                @block.gpsimd
                def _(pool):
                    def program(pool):
                        bound = pool.to_reg(rows.shape[0] - 1)
                        pool.wait_ge(paced, 1)

                        def body(k):
                            for b in range(4):
                                pool.wait_ge(ranked, 4 * k + b + 1)
                                pool.sem_inc(paced, 1)
                                for r in range(b * U, b * U + U):
                                    pool.indirect_dma_start(
                                        out=rows[:, :], out_offset=bass.IndirectOffsetOnAxis(ap=row_u[:, r:r + 1], axis=0),
                                        in_=stage[:, r, :], in_offset=None,
                                        bounds_check=bound, oob_is_err=False).then_inc(scattered[b], 16)
                        turns(pool, TURNS, body)
                        for b in range(4):
                            pool.wait_ge(scattered[b], 16 * U * TURNS)
                        pool.sem_inc(list_done, 1)
                    unless_sorted(pool, program)

        second = start_sort(1, edges[0], edges[1], E2, C2, False)
        scatter_sorted(second, False)
        first = start_sort(0, src, dst, E1, C1, True)
        scatter_sorted(first, True)

        place = Place()
        place.at = first.place.at
        CC = -(-S1 // P)
        cols = first.cols
        src_f, key_f = place([C1]), place([C1])
        srcs = src_rows.rearrange("r e -> (r e)").rearrange("(p c) -> p c", p=P)
        keys = key_rows_dram.rearrange("r e -> (r e)").rearrange("(p c) -> p c", p=P)
        first_i, last_i = place([NB], i32), place([NB], i32)
        first_f, last_f, taken, ends, shared = (place([NB]) for _ in range(5))
        seen, seen2 = place([NB]), place([NB])
        chunk_no, blocks, rows_back, base = (place([CC]) for _ in range(4))
        row_u, block_i = place([CC], u32), place([CC], i32)
        place.at = ARENA - 2 * CC * P
        got = got_of_chunks = place([2 * CC, P])
        with stage_of() as block:
            split, listed, rooted, chunks_made, copied = (sem(n) for n in ("split", "listed", "rooted", "chunks_made", "copied"))
            fetched_rows = sem("fetched_rows")

            @block.vector
            def _(dve):
                def do(ins):
                    dve_step.done(ins, dve)

                dve.tensor_copy(src_f, cols[:, :, 0:1].rearrange("p c a -> p (c a)"))
                dve.tensor_copy(key_f, cols[:, :, 1:2].rearrange("p c a -> p (c a)")).then_inc(split, 1)
                do(dve.tensor_scalar(dinv[:, :], counts[0][:, :], 1.0, None, ALU.add))
                dve.tensor_copy(small[:, 4, :], dinv[:, :]).then_inc(rooted, 1)
                do(dve.tensor_copy(first_i, block_start[0][:, :]))
                do(dve.tensor_scalar(first_i, first_i, 7, None, ALU.logical_shift_right))
                do(dve.tensor_copy(first_f, first_i))
                dve.memset(last_f[:, NB - 1:NB], float(E1 + P - 1))
                do(dve.tensor_scalar(last_f[:, 0:NB - 1], block_start[0][:, 1:NB], float(P - 1), None, ALU.add))
                do(dve.tensor_copy(last_i, last_f))
                do(dve.tensor_scalar(last_i, last_i, 7, None, ALU.logical_shift_right))
                do(dve.tensor_copy(last_f, last_i))
                do(dve.tensor_tensor(taken, last_f, first_f, ALU.subtract))
                do(dve.tensor_tensor_scan(ends, ones[:, 0:NB], taken, 0.0, ALU.mult, ALU.add))
                dve.memset(shared[:, NB - 1:NB], 0.0)
                do(dve.tensor_tensor(shared[:, 0:NB - 1], last_f[:, 0:NB - 1], first_f[:, 1:NB], ALU.subtract))
                do(dve.tensor_scalar(chunk_no, iota_row[:, 0:CC], float(P), iota_col[:, :], ALU.mult, ALU.add))
                for c in range(CC):
                    dve.tensor_scalar(seen, ends, chunk_no[:, c:c + 1], 0.0, ALU.is_le, ALU.add, accum_out=blocks[:, c:c + 1])
                    do(dve.scalar_tensor_tensor(seen2, ends, chunk_no[:, c:c + 1], shared, ALU.is_le, ALU.mult,
                                                accum_out=rows_back[:, c:c + 1]))
                do(dve.tensor_scalar(blocks, blocks, float(NB - 1), None, ALU.min))
                do(dve.tensor_copy(block_i, blocks))
                do(dve.tensor_tensor(rows_back, chunk_no, rows_back, ALU.subtract))
                dve.tensor_scalar(row_u, rows_back, float(C1 - 1), None, ALU.min).then_inc(chunks_made, 1)
                do(dve.tensor_scalar(base, blocks, float(P), None, ALU.mult))
                dve.wait_ge(rooted, 2)
                do(dve.reciprocal(dinv[:, :], small[:, 5, :]))
                dve.wait_ge(fetched_rows, 32 * CC)
                for c in range(CC):
                    last = dve.tensor_scalar(got[:, CC + c, :], got[:, CC + c, :], base[:, c:c + 1], None, ALU.subtract)
                do(last)

            @block.scalar
            def _(act):
                act.wait_ge(rooted, 1)
                act.activation(small[:, 5, :], small[:, 4, :], ACT.Sqrt).then_inc(rooted, 1)

            @block.sync
            def _(sp):
                sp.wait_ge(split, 1)
                sp.dma_start(srcs, src_f).then_inc(listed, 16)
                sp.dma_start(keys, key_f).then_inc(listed, 16)
                sp.wait_ge(chunks_made, 1)
                with nc.allow_non_contiguous_dma("a few words"):
                    sp.dma_start(chunk_dram.rearrange("(c p) -> p c", p=P), block_i).then_inc(copied, 16)
                sp.wait_ge(copied, 16)

            @block.gpsimd
            def _(pool):
                pool.wait_ge(listed, 32)
                pool.wait_ge(chunks_made, 1)
                for i, table_ in enumerate((src_rows, key_rows_dram)):
                    for c in range(CC):
                        pool.indirect_dma_start(
                            out=got[:, i * CC + c, :], out_offset=None, in_=table_[:, :],
                            in_offset=bass.IndirectOffsetOnAxis(ap=row_u[:, c:c + 1], axis=0),
                            bounds_check=C1 - 1, oob_is_err=False).then_inc(fetched_rows, 16)
                pool.wait_ge(fetched_rows, 32 * CC)

        place = Place()
        x_sb = place([NB, D])
        acc = place([NB, D])
        src_u = place([S1], u32)
        dst_lo = place([S1])
        assert place.at <= ARENA - 2 * CC * P
        fetched = place([RING, D])
        hot = place([RING, P])
        idx = place([RING], u32)
        lo_stage = place([RING])
        chunk_row = place([S1], i32)
        W_sb = place([KD, D])
        bias = place([D])
        SO = 7
        flat = fetched.rearrange("p r d -> p (r d)")
        o_ring = flat[:, 0:SO * D].rearrange("p (u d) -> p u d", d=D)
        oT_ring = flat[:, SO * D:2 * SO * D].rearrange("p (u k c) -> p u k c", k=KD, c=P)
        stats = place([NB, 6])
        mv = place([NB, 2])
        rstd = place([NB])
        got = got_of_chunks
        table_v = table.rearrange("(b p) f -> p b f", p=P)
        psum_T = psum[:, 0:4, 0:D].rearrange("p b (k c) -> p b k c", k=KD)
        psum_M = psum[:, 4:8, 0:D]

        def norm_stats(tag, before_it=None):
            with stage_of() as block:
                var_ready, root_ready = sem(f"var_ready{tag}"), sem(f"root_ready{tag}")

                @block.vector
                def _(dve):
                    if before_it:
                        before_it(dve)
                    for n in range(NB):
                        last = dve.bn_stats(stats[:, n, :], x_sb[:, n, :])
                    dve_step.done(last, dve)
                    for n in range(NB):
                        last = dve.bn_aggr(mv[:, n, :], stats[:, n, :])
                    dve_step.done(last, dve)
                    dve.tensor_scalar(rstd, mv[:, :, 1:2].rearrange("p n a -> p (n a)"), EPS, None, ALU.add).then_inc(var_ready, 1)
                    dve.wait_ge(root_ready, 1)
                    dve_step.done(dve.reciprocal(rstd, rstd), dve)

                @block.scalar
                def _(act):
                    act.wait_ge(var_ready, 1)
                    act.activation(rstd, rstd, ACT.Sqrt).then_inc(root_ready, 1)

        def project(tag, rows_of_block, width, finish, transposed_too=None, weights=None):
            with stage_of() as block:
                rows_ready, turned, T_ready, multiplied, ended, left, sent = (
                    sem(f"{n}{tag}") for n in ("rows_ready", "turned", "T_ready", "multiplied", "ended", "left", "sent"))
                t_out = sem(f"t_out{tag}")

                @block.vector
                def _(dve):
                    def body(k):
                        for u in range(SO):
                            wait(dve, turned, k * SO + (u + 1 - SO))
                            rows_of_block(dve, k * SO + u, o_ring[:, u, :]).then_inc(rows_ready, 1)
                    turns(dve, G7, body)

                @block.tensor
                def _(pe):
                    pe.wait_ge(loads, loaded[0])

                    def body(k):
                        for u in range(SO):
                            pe.wait_ge(rows_ready, k * SO + (u + 1))
                            wait(pe, T_ready, k * SO + max(u - 3, 0))
                            for c in range(KD):
                                last = pe.transpose(psum_T[:, u % 4, c, :], o_ring[:, u, c * P:(c + 1) * P], ident[:, :])
                            last.then_inc(turned, 1)
                        for u in range(SO):
                            pe.wait_ge(T_ready, k * SO + (u + 1))
                            wait(pe, ended, k * SO + max(u - 3, 0))
                            for c in range(KD):
                                last = pe.matmul(psum_M[:, u % 4, 0:width], oT_ring[:, u, c, :], weights[:, c, 0:width],
                                                 start=c == 0, stop=c == KD - 1)
                            last.then_inc(multiplied, 1)
                    turns(pe, G7, body)

                @block.scalar
                def _(act):
                    def body(k):
                        for u in range(SO):
                            act.wait_ge(turned, k * SO + (u + 1))
                            wait(act, multiplied, k * SO + (u + 1 - SO))
                            if transposed_too is not None:
                                wait(act, t_out, k * 16)
                            act.copy(oT_ring[:, u, :, :], psum_T[:, u % 4, :, :]).then_inc(T_ready, 1)
                        for u in range(SO):
                            act.wait_ge(multiplied, k * SO + (u + 1))
                            finish(act, k * SO + u, psum_M[:, u % 4, 0:width]).then_inc(ended, 1)
                    turns(act, G7, body)

                @block.sync
                def _(sp):
                    paced = sem(f"paced{tag}")

                    def body(k):
                        if transposed_too is None:
                            sp.wait_ge(ended, k * SO + SO)
                            sp.sem_inc(paced, 1)
                            sp.dma_start(table_v[:, bass.ds(k * SO, SO), :], acc[:, bass.ds(k * SO, SO), :]).then_inc(left, 16)
                        else:
                            sp.wait_ge(T_ready, k * SO + SO)
                            sp.sem_inc(paced, 1)
                            view = transposed_too[:, :, bass.ds(k * (SO * P), SO * P)]
                            for c in range(KD):
                                sp.dma_start(view[:, c, :].rearrange("p (u n) -> p u n", n=P), oT_ring[:, :, c, :]).then_inc(
                                    t_out if c == KD - 1 else left, 16)
                            sp.wait_ge(left, 16 * (k + 1))
                            sp.wait_ge(t_out, 16 * (k + 1))
                            sp.sem_inc(paced, 1)
                    turns(sp, G7, body)
                    sp.wait_ge(left, 16 * G7)

        with stage_of() as block:
            zeroed, col_made, col_used = sem("zeroed"), sem("col_made"), sem("col_used")

            @block.sync
            def _(sp):
                load(sp, chunk_row[0:1, :], chunk_dram[0:S1].rearrange("(a c) -> a c", a=1))
                sp.wait_ge(zeroed, 1)
                nf = N // P
                load(sp, x_sb[:, 0:nf, :], x[0:nf * P, :].rearrange("(b p) f -> p b f", p=P))
                load(sp, x_sb[0:N - nf * P, nf, :], x[nf * P:N, :])

            want = loaded[0]

            @block.tensor
            def _(pe):
                for n in range(2 * CC):
                    wait(pe, col_used, n - 7)
                    pe.transpose(psum[:, n % 8, 0:P], got[:, n, :], ident[:, :]).then_inc(col_made, 1)

            @block.vector
            def _(dve):
                dve.memset(x_sb[:, NB - 1, :], 0.0).then_inc(zeroed, 1)
                for n in range(2 * CC):
                    c = n % CC
                    m = min(P, S1 - c * P)
                    dve.wait_ge(col_made, n + 1)
                    to = (src_u, dst_lo)[n // CC]
                    dve.tensor_copy(to[:, c * P:c * P + m], psum[:, n % 8, 0:m]).then_inc(col_used, 1)
                dve.wait_ge(loads, want)

        norm_stats("a")

        def normed(dve, n, to):
            return dve.tensor_scalar(to, x_sb[:, bass.ds(n, 1), :].rearrange("p a f -> p (a f)"),
                                     mv[:, bass.ds(n, 1), 0:1].rearrange("p a f -> p (a f)"), rstd[:, bass.ds(n, 1)],
                                     ALU.subtract, ALU.mult)

        def conv_out(dve, n, to):
            return dve.scalar_tensor_tensor(to, acc[:, bass.ds(n, 1), :].rearrange("p a f -> p (a f)"),
                                            dinv[:, bass.ds(n, 1)], bias, ALU.mult, ALU.add)

        def scaled(act, n, got):
            return act.activation(acc[:, bass.ds(n, 1), :].rearrange("p a f -> p (a f)"), got, ACT.Copy,
                                  scale=dinv[:, bass.ds(n, 1)])

        def load_layer(layer):
            with stage_of() as block:
                @block.sync
                def _(sp):
                    load(sp, W_sb, gW[layer].rearrange("(k p) n -> p k n", p=P))
                    if layer:
                        load(sp, bias, gb[layer - 1].partition_broadcast(P))
                    sp.wait_ge(loads, loaded[0])

        def add_neighbours(layer):
            with stage_of() as block:
                names = ("idx_ready", "lo_ready", "hot_ready", "multiplied", "added")
                idx_ready, lo_ready, hot_ready, multiplied, added = (sem(f"c{layer}_{n}") for n in names)
                arrived = [sem(f"c{layer}_arrived{b}") for b in range(2)]
                slots = psum[:, :, 0:D]
                TURNS = S1 // RING

                @block.scalar
                def _(act):
                    def body(k):
                        for b in range(2):
                            half = slice(b * U, b * U + U)
                            wait(act, arrived[b], k * (16 * U))
                            act.copy(idx[:, half], src_u[:, bass.ds(k * RING + b * U, U)]).then_inc(idx_ready, 1)
                            wait(act, hot_ready, (2 * k + b - 1) * U)
                            act.copy(lo_stage[:, half], dst_lo[:, bass.ds(k * RING + b * U, U)]).then_inc(lo_ready, 1)
                    turns(act, TURNS, body)

                @block.gpsimd
                def _(pool):
                    paced = sem("paced")
                    bound = pool.to_reg(NP - 1)

                    def body(k):
                        for b in range(2):
                            pool.wait_ge(idx_ready, 2 * k + b + 1)
                            wait(pool, multiplied, (2 * k + b - 1) * U)
                            pool.sem_inc(paced, 1)
                            for r in range(b * U, b * U + U):
                                pool.indirect_dma_start(
                                    out=fetched[:, r, :], out_offset=None, in_=table[:, :],
                                    in_offset=bass.IndirectOffsetOnAxis(ap=idx[:, r:r + 1], axis=0),
                                    bounds_check=bound, oob_is_err=False).then_inc(arrived[b], 16)
                    turns(pool, TURNS, body)

                @block.vector
                def _(dve):
                    reg = [dve.alloc_register(f"blk{layer}_{u}") for u in range(U)]

                    def body(k):
                        for b in range(2):
                            dve.wait_ge(lo_ready, 2 * k + b + 1)
                            wait(dve, multiplied, (2 * k + b - 1) * U)
                            for r in range(b * U, b * U + U):
                                dve.tensor_scalar(hot[:, r, :], iota_row[:, :], lo_stage[:, r:r + 1], None, ALU.is_equal).then_inc(hot_ready, 1)
                            dve.load(reg, chunk_row[0:1, bass.ds(k * RING + b * U, U)])
                            for u in range(U):
                                n = k * RING + (b * U + u)
                                where = bass.ds(dve.snap(reg[u], min_val=0, max_val=NB - 1), 1)
                                to = acc[:, where, :].rearrange("p a f -> p (a f)")
                                dve.wait_ge(multiplied, n + 1)
                                wait(dve, added, n)
                                dve.tensor_tensor(to, to, slots[:, u, :], ALU.add).then_inc(added, 1)
                    turns(dve, TURNS, body)
                    dve.wait_ge(added, S1)

                @block.tensor
                def _(pe):
                    def body(k):
                        for b in range(2):
                            pe.wait_ge(arrived[b], (k + 1) * (16 * U))
                            for u in range(U):
                                n = k * RING + (b * U + u)
                                pe.wait_ge(hot_ready, n + 1)
                                wait(pe, added, n - U + 1)
                                pe.matmul(slots[:, u, :], hot[:, b * U + u, :], fetched[:, b * U + u, :], start=True, stop=True).then_inc(multiplied, 1)
                    turns(pe, TURNS, body)

        for layer in range(3):
            load_layer(layer)
            project(f"_l{layer}", conv_out if layer else normed, D, scaled, weights=W_sb)
            add_neighbours(layer)

        Wg = place([KD, HE])
        att = place([2, HE])
        last_bias = place([D])
        with stage_of() as block:
            stored = sem("x1_stored")
            x1_ready = sem("x1_ready")

            @block.sync
            def _(sp):
                load(sp, last_bias, gb[2].partition_broadcast(P))
                load(sp, Wg, W_gat.rearrange("(k p) n -> p k n", p=P))
                load(sp, att[:, 0, :], att_src.rearrange("h e -> (h e)").partition_broadcast(P))
                load(sp, att[:, 1, :], att_dst.rearrange("h e -> (h e)").partition_broadcast(P))
                sp.wait_ge(x1_ready, 1)
                sp.dma_start(x1_dram.rearrange("(b p) f -> p b f", p=P), x_sb).then_inc(stored, 16)
                sp.wait_ge(stored, 16)
                sp.wait_ge(loads, loaded[0])

            want = loaded[0]

            @block.vector
            def _(dve):
                dve.wait_ge(loads, want)
                for n in range(NB):
                    last = dve.scalar_tensor_tensor(acc[:, n, :], acc[:, n, :], dinv[:, n:n + 1], last_bias, ALU.mult, ALU.add)
                dve_step.done(last, dve)
                dve.tensor_tensor(x_sb, x_sb, acc, ALU.add).then_inc(x1_ready, 1)
                dve.wait_ge(x1_ready, 1)

        norm_stats("b")

        def features(act, n, got):
            return act.copy(node_feat[:, bass.ds(n, 1), 0:HE].rearrange("p a f -> p (a f)"), got)

        project("_gat", normed, HE, features, transposed_too=xT_dram, weights=Wg)

        attw = sb("attw", [P, 2, HE])
        place = Place()
        packed = place([NB, TW])
        prod = place([NB, HE])
        with stage_of() as block:
            stored, packed_ready = sem("table2_stored"), sem("packed_ready")

            @block.vector
            def _(dve):
                dve.memset(packed, 0.0)
                dve_step.done(dve.tensor_copy(attw[:, :, :], att), dve)
                for s in range(2):
                    dve_step.done(dve.tensor_tensor(prod, node_feat[:, :, 0:HE],
                                                    attw[:, s:s + 1, :].to_broadcast([P, NB, HE]), ALU.mult), dve)
                    dve_step.done(dve.tensor_reduce(node_feat[:, :, HE + H * s:HE + H * s + H],
                                                    prod.rearrange("p n (h e) -> p n h e", h=H), AX.X, ALU.add), dve)
                dve.tensor_copy(packed[:, :, 0:24], node_feat[:, :, :]).then_inc(packed_ready, 1)

            @block.sync
            def _(sp):
                sp.wait_ge(packed_ready, 1)
                sp.dma_start(table2.rearrange("(b p) f -> p b f", p=P), packed).then_inc(stored, 16)
                sp.wait_ge(stored, 16)

        place = Place()
        EW = HE + H
        edge = place([S2, EW])
        same = place([S2])
        apart = place([S2])
        idx2_all = place([S2 + RING], u32)
        fetched2 = place([RING, TW])
        idx2 = place([RING], u32)
        node_max = place([NB, H])
        node_pay = place([NB, 2 * H])
        node_sum = place([NB, EW])
        first_row, last_row = place([NB], u32), place([NB], u32)
        node_tmp = place([NB, H])
        node_tmp2 = place([NB, H])
        node_big = place([NB, HE])
        carry_rows = place([4, P])
        end_cols = place([2, 24])
        nt1, nt2 = place([NB]), place([NB])
        vecs = place([3, HE])
        all_same = place([1])
        shared_from = place.at
        far = place([S2, 2 * H])
        score = place([S2, H])
        maxed = place([S2, H])

        with stage_of() as block:
            rec_in, rec_used, vec_in = sem("rec2_in"), sem("rec2_used"), sem("vec_in")
            spread0 = sem("spread_zeroed")
            rv = sorted2[1:P * S2 + 1, :].rearrange("(p c) f -> p c f", c=S2)
            rprev = sorted2[0:P * S2, :].rearrange("(p c) f -> p c f", c=S2)
            recv = far.rearrange("p c f -> p (c f)")[:, 0:S2 * 4].rearrange("p (c f) -> p c f", f=4)

            @block.sync
            def _(sp):
                sp.dma_start(recv, rv).then_inc(rec_in, 16)
                sp.wait_ge(rec_used, 1)
                sp.dma_start(recv, rprev).then_inc(rec_in, 16)
                for i, v in enumerate((b_gat, ln_g, ln_b)):
                    sp.dma_start(vecs[:, i, :], v.partition_broadcast(P)).then_inc(vec_in, 16)
                sp.wait_ge(vec_in, 48)
                sp.wait_ge(rec_used, 2)
                sp.dma_start(spread.rearrange("(p c) f -> p c f", c=S2), far).then_inc(spread0, 16)
                sp.wait_ge(spread0, 16)

            @block.vector
            def _(dve):
                dve.memset(node_max, -BIG)
                dve.memset(node_sum, 0.0)
                dve.wait_ge(rec_in, 16)
                dve.memset(idx2_all[:, S2:S2 + RING], 0)
                dve.tensor_copy(idx2_all[:, 0:S2], recv[:, :, 0:1].rearrange("p c a -> p (c a)"))
                dve.tensor_copy(same, recv[:, :, 1:2].rearrange("p c a -> p (c a)")).then_inc(rec_used, 1)
                dve.wait_ge(rec_in, 32)
                dve_step.done(dve.tensor_tensor(same, same, recv[:, :, 1:2].rearrange("p c a -> p (c a)"), ALU.is_equal), dve)
                dve.memset(far, 0.0).then_inc(rec_used, 1)
                dve_step.done(dve.tensor_scalar(apart, same, 1.0, BIG, ALU.subtract, ALU.mult), dve)
                dve_step.done(dve.tensor_reduce(all_same, same, AX.X, ALU.min), dve)
                dve_step.done(dve.tensor_scalar(nt1, counts[1][:, :], 0.0, SKIP, ALU.is_equal, ALU.mult), dve)
                dve_step.done(dve.tensor_tensor(nt2, nt1, starts[1][:, :], ALU.add), dve)
                dve.tensor_copy(first_row, nt2)
                dve_step.done(dve.tensor_tensor(nt1, nt2, counts[1][:, :], ALU.add), dve)
                dve_step.done(dve.tensor_scalar(last_row, nt1, 1.0, None, ALU.subtract), dve)

        mlp = Place()
        mlp.at = shared_from
        GN = SO * P
        HN = GN // 2
        HT, YT = 2 * FC, SO
        PAIRS = G7 // 2
        assert G7 % 2 == 1
        W1_sb = mlp([NE * KD, F])
        W2_sb = mlp([NE * FC, D])
        b1_sb = mlp([NE, FC])
        b2_sb = mlp([NE, D])
        xT = mlp([2 * KD, GN])
        hh = mlp([2 * FC, GN])
        y_ring = mlp([YT, D])
        psum_H = psum[:, 0:4, 0:HN]
        psum_Y = psum[:, 4:8, 0:D]

        def groups(eng, one, steps=(), per=()):
            def body(k):
                for s in range(2):
                    one(2 * k + s, s, k)
            turns(eng, PAIRS, body, steps, per)
            one(G7 - 1, 0, PAIRS)

        with stage_of() as block:
            idx_ready, copied2 = sem("idx_ready"), sem("copied")
            arrived2 = [sem(f"arrived{b}") for b in range(2)]
            w_in, hid, gelud, y_made, y_taken, up_done = (sem(n) for n in ("w_in", "hid", "gelud", "y_made", "y_taken", "up_done"))
            x_in = [sem(f"x_in{i}") for i in range(2)]
            y_out = [sem(f"y_out{u}") for u in range(YT)]
            paced, sp_paced = sem("paced"), sem("sp_paced")

            @block.gpsimd
            def _(pool):
                bound = pool.to_reg(NP - 1)

                def body(k):
                    for b in range(2):
                        pool.wait_ge(idx_ready, 2 * k + b + 1)
                        wait(pool, copied2, 2 * k + b - 1)
                        pool.sem_inc(paced, 1)
                        for r in range(b * U, b * U + U):
                            pool.indirect_dma_start(
                                out=fetched2[:, r, :], out_offset=None, in_=table2[:, :],
                                in_offset=bass.IndirectOffsetOnAxis(ap=idx2[:, r:r + 1], axis=0),
                                bounds_check=bound, oob_is_err=False).then_inc(arrived2[b], 16)
                turns(pool, S2 // RING, body)

            @block.vector
            def _(dve):
                dve.tensor_copy(idx2[:, 0:U], idx2_all[:, 0:U]).then_inc(idx_ready, 1)
                dve.tensor_copy(idx2[:, U:RING], idx2_all[:, U:RING]).then_inc(idx_ready, 1)

                def body(k):
                    for b in range(2):
                        half = slice(b * U, b * U + U)
                        dve.wait_ge(arrived2[b], (k + 1) * (16 * U))
                        dve.tensor_copy(idx2[:, half], idx2_all[:, bass.ds(k * RING + (RING + b * U), U)]).then_inc(idx_ready, 1)
                        dve.tensor_copy(edge[:, bass.ds(k * RING + b * U, U), :], fetched2[:, half, 0:EW]).then_inc(copied2, 1)
                turns(dve, S2 // RING, body)
                dve.wait_ge(copied2, 2 * (S2 // RING))

            @block.sync
            def _(sp):
                sp.dma_start(W1_sb, W1.rearrange("e (k p) f -> p (e k) f", p=P)).then_inc(w_in, 16)
                sp.dma_start(W2_sb, W2.rearrange("e (c p) d -> p (e c) d", p=P)).then_inc(w_in, 16)
                with nc.allow_non_contiguous_dma("biases, one word a row"):
                    for e in range(NE):
                        sp.dma_start(b1_sb[:, e, :], b1[e].rearrange("(c p) -> p c", p=P)).then_inc(w_in, 16)
                sp.dma_start(b2_sb[0:1, :, :], b2.rearrange("(a e) d -> a e d", a=1)).then_inc(w_in, 16)

                def fetch(t, s):
                    wait(sp, up_done, t - 1)
                    sp.sem_inc(sp_paced, 1)
                    sp.dma_start(xT[:, s * KD:(s + 1) * KD, :], xT_dram[:, :, bass.ds(t * GN, GN)]).then_inc(x_in[s], 16)

                fetch(0, 0)

                def one(t, s, k):
                    if not (isinstance(t, int) and t == G7 - 1):
                        fetch(t + 1, 1 - s)
                    for e in range(NE):
                        for u in range(YT):
                            sp.wait_ge(y_taken, t * (NE * YT) + (e * YT + u + 1))
                            sp.sem_inc(sp_paced, 1)
                            sp.dma_start(y_dram[e, bass.ds(t * GN + u * P, P), :], y_ring[:, u, :]).then_inc(y_out[u], 16)
                groups(sp, one)
                for u in range(YT):
                    sp.wait_ge(y_out[u], 16 * G7 * NE)

            @block.tensor
            def _(pe):
                pe.wait_ge(w_in, 16 * (3 + NE))

                def up(t, s, k, e):
                    if e == 0:
                        pe.wait_ge(x_in[s], (k + 1) * 16)
                    for i in range(HT):
                        fc, half = i // 2, i % 2
                        wait(pe, gelud, t * (NE * HT) + (e * HT + i - 3))
                        for c in range(KD):
                            last = pe.matmul(psum_H[:, i % 4, :], W1_sb[:, e * KD + c, fc * P:(fc + 1) * P],
                                             xT[:, s * KD + c, half * HN:(half + 1) * HN], start=c == 0, stop=c == KD - 1)
                        last.then_inc(hid, 1)

                def down(t, s, k, e):
                    pe.wait_ge(gelud, t * (NE * HT) + (e + 1) * HT)
                    for u in range(YT):
                        wait(pe, y_taken, t * (NE * YT) + (e * YT + max(u - 3, 0)))
                        for fc in range(FC):
                            pe.matmul(psum_Y[:, u % 4, :], hh[:, (e % 2) * FC + fc, u * P:(u + 1) * P], W2_sb[:, e * FC + fc, :],
                                      start=fc == 0, stop=False)
                        last = pe.matmul(psum_Y[:, u % 4, :], ones[0:1, :], b2_sb[0:1, e, :], start=False, stop=True)
                        last.then_inc(y_made, 1)

                def one(t, s, k):
                    up(t, s, k, 0)
                    for e in range(NE):
                        if e + 1 < NE:
                            up(t, s, k, e + 1)
                        down(t, s, k, e)
                    pe.sem_inc(up_done, 1)
                groups(pe, one)

            @block.scalar
            def _(act):
                act.wait_ge(w_in, 16 * (3 + NE))

                def gelu(t, e):
                    wait(act, y_made, t * (NE * YT) + (e - 1) * YT)
                    for i in range(HT):
                        fc, half = i // 2, i % 2
                        act.wait_ge(hid, t * (NE * HT) + (e * HT + i + 1))
                        act.activation(hh[:, (e % 2) * FC + fc, half * HN:(half + 1) * HN], psum_H[:, i % 4, :], ACT.Gelu,
                                       bias=b1_sb[:, e, fc:fc + 1]).then_inc(gelud, 1)

                def one(t, s, k):
                    gelu(t, 0)
                    for e in range(NE):
                        if e + 1 < NE:
                            gelu(t, e + 1)
                        for u in range(YT):
                            wait(act, y_out[u], t * (16 * NE) + 16 * e)
                            act.wait_ge(y_made, t * (NE * YT) + (e * YT + u + 1))
                            act.copy(y_ring[:, u, :], psum_Y[:, u % 4, :]).then_inc(y_taken, 1)
                groups(act, one)

        def segment_scan(tag, width, data, result, gate, op0, neutral):
            with stage_of() as block:
                scanned, turned, combined, back = (sem(f"{n}{tag}") for n in ("scanned", "turned", "combined", "back"))
                ends, gates_ = end_cols[:, 0, 0:width], end_cols[:, 1, 0:width]
                T1, T2 = psum[0:width, 0, 0:P], psum[0:width, 1, 0:P]
                R1, R2, R3, R4 = (carry_rows[0:width, i, :] for i in range(4))
                TB = psum[:, 2, 0:width]

                @block.vector
                def _(dve):
                    for f in range(width):
                        last = dve.tensor_tensor_scan(result(f), gate, data(f), neutral, op0[0], op0[1])
                    dve_step.done(last, dve)
                    for f in range(width):
                        dve.tensor_copy(ends[:, f:f + 1], result(f)[:, S2 - 1:S2])
                        if neutral == 0.0:
                            last = dve.tensor_copy(gates_[:, f:f + 1], all_same)
                        else:
                            last = dve.tensor_scalar(gates_[:, f:f + 1], all_same, 1.0, BIG, ALU.subtract, ALU.mult)
                    last.then_inc(scanned, 1)
                    dve.wait_ge(turned, 1)
                    dve.tensor_copy(R1, T1)
                    dve_step.done(dve.tensor_copy(R2, T2), dve)
                    dve_step.done(dve.tensor_tensor_scan(R3, R2, R1, neutral, op0[0], op0[1]), dve)
                    dve_step.done(dve.memset(R4, neutral), dve)
                    dve.tensor_copy(R4[:, 1:P], R3[:, 0:P - 1]).then_inc(combined, 1)
                    dve.wait_ge(back, 1)
                    dve_step.done(dve.tensor_copy(ends, TB), dve)
                    for f in range(width):
                        last = dve.tensor_tensor_scan(result(f), gate, data(f), ends[:, f:f + 1], op0[0], op0[1])
                    dve_step.done(last, dve)

                @block.tensor
                def _(pe):
                    pe.wait_ge(scanned, 1)
                    pe.transpose(T1, ends, ident[:, :])
                    pe.transpose(T2, gates_, ident[:, :]).then_inc(turned, 1)
                    pe.wait_ge(combined, 1)
                    pe.transpose(TB, R4, ident[0:width, 0:width]).then_inc(back, 1)

        def column(t, f):
            return t[:, :, f:f + 1].rearrange("p c a -> p (c a)")

        def node_rows(tag, tensor, to, rows, scatter):
            with stage_of() as block:
                moved = sem(f"node_moved{tag}")

                @block.gpsimd
                def _(pool):
                    bound = pool.to_reg(P * S2 - 1)
                    for n in range(NB):
                        off = bass.IndirectOffsetOnAxis(ap=rows[:, n:n + 1], axis=0)
                        if scatter:
                            pool.indirect_dma_start(out=tensor[:, :], out_offset=off, in_=to[:, n, :], in_offset=None,
                                                    bounds_check=bound, oob_is_err=False).then_inc(moved, 16)
                        else:
                            pool.indirect_dma_start(out=to[:, n, :], out_offset=None, in_=tensor[:, :], in_offset=off,
                                                    bounds_check=bound, oob_is_err=False).then_inc(moved, 16)
                    pool.wait_ge(moved, 16 * NB)

        def move(tag, to, of):
            with stage_of() as block:
                moved = sem(f"moved{tag}")

                @block.sync
                def _(sp):
                    sp.dma_start(to, of).then_inc(moved, 16)
                    sp.wait_ge(moved, 16)

        segment_scan("_max", H, lambda f: column(edge, HE + f), lambda f: column(maxed, f), apart, (ALU.add, ALU.max), -BIG)
        move("_max", maxes.rearrange("(p c) f -> p c f", c=S2), maxed)
        node_rows("_max", maxes, node_max, last_row, False)

        with stage_of() as block:
            @block.vector
            def _(dve):
                a_src, a_dst = node_feat[:, :, HE:HE + H], node_feat[:, :, HE + H:HE + 2 * H]
                dve.tensor_copy(node_pay[:, :, 0:H], a_dst)
                dve_step.done(dve.tensor_tensor(node_max, node_max, a_src, ALU.max), dve)
                dve_step.done(dve.tensor_tensor(node_tmp, node_max, a_dst, ALU.add), dve)
                dve_step.done(dve.scalar_tensor_tensor(node_pay[:, :, H:2 * H], node_tmp, 0.2, node_tmp, ALU.mult, ALU.max), dve)
        node_rows("_pay", spread, node_pay, first_row, True)
        move("_pay", far, spread.rearrange("(p c) f -> p c f", c=S2))

        segment_scan("_far0", H, lambda f: column(far, f), lambda f: column(score, f), same, (ALU.mult, ALU.add), 0.0)
        segment_scan("_far1", H, lambda f: column(far, H + f), lambda f: column(maxed, f), same, (ALU.mult, ALU.add), 0.0)

        with stage_of() as block:
            raw_ready, exp_ready = sem("raw_ready"), sem("exp_ready")

            @block.vector
            def _(dve):
                a_src = edge[:, :, HE:HE + H]
                dve_step.done(dve.tensor_tensor(score, score, a_src, ALU.add), dve)
                dve_step.done(dve.scalar_tensor_tensor(far[:, :, 0:H], score, 0.2, score, ALU.mult, ALU.max), dve)
                dve.tensor_tensor(score, far[:, :, 0:H], maxed, ALU.subtract).then_inc(raw_ready, 1)
                dve.wait_ge(exp_ready, 1)
                for h in range(H):
                    part_ = edge[:, :, h * NE:(h + 1) * NE]
                    dve.tensor_tensor(part_, part_, score[:, :, h:h + 1].to_broadcast([P, S2, NE]), ALU.mult)
                dve_step.done(dve.tensor_copy(edge[:, :, HE:HE + H], score), dve)

            @block.scalar
            def _(act):
                act.wait_ge(raw_ready, 1)
                act.activation(score, score, ACT.Exp).then_inc(exp_ready, 1)


        for part_no, (f0, f1) in enumerate(((0, 8), (8, 16), (16, 20))):
            w = f1 - f0
            tgt = far if w == 8 else score
            segment_scan(f"_sum{part_no}", w, lambda f, f0=f0: column(edge, f0 + f), lambda f, tgt=tgt: column(tgt, f),
                         same, (ALU.mult, ALU.add), 0.0)
            with stage_of() as block:
                @block.vector
                def _(dve, f0=f0, f1=f1, tgt=tgt, w=w):
                    dve_step.done(dve.tensor_copy(edge[:, :, f0:f1], tgt[:, :, 0:w]), dve)
        move("_sum", sums.rearrange("(p c) f -> p c f", c=S2), edge)
        node_rows("_sum", sums, node_sum, last_row, False)

        with stage_of() as block:
            s_raw, s_exp, s_var, s_root = sem("s_raw"), sem("s_exp"), sem("s_var"), sem("s_root")
            a_src, a_dst = node_feat[:, :, HE:HE + H], node_feat[:, :, HE + H:HE + 2 * H]
            agg = node_sum[:, :, 0:HE]
            sc = node_tmp2

            @block.vector
            def _(dve):
                def do(ins):
                    dve_step.done(ins, dve)

                do(dve.tensor_tensor(node_tmp, a_src, a_dst, ALU.add))
                do(dve.scalar_tensor_tensor(node_tmp2, node_tmp, 0.2, node_tmp, ALU.mult, ALU.max))
                dve.tensor_tensor(node_tmp, node_tmp2, node_pay[:, :, H:2 * H], ALU.subtract).then_inc(s_raw, 1)
                dve.wait_ge(s_exp, 1)
                for h in range(H):
                    last = dve.tensor_tensor(node_big[:, :, h * NE:(h + 1) * NE], node_feat[:, :, h * NE:(h + 1) * NE],
                                             node_tmp[:, :, h:h + 1].to_broadcast([P, NB, NE]), ALU.mult)
                do(last)
                do(dve.tensor_tensor(agg, agg, node_big, ALU.add))
                do(dve.tensor_tensor(node_tmp2, node_sum[:, :, HE:EW], node_tmp, ALU.add))
                do(dve.tensor_scalar(node_tmp2, node_tmp2, 1e-16, None, ALU.add))
                do(dve.reciprocal(node_tmp, node_tmp2))
                for h in range(H):
                    last = dve.tensor_tensor(agg[:, :, h * NE:(h + 1) * NE], agg[:, :, h * NE:(h + 1) * NE],
                                             node_tmp[:, :, h:h + 1].to_broadcast([P, NB, NE]), ALU.mult)
                do(last)
                do(dve.tensor_tensor(agg, agg, vecs[:, 0:1, :].to_broadcast([P, NB, HE]), ALU.add))
                do(dve.tensor_reduce(nt1, agg, AX.X, ALU.add))
                do(dve.tensor_scalar(nt1, nt1, 1.0 / HE, None, ALU.mult))
                do(dve.tensor_tensor(agg, agg, nt1.rearrange("p (n a) -> p n a", a=1).to_broadcast([P, NB, HE]), ALU.subtract))
                do(dve.tensor_tensor(node_big, agg, agg, ALU.mult))
                do(dve.tensor_reduce(nt1, node_big, AX.X, ALU.add))
                dve.tensor_scalar(nt1, nt1, 1.0 / HE, EPS, ALU.mult, ALU.add).then_inc(s_var, 1)
                dve.wait_ge(s_root, 1)
                do(dve.reciprocal(nt2, nt1))
                do(dve.tensor_tensor(agg, agg, nt2.rearrange("p (n a) -> p n a", a=1).to_broadcast([P, NB, HE]), ALU.mult))
                do(dve.tensor_tensor(agg, agg, vecs[:, 1:2, :].to_broadcast([P, NB, HE]), ALU.mult))
                do(dve.tensor_tensor(agg, agg, vecs[:, 2:3, :].to_broadcast([P, NB, HE]), ALU.add))
                do(dve.tensor_reduce(sc, agg.rearrange("p n (h e) -> p n e h", h=H), AX.X, ALU.add))
                do(dve.tensor_scalar(sc, sc, 1.0 / H, None, ALU.mult))
                place_ = node_pay[:, :, 0:NE]
                do(dve.memset(place_, 0.0))
                for e in range(NE):
                    for o in range(NE):
                        if o != e:
                            do(dve.tensor_tensor(node_tmp[:, :, 0:1], sc[:, :, o:o + 1], sc[:, :, e:e + 1],
                                                 ALU.is_ge if o < e else ALU.is_gt))
                            do(dve.tensor_tensor(place_[:, :, e:e + 1], place_[:, :, e:e + 1], node_tmp[:, :, 0:1], ALU.add))
                do(dve.tensor_scalar(place_, place_, 1.5, None, ALU.is_lt))
                do(dve.tensor_reduce(nt1, sc, AX.X, ALU.max))
                dve.tensor_tensor(sc, sc, nt1.rearrange("p (n a) -> p n a", a=1).to_broadcast([P, NB, NE]), ALU.subtract).then_inc(s_raw, 1)
                dve.wait_ge(s_exp, 2)
                do(dve.tensor_tensor(gates[:, :, :], sc, place_, ALU.mult))
                do(dve.tensor_reduce(nt1, gates[:, :, :], AX.X, ALU.add))
                do(dve.reciprocal(nt2, nt1))
                do(dve.tensor_tensor(gates[:, :, :], gates[:, :, :], nt2.rearrange("p (n a) -> p n a", a=1).to_broadcast([P, NB, NE]), ALU.mult))

            @block.scalar
            def _(act):
                act.wait_ge(s_raw, 1)
                act.activation(node_tmp, node_tmp, ACT.Exp).then_inc(s_exp, 1)
                act.wait_ge(s_var, 1)
                act.activation(nt1, nt1, ACT.Sqrt).then_inc(s_root, 1)
                act.wait_ge(s_raw, 2)
                act.activation(sc, sc, ACT.Exp).then_inc(s_exp, 1)

        place = Place()
        ya = place([2 * SO, D])
        ye = place([2 * NE * SO, D])
        gate_ring = place([2 * SO, NE])
        out_v = out[0:(NB - 1) * P, :].rearrange("(b p) f -> p b f", p=P)
        x1_v = x1_dram.rearrange("(b p) f -> p b f", p=P)
        with stage_of() as block:
            added, paced = sem("added"), sem("paced")
            y_in, y_out = ([sem(f"{n}{i}") for i in range(2)] for n in ("y_in", "y_out"))
            A = NE * SO
            PARTS = 1 + NE

            @block.sync
            def _(sp):
                def fetch(t, s, k):
                    wait(sp, y_out[s], k * 16)
                    sp.sem_inc(paced, 1)
                    sp.dma_start(ya[:, s * SO:(s + 1) * SO, :], x1_v[:, bass.ds(t * SO, SO), :]).then_inc(y_in[s], 16)
                    for e in range(NE):
                        sp.dma_start(ye[:, (s * NE + e) * SO:(s * NE + e + 1) * SO, :],
                                     y_dram[e].rearrange("(b p) f -> p b f", p=P)[:, bass.ds(t * SO, SO), :]).then_inc(y_in[s], 16)

                def store(t, s, k):
                    sp.wait_ge(added, (t + 1) * A)
                    sp.sem_inc(paced, 1)
                    sp.dma_start(out_v[:, bass.ds(t * SO, SO), :], ya[:, s * SO:(s + 1) * SO, :]).then_inc(y_out[s], 16)

                def body(k, last):
                    store(2 * k, 0, k)
                    fetch(2 * k + 2, 0, k + 1)
                    store(2 * k + 1, 1, k)
                    if not last:
                        fetch(2 * k + 3, 1, k + 1)
                fetch(0, 0, 0)
                fetch(1, 1, 0)
                turns_ahead(sp, PAIRS, body)
                sp.wait_ge(added, G7 * A)
                sp.dma_start(out_v[:, (G7 - 1) * SO:NB - 1, :], ya[:, 0:SO - 1, :]).then_inc(y_out[0], 16)
                sp.dma_start(out[(NB - 1) * P:N, :], ya[0:N - (NB - 1) * P, SO - 1, :]).then_inc(y_out[1], 16)
                for s in range(2):
                    sp.wait_ge(y_out[s], 16 * (PAIRS + 1))

            @block.vector
            def _(dve):
                def one(t, s, k):
                    dve.wait_ge(y_in[s], (k + 1) * (16 * PARTS))
                    cut = slice(s * SO, (s + 1) * SO)
                    dve_step.done(dve.tensor_copy(gate_ring[:, cut, :], gates[:, bass.ds(t * SO, SO), :]), dve)
                    for e in range(NE):
                        for u in range(SO):
                            wait(dve, added, t * A + (e * SO + u - (SO - 1)))
                            to = ya[:, s * SO + u, :]
                            dve.scalar_tensor_tensor(to, ye[:, (s * NE + e) * SO + u, :], gate_ring[:, s * SO + u, e:e + 1], to,
                                                     ALU.mult, ALU.add).then_inc(added, 1)
                groups(dve, one, [dve_step], [2])


_INS = ['x', 'src', 'dst', 'L0_gnn_W1', 'L0_gnn_b1', 'L0_gnn_W2', 'L0_gnn_b2', 'L0_gnn_W3', 'L0_gnn_b3',
        'L0_ffn_W_gat', 'L0_ffn_att_src', 'L0_ffn_att_dst', 'L0_ffn_b_gat', 'L0_ffn_ln_gamma', 'L0_ffn_ln_beta',
        'L0_ffn_W1', 'L0_ffn_b1', 'L0_ffn_W2', 'L0_ffn_b2', 'L0_ffn_edge_index']


def build(nc, a, out):
    gnn_moe_kernel(nc, a['x'], a['src'], a['dst'],
                   [a[f'L0_gnn_W{i}'] for i in (1, 2, 3)], [a[f'L0_gnn_b{i}'] for i in (1, 2, 3)],
                   a['L0_ffn_W_gat'], a['L0_ffn_att_src'], a['L0_ffn_att_dst'], a['L0_ffn_b_gat'],
                   a['L0_ffn_ln_gamma'], a['L0_ffn_ln_beta'], a['L0_ffn_W1'], a['L0_ffn_b1'],
                   a['L0_ffn_W2'], a['L0_ffn_b2'], a['L0_ffn_edge_index'], out)


def kernel(**inputs):
    import numpy as _np
    import concourse.bacc as _bacc
    from concourse import mybir as _mybir
    from concourse.bass_utils import run_bass_kernel_spmd as _run

    nc = _bacc.Bacc("TRN2", target_bir_lowering=False, num_devices=1)
    arrays, args = {}, {}
    for name in _INS:
        a = _np.ascontiguousarray(inputs[name])
        arrays[f"in_{name}_dram"] = a
        args[name] = nc.dram_tensor(f"in_{name}_dram", a.shape, _mybir.dt.from_np(a.dtype), kind="ExternalInput").ap()
    out = nc.dram_tensor("out_0_dram", inputs['x'].shape, _mybir.dt.float32, kind="ExternalOutput").ap()
    build(nc, args, out)
    r = _run(nc, [arrays], core_ids=[0])
    return r.results[0]["out_0_dram"]
```

```python
import concourse.bass as bass
from concourse import mybir
from contextlib import ExitStack, contextmanager


class Steps:

    def __init__(self, sem):
        self.sem, self.n, self.base, self.k, self.per = sem, 0, 0, None, 0

    def enter(self, k, per):
        if isinstance(k, int):
            self.k = None
            return
        self.k, self.per, self.i = k, per, 0

    def leave(self, turns):
        if self.k is not None:
            assert self.i == self.per, (self.i, self.per)
            self.n += turns * self.per
            self.k = None

    def done(self, ins, eng):
        ins.then_inc(self.sem, 1)
        if self.k is None:
            self.n += 1
            eng.wait_ge(self.sem, self.n)
        else:
            self.i += 1
            eng.wait_ge(self.sem, (self.k - 1) * self.per + (self.n + self.i))


def wait(eng, sem, value):
    if isinstance(value, int) and value <= 0:
        return
    eng.wait_ge(sem, value)


def turns(eng, count, body, steps=(), per=()):
    body(0)
    if count > 1:
        with eng.Fori(1, count) as k:
            for s, p in zip(steps, per):
                s.enter(k, p)
            body(k)
        for s in steps:
            s.leave(count - 1)


def turns_ahead(eng, count, body, steps=(), per=()):
    body(0, count == 1)
    if count > 2:
        with eng.Fori(1, count - 1) as k:
            for s, p in zip(steps, per):
                s.enter(k, p)
            body(k, False)
        for s in steps:
            s.leave(count - 2)
    if count > 1:
        body(count - 1, True)


def gnn_moe_kernel(nc, x, src, dst, gW, gb, W_gat, att_src, att_dst, b_gat, ln_g, ln_b,
                   W1, b1, W2, b2, edges, out):
    f32, bf16 = mybir.dt.float32, mybir.dt.bfloat16
    i32, u32 = mybir.dt.int32, mybir.dt.uint32
    ALU, ACT, AX = mybir.AluOpType, mybir.ActivationFunctionType, mybir.AxisListType
    P = 128

    N, D = x.shape
    NB = -(-N // P)
    NP = NB * P
    E1, E2 = src.shape[0], edges.shape[1]
    NE, _, F = W1.shape
    H = att_src.shape[0]
    HE = H * NE
    KD, FC = D // P, F // P
    EPS = 1e-5
    U = 8
    RING = 2 * U
    C1 = -(-(-(-E1 // P)) // (4 * U)) * (4 * U)
    C2 = -(-(-(-E2 // P)) // (4 * U)) * (4 * U)
    S1 = -(-(-(-E1 // P) + NB) // RING) * RING
    S2 = C2
    assert E2 == P * C2 and NB % 7 == 0
    INVALID = 8192
    SKIP = float(1 << 20)
    BIG = 1e30
    G7 = NB // 7
    FILL = 512

    sorted1 = nc.dram_tensor("sorted1", (P * C1 + 1, 4), f32).ap()
    src_rows = nc.dram_tensor("src_rows", (C1, P), f32).ap()
    key_rows_dram = nc.dram_tensor("key_rows_dram", (C1, P), f32).ap()
    sorted2 = nc.dram_tensor("sorted2", (P * S2 + 1, 4), f32).ap()
    chunk_dram = nc.dram_tensor("chunk_block", (-(-S1 // P) * P,), i32).ap()
    table = nc.dram_tensor("table", (NP, D), f32).ap()
    x1_dram = nc.dram_tensor("x1_dram", (NP, D), f32).ap()
    xT_dram = nc.dram_tensor("xT_dram", (P, KD, NP), f32).ap()
    y_dram = nc.dram_tensor("y_dram", (NE, NP, D), f32).ap()
    LO, BLK = 7, 20
    CELLS = NB << BLK
    LANES = U
    adjacency = nc.dram_tensor("adjacency", (CELLS + (1 + LANES) * P, 1), f32).ap()
    adjacency_bf = nc.dram_tensor("adjacency_bf", (NB, P, NB * P), bf16).ap()
    COUNT_MAX = 256
    LANE_ROWS = C1 // LANES
    DEGREE_MAX = (LANE_ROWS - 3) * P
    TW = 32
    table2 = nc.dram_tensor("table2", (NP, TW), f32).ap()
    maxes = nc.dram_tensor("maxes", (P * S2, H), f32).ap()
    spread = nc.dram_tensor("spread", (P * S2, 2 * H), f32).ap()
    sums = nc.dram_tensor("sums", (P * S2, HE + H), f32).ap()

    ctx = ExitStack()
    with ctx:
        def sb(name, shape, dt=f32):
            return ctx.enter_context(nc.sbuf_tensor(name, shape, dt))

        def kept_sem(name):
            return ctx.enter_context(nc.semaphore(name))

        scope, names_made = [], []

        def sem(name):
            names_made.append(name)
            scope[-1].append(nc.alloc_semaphore(name=f"{name}_{names_made.count(name)}"))
            return scope[-1][-1]

        @contextmanager
        def stage_of():
            scope.append([])
            with nc.Block() as block:
                yield block
            nc.clear_and_free_semaphores(scope.pop())
            nc.all_engine_barrier()

        iota_row = sb("iota_row", [P, P])
        iota_col = sb("iota_col", [P, 1])
        iota_bf3 = sb("iota_bf3", [P, 1, P], bf16)
        iota_bf = iota_bf3[:, 0, :]
        ident = sb("ident", [P, P])
        ident_bf = sb("ident_bf", [P, P], bf16)
        before = sb("before", [P, 2 * P])
        after = sb("after", [P, P])
        ones = sb("ones", [P, P])
        iota_i = sb("iota_i", [P, P], i32)
        iota_pi = sb("iota_pi", [P, 1], i32)
        counts = [sb(f"counts{g}", [P, NB]) for g in range(2)]
        starts = [sb(f"starts{g}", [P, NB]) for g in range(2)]
        block_start = [sb(f"block_start{g}", [P, NB]) for g in range(2)]
        dinv = sb("dinv", [P, NB])
        small = sb("small", [P, 8, NB])
        small_i = sb("small_i", [P, 2, NB], i32)
        node_feat = sb("node_feat", [P, NB, 24])
        gates = sb("gates", [P, NB, NE])
        ARENA = 49600
        arena = sb("arena", [P, ARENA])
        psum = ctx.enter_context(nc.psum_tensor("psum", [P, 8, 512], f32))

        class Place:

            def __init__(self, end=ARENA):
                self.at, self.end = 0, end

            def __call__(self, shape, dt=f32):
                n = 1
                for s in shape:
                    n *= s
                words = n if dt != bf16 else -(-n // 2)
                words = -(-words // 8) * 8
                v = arena[:, self.at:self.at + words]
                self.at += words
                assert self.at <= self.end, self.at
                if dt != f32:
                    v = v.bitcast(dt)
                v = v[:, 0:n]
                if len(shape) == 2:
                    v = v.rearrange("p (a b) -> p a b", b=shape[1])
                elif len(shape) == 3:
                    v = v.rearrange("p (a b c) -> p a b c", b=shape[1], c=shape[2])
                return v

        dve_step = Steps(kept_sem("dve_step"))
        loads = kept_sem("loads")
        loaded = [0]

        def load(eng, to, of):
            eng.dma_start(to, of).then_inc(loads, 16)
            loaded[0] += 16

        cells_zero = kept_sem("cells_zero")
        cells_zeroed = [0]
        BY_BF16, BY_FLOAT, BY_ROWS = 0, 1, 2
        way = sb("way", [P, 2], i32)
        SHARES = 7
        largest = sb("largest", [P, (NB // (C2 // (16 * U))) * SHARES])

        with stage_of() as block:
            iotas = sem("iotas")
            zeros = arena[:, ARENA - NB * P:ARENA]

            @block.gpsimd
            def _(pool):
                pool.iota(iota_i[:, :], pattern=[[1, P]], base=0, channel_multiplier=0).then_inc(iotas, 1)
                pool.iota(iota_pi[:, :], pattern=[[0, 1]], base=0, channel_multiplier=1).then_inc(iotas, 1)

            @block.vector
            def _(dve):
                dve.memset(zeros, 0.0)
                dve.memset(ones[:, :], 1.0)
                dve.wait_ge(iotas, 2)
                dve.tensor_copy(iota_col[:, :], iota_pi[:, :])
                dve_step.done(dve.tensor_copy(iota_row[:, :], iota_i[:, :]), dve)
                dve.tensor_copy(iota_bf[:, :], iota_row[:, :])
                dve.tensor_scalar(ident[:, :], iota_row[:, :], iota_col[:, :], None, ALU.is_equal)
                dve.tensor_scalar(ident_bf[:, :], iota_row[:, :], iota_col[:, :], None, ALU.is_equal)
                dve.memset(before[:, 0:P], 1.0)
                dve.tensor_scalar(before[:, P:2 * P], iota_row[:, :], iota_col[:, :], None, ALU.is_lt)
                dve_step.done(dve.tensor_scalar(after[:, :], iota_row[:, :], iota_col[:, :], None, ALU.is_gt), dve)

        class Sort:
            pass

        def start_sort(g, src_ap, dst_ap, E, C, may_be_sorted, place, cols, after_loads=None):
            q = Sort()
            q.g, q.C = g, C
            q.rows = (sorted1, sorted2)[g]
            q.place = place
            q.cols = cols
            q.fill = place([FILL, 4])
            q.flag = place([8], i32)
            kept = place.at
            src_i, dst_i, next_i = place([C], i32), place([C], i32), place([C], i32)
            key_i, part_i = place([C], i32), place([C], i32)
            worst = place([1])
            cols, fill = q.cols, q.fill
            full = E // C

            def spread_out(to, of, n):
                f = n // C
                load(nc.sync, to[0:f, :], of[0:f * C].rearrange("(p c) -> p c", c=C))
                if n > f * C:
                    load(nc.sync, to[f:f + 1, 0:n - f * C], of[f * C:n].rearrange("(a c) -> a c", a=1))

            with stage_of() as block:
                clean, disorder, judged = sem("clean"), sem("disorder"), sem("judged")

                @block.sync
                def _(sp):
                    sp.wait_ge(clean, 1)
                    spread_out(src_i, src_ap, E)
                    spread_out(dst_i, dst_ap, E)
                    if may_be_sorted:
                        spread_out(next_i, dst_ap[1:E], E - 1)
                    if after_loads:
                        after_loads(sp)

                want = loaded[0]

                @block.vector
                def _(dve):
                    dve.memset(src_i, 0)
                    if may_be_sorted:
                        dve.memset(next_i, INVALID - 1)
                    dve.memset(dst_i, INVALID - 1).then_inc(clean, 1)
                    dve.memset(fill[:, :, 0:1], 0.0)
                    dve.memset(fill[:, :, 1:2], 2.0 * INVALID)
                    dve.memset(fill[:, :, 2:4], 2.0 * P)
                    dve.wait_ge(loads, want)
                    if may_be_sorted:
                        dve_step.done(dve.tensor_tensor(part_i, dst_i, next_i, ALU.is_gt), dve)
                        dve.tensor_reduce(worst, part_i, AX.X, ALU.max).then_inc(disorder, 1)
                    dve_step.done(dve.tensor_scalar(key_i, dst_i, float(N), float(INVALID), ALU.is_ge, ALU.mult), dve)
                    dve_step.done(dve.tensor_tensor(key_i, key_i, dst_i, ALU.add), dve)
                    dve.tensor_scalar(cols[:, :, 0:1].rearrange("p c a -> p (c a)"), src_i, float(N - 1), None, ALU.min)
                    dve.tensor_copy(cols[:, :, 1:2].rearrange("p c a -> p (c a)"), key_i)
                    dve_step.done(dve.tensor_scalar(part_i, key_i, P - 1, None, ALU.bitwise_and), dve)
                    dve_step.done(dve.tensor_copy(cols[:, :, 2:3].rearrange("p c a -> p (c a)"), part_i), dve)
                    dve_step.done(dve.tensor_scalar(part_i, key_i, 7, None, ALU.logical_shift_right), dve)
                    dve_step.done(dve.tensor_copy(cols[:, :, 3:4].rearrange("p c a -> p (c a)"), part_i), dve)
                    if may_be_sorted:
                        dve.wait_ge(judged, 1)
                        dve_step.done(dve.tensor_scalar(q.flag[:, 0:1], psum[:, 0, 0:1], 0.0, None, ALU.is_equal), dve)

                if may_be_sorted:
                    @block.tensor
                    def _(pe):
                        pe.wait_ge(disorder, 1)
                        pe.matmul(psum[:, 0, 0:1], ones[:, :], worst, start=True, stop=True).then_inc(judged, 1)

            place.at = kept
            stage = place([RING, 2], bf16)
            hot_lo = place([RING, P], bf16)
            hot_hi = place([RING, NB], bf16)
            ends = place([NB])
            hist, total, within = psum[:, 0, 0:NB], psum[:, 1, 0:NB], psum[:, 2, 0:NB]

            with stage_of() as block:
                staged, hot, counted, summed = sem("staged"), sem("hot"), sem("counted"), sem("summed")

                @block.scalar
                def _(act):
                    def body(k):
                        for b in range(2):
                            wait(act, hot, 2 * k + b - 1)
                            act.copy(stage[:, b * U:b * U + U, :], cols[:, bass.ds(k * RING + b * U, U), 2:4]).then_inc(staged, 1)
                    turns(act, C // RING, body)

                @block.vector
                def _(dve):
                    def body(k):
                        for b in range(2):
                            dve.wait_ge(staged, 2 * k + b + 1)
                            wait(dve, counted, (2 * k + b - 1) * U)
                            half = slice(b * U, b * U + U)
                            dve.tensor_tensor(hot_lo[:, half, :], iota_bf3[:, :, :].to_broadcast([P, U, P]),
                                              stage[:, half, 0:1].to_broadcast([P, U, P]), ALU.is_equal)
                            dve.tensor_tensor(hot_hi[:, half, :], iota_bf3[:, :, 0:NB].to_broadcast([P, U, NB]),
                                              stage[:, half, 1:2].to_broadcast([P, U, NB]), ALU.is_equal).then_inc(hot, 1)
                    turns(dve, C // RING, body)
                    dve.wait_ge(counted, C)
                    dve.tensor_copy(counts[g][:, :], hist).then_inc(summed, 1)
                    dve.wait_ge(summed, 2)
                    dve_step.done(dve.tensor_tensor_scan(ends, ones[:, 0:NB], total, 0.0, ALU.mult, ALU.add), dve)
                    dve_step.done(dve.tensor_tensor(block_start[g][:, :], ends, total, ALU.subtract), dve)
                    dve_step.done(dve.tensor_tensor(starts[g][:, :], block_start[g][:, :], within, ALU.add), dve)

                @block.tensor
                def _(pe):
                    def body(k):
                        for b in range(2):
                            pe.wait_ge(hot, 2 * k + b + 1)
                            for u in range(b * U, b * U + U):
                                first = isinstance(k, int) and u == 0
                                pe.matmul(hist, hot_lo[:, u, :], hot_hi[:, u, :], start=first, stop=True,
                                          skip_group_check=True).then_inc(counted, 1)
                    turns(pe, C // RING, body)
                    pe.wait_ge(summed, 1)
                    pe.matmul(total, ones[:, :], counts[g][:, :], start=True, stop=True)
                    pe.matmul(within, after[:, :], counts[g][:, :], start=True, stop=True).then_inc(summed, 1)
            place.at = kept
            return q

        def fill_list(sp, q, filled):
            nrow = q.rows.shape[0]
            sp.dma_start(q.rows[0:1, :], q.fill[0:1, 0, :]).then_inc(filled, 16)
            body = q.rows[1:nrow, :].rearrange("(p c) f -> p c f", p=P)
            at, made = 0, 16
            while at < q.C:
                m = min(FILL, q.C - at)
                sp.dma_start(body[:, at:at + m, :], q.fill[:, 0:m, :]).then_inc(filled, 16)
                at, made = at + m, made + 16
            sp.wait_ge(filled, made)

        def load_cells(sp, cells_used, cells_in, paced):
            def one(n, s_, k):
                wait(sp, cells_used, n - 1)
                sp.sem_inc(paced, 1)
                of = adjacency[0:CELLS, :].rearrange("(b p c) a -> p b (c a)", b=NB, p=P)
                sp.dma_start(cells[:, s_ * NB:(s_ + 1) * NB, :].rearrange("p s d -> p (s d)"),
                             of[:, bass.ds(n, 1), 0:NB * P].rearrange("p b c -> p (b c)")).then_inc(cells_in[s_], 16)
            in_pairs(sp, NB, one)

        def one_hots(dve, hot_lo, hot_hi, stage, to, of):
            for u in range(U):
                dve.tensor_scalar(hot_lo[:, to + u, :], iota_bf[:, :], stage[:, of + u, 2:3], None, ALU.is_equal)
            return dve.tensor_tensor(hot_hi[:, to:to + U, :], iota_bf3[:, :, 0:NB].to_broadcast([P, U, NB]),
                                     stage[:, of:of + U, 3:4].to_broadcast([P, U, NB]), ALU.is_equal)

        def scatter_sorted(q, place, gate, brought_back=False, beside=False):
            g, C, rows, cols, fill = q.g, q.C, q.rows, q.cols, q.fill
            SR = 4 * U
            stage = place([SR, 4])
            stage_bf = place([SR, 2], bf16)
            hot_lo = place([RING, P], bf16)
            hot_hi = place([RING, NB], bf16)
            hot_loT = place([U, P])
            place_of = place([2, NB])
            scrap, picked = place([U, 2 * P]), place([U, NB])
            rank, looked = place([RING]), place([RING])
            skip = place([RING])
            row_u = place([SR], u32)
            heap = psum[:, 0, 0:NB]
            look = [psum[:, 1 + b, 0:U * NB].rearrange("p (u c) -> p u c", c=NB) for b in range(2)]
            key_rows = psum[:, 3:5, :].rearrange("p b c -> p (b c)")
            turned = psum[:, 5, :].bitcast(bf16).rearrange("p (u c) -> p u c", c=P)
            FOLD = 4 if beside else 1
            HALVES = 4 * FOLD
            TURNS = C // (SR * FOLD)
            assert C % (SR * FOLD) == 0
            BLOCKS = NB // TURNS if beside else 0
            if beside:
                ending = Place()
                ending.at = ARENA - 1024
                shrunk_ring = ending([2, NB // SHARES * P], bf16)
                worst = ending([BLOCKS * SHARES])
                assert NB % SHARES == 0 and BLOCKS % 2 == 0 and TURNS * BLOCKS + 1 == NB
            GAPS = 2 + U // 2

            def products_by(gap):
                return BLOCKS * NB * (gap + 1) // (HALVES * GAPS)

            with stage_of() as block:
                names = ("staged", "heap_set", "place_set", "keys_made", "hot_made", "keys_used", "hot_turned",
                         "hotT_made", "looked", "moved", "ranked", "list_done", "list_back", "filled", "paced")
                (staged, heap_set, place_set, keys_made, hot_made, keys_used, hot_turned,
                 hotT_made, looked_up, moved, ranked, list_done, list_back, filled, paced) = (sem(n) for n in names)
                scattered = [sem(f"scattered{b}") for b in range(4)]
                rank_step = Steps(sem("rank_step"))

                if beside:
                    cells_used, summed_up, sp_paced = sem("cells_used"), sem("summed_up"), sem("sp_paced")
                    cells_in = [sem(f"cells_in{i}") for i in range(2)]
                    shrunk, checked = sem("shrunk"), sem("checked")
                    shrunk_stored = [sem(f"shrunk_stored{i}") for i in range(2)]

                def shares_of(h):
                    return range(products_by(h * GAPS - 1) * SHARES // NB, products_by(h * GAPS + GAPS - 1) * SHARES // NB)

                def share(p):
                    i, part = p // SHARES % 2, p % SHARES
                    n = NB // SHARES
                    return cells[:, i * NB + part * n:i * NB + (part + 1) * n, :].rearrange("p c d -> p (c d)")

                def await_share(eng, K, p):
                    i = p // SHARES
                    eng.wait_ge(cells_in[i % 2], (K * (BLOCKS // 2) + (i // 2 + 1)) * 16)

                def shrink(act, K, p):
                    await_share(act, K, p)
                    wait(act, shrunk_stored[p % 2], (K * (BLOCKS * SHARES // 2) + p // 2) * 16)
                    act.copy(shrunk_ring[:, p % 2, :], share(p)).then_inc(shrunk, 1)

                def check(dve, K, p):
                    await_share(dve, K, p)
                    dve.tensor_reduce(worst[:, p:p + 1], share(p), AX.X, ALU.max).then_inc(checked, 1)

                def gated(eng, program):
                    with gate(eng):
                        program(eng)

                @block.sync
                def _(sp):
                    def program(sp):
                        fill_list(sp, q, filled)
                        sp.sem_inc(paced, 1)
                        if brought_back:
                            sp.wait_ge(list_done, 1)
                            sp.dma_start(cols, rows[1:rows.shape[0], :].rearrange("(p c) f -> p c f", p=P)).then_inc(list_back, 16)
                            sp.wait_ge(list_back, 16)

                    def program_beside(sp):
                        sp.sem_inc(paced, 1)

                        def load_block(n, s_):
                            of = adjacency[0:CELLS, :].rearrange("(b p c) a -> p b (c a)", b=NB, p=P)
                            sp.dma_start(cells[:, s_ * NB:(s_ + 1) * NB, :].rearrange("p s d -> p (s d)"),
                                         of[:, bass.ds(n, 1), 0:NB * P].rearrange("p b c -> p (b c)")).then_inc(cells_in[s_], 16)

                        def store_block(n, s_):
                            width = NB // SHARES * P
                            to = adjacency_bf.rearrange("b p c -> p b c")[:, bass.ds(n, 1), :].rearrange("p b c -> p (b c)")
                            for i in range(SHARES):
                                sp.wait_ge(shrunk, n * SHARES + (i + 1))
                                sp.sem_inc(sp_paced, 1)
                                slot = (s_ + i) % 2
                                sp.dma_start(to[:, i * width:(i + 1) * width], shrunk_ring[:, slot, :]).then_inc(shrunk_stored[slot], 16)

                        load_block(0, 0)
                        load_block(1, 1)

                        def body(k, last):
                            for s_ in range(2):
                                n = 2 * k + s_
                                store_block(n, s_)
                                if not (last and s_):
                                    sp.wait_ge(cells_used, n + 1)
                                    sp.sem_inc(sp_paced, 1)
                                    sp.wait_ge(checked, (n + 1) * SHARES)
                                    sp.sem_inc(sp_paced, 1)
                                    load_block(n + 2, s_)
                        turns_ahead(sp, NB // 2, body)
                        store_block(NB - 1, 0)
                        for i in range(2):
                            sp.wait_ge(shrunk_stored[i], (NB * SHARES + 1 - i) // 2 * 16)
                    gated(sp, program_beside if beside else program)

                @block.scalar
                def _(act):
                    def stage_half(k, b):
                        wait(act, scattered[b], k * (16 * U))
                        half = slice(b * U, b * U + U)
                        act.copy(stage[:, half, :], cols[:, bass.ds(k * SR + b * U, U), :])
                        act.copy(stage_bf[:, half, 0:1], cols[:, bass.ds(k * SR + b * U, U), 2:3])
                        act.mul(stage_bf[:, half, 1:2], cols[:, bass.ds(k * SR + b * U, U), 3:4], float(P)).then_inc(staged, 1)

                    def program(act):
                        act.wait_ge(heap_set, 1)
                        act.copy(place_of[:, 0, :], heap).then_inc(place_set, 1)
                        stage_half(0, 0)

                        def body(K, last):
                            for h in range(HALVES):
                                k, b = K * FOLD + h // 4, h % 4
                                act.wait_ge(hot_turned, 4 * k + b + 1)
                                act.copy(hot_loT, turned).then_inc(hotT_made, 1)
                                if b < 3:
                                    stage_half(k, b + 1)
                                elif not (last and h == HALVES - 1):
                                    stage_half(k + 1, 0)
                                for v in range(U // 2):
                                    act.wait_ge(moved, k * (SR // 2) + (b * (U // 2) + v + 1))
                                    act.copy(place_of[:, (v + 1) % 2, :], heap).then_inc(place_set, 1)
                                    for p in shares_of(h)[v:v + 1]:
                                        shrink(act, K, p)
                        turns_ahead(act, TURNS, body)
                        for p in range(SHARES if beside else 0):
                            shrink(act, TURNS, p)
                    gated(act, program)

                @block.tensor
                def _(pe):
                    def program(pe):
                        pe.matmul(heap, ident[:, :], starts[g][:, :], start=True, stop=True).then_inc(heap_set, 1)

                        def products(K):
                            for i in range(BLOCKS):
                                pe.wait_ge(cells_in[i % 2], (K * (BLOCKS // 2) + (i // 2 + 1)) * 16)
                                wait(pe, summed_up, K * BLOCKS + (i - 1))
                                for c in range(NB):
                                    last = pe.matmul(psum[:, 6 + i % 2, 0:D], cells[:, (i % 2) * NB + c, :], acc[:, c, :],
                                                     start=c == 0, stop=c == NB - 1)
                                    if c == NB - 1:
                                        last.then_inc(cells_used, 1)
                                    yield

                        def body(K):
                            more = products(K)

                            def fill_gap(gap):
                                for _ in range(products_by(gap) - products_by(gap - 1)):
                                    next(more)

                            for h in range(HALVES):
                                k, b = K * FOLD + h // 4, h % 4
                                j = 4 * k + b
                                pe.wait_ge(staged, j + 1)
                                wait(pe, keys_used, j)
                                for u in range(U):
                                    lo = stage_bf[:, b * U + u, 0:1].to_broadcast([P, P])
                                    hi = stage_bf[:, b * U + u, 1:2].to_broadcast([P, P])
                                    pe.matmul(key_rows[:, u * P:(u + 1) * P], hi, ident_bf[:, :], start=True, stop=False)
                                    last = pe.matmul(key_rows[:, u * P:(u + 1) * P], lo, ident_bf[:, :], start=False, stop=True)
                                last.then_inc(keys_made, 1)
                                fill_gap(h * GAPS)
                                pe.wait_ge(hot_made, j + 1)
                                for u in range(U):
                                    last = pe.transpose(turned[:, u, :], hot_lo[:, (b % 2) * U + u, :], ident_bf[:, :])
                                last.then_inc(hot_turned, 1)
                                fill_gap(h * GAPS + 1)
                                pe.wait_ge(hotT_made, j + 1)
                                wait(pe, ranked, j - 1)
                                for v in range(U // 2):
                                    pe.wait_ge(place_set, k * (SR // 2) + (b * (U // 2) + v + 1))
                                    for u in (2 * v, 2 * v + 1):
                                        r = (b % 2) * U + u
                                        last = pe.matmul(heap, hot_lo[:, r, :], hot_hi[:, r, :], start=False, stop=True,
                                                         skip_group_check=True)
                                    last.then_inc(moved, 1)
                                    fill_gap(h * GAPS + 2 + v)
                                    for u in (2 * v, 2 * v + 1):
                                        last = pe.matmul(look[b % 2][:, u, :], hot_loT[:, u, :], place_of[:, v % 2, :], start=True, stop=True)
                                last.then_inc(looked_up, 1)
                        turns(pe, TURNS, body)
                        if beside:
                            sum_blocks(pe, range(BLOCKS * TURNS, NB), cells_in, cells_used, summed_up)
                    gated(pe, program)

                @block.vector
                def _(dve):
                    def program(dve):
                        dve.wait_ge(staged, 1)
                        one_hots(dve, hot_lo, hot_hi, stage, 0, 0).then_inc(hot_made, 1)

                        def body(K, last):
                            for h in range(HALVES):
                                k, b = K * FOLD + h // 4, h % 4
                                j = 4 * k + b
                                half = slice((b % 2) * U, (b % 2) * U + U)
                                out_half = slice(b * U, b * U + U)
                                dve.wait_ge(keys_made, j + 1)
                                for u in range(U):
                                    r, w = b * U + u, P * (1 + u % 2)
                                    done = dve.scalar_tensor_tensor(scrap[:, u, 0:w], key_rows[:, (u - u % 2) * P:(u + 1) * P],
                                                                    stage[:, r, 1:2], before[:, 2 * P - w:2 * P],
                                                                    ALU.is_equal, ALU.mult, accum_out=rank[:, (b % 2) * U + u:(b % 2) * U + u + 1])
                                done.then_inc(keys_used, 1)
                                dve.tensor_scalar(skip[:, half], stage[:, out_half, 1:2].rearrange("p u a -> p (u a)"), float(INVALID), SKIP,
                                                  ALU.is_ge, ALU.mult)
                                if not (last and h == HALVES - 1):
                                    dve.wait_ge(staged, j + 2)
                                    one_hots(dve, hot_lo, hot_hi, stage, ((b + 1) % 2) * U, ((b + 1) % 4) * U).then_inc(hot_made, 1)
                                for p in shares_of(h):
                                    check(dve, K, p)
                                dve.wait_ge(looked_up, j + 1)
                                rank_step.done(dve.tensor_tensor(picked, look[b % 2], hot_hi[:, half, :], ALU.mult), dve)
                                rank_step.done(dve.tensor_reduce(looked[:, half], picked, AX.X, ALU.add), dve)
                                rank_step.done(dve.scalar_tensor_tensor(rank[:, half], rank[:, half], 1.0, looked[:, half], ALU.add, ALU.add), dve)
                                dve.tensor_tensor(row_u[:, out_half], rank[:, half], skip[:, half], ALU.add).then_inc(ranked, 1)
                                for i in range(products_by(h * GAPS - 1) // NB, products_by(h * GAPS + GAPS - 1) // NB):
                                    add_block(dve, K * BLOCKS + i, 6 + i % 2, cells_used, summed_up)
                            if beside:
                                dve.wait_ge(checked, (K + 1) * (BLOCKS * SHARES))
                                rank_step.done(dve.tensor_tensor(largest[:, :], largest[:, :], worst, ALU.max), dve)
                        turns_ahead(dve, TURNS, body, [rank_step], [3 * HALVES + (1 if beside else 0)])
                        for p in range(SHARES if beside else 0):
                            check(dve, TURNS, p)
                        for n in range(BLOCKS * TURNS, NB if beside else 0):
                            add_block(dve, n, 6 + n % 2, cells_used, summed_up)
                        if beside:
                            dve.wait_ge(checked, NB * SHARES)
                            rank_step.done(dve.tensor_tensor(largest[:, :], largest[:, :], worst, ALU.max), dve)
                            dve.wait_ge(summed_up, NB)
                    gated(dve, program)

                @block.gpsimd
                def _(pool):
                    def program(pool):
                        bound = pool.to_reg(rows.shape[0] - 1)
                        pool.wait_ge(paced, 1)

                        def body(K):
                            for h in range(HALVES):
                                k, b = K * FOLD + h // 4, h % 4
                                pool.wait_ge(ranked, 4 * k + b + 1)
                                pool.sem_inc(paced, 1)
                                for r in range(b * U, b * U + U):
                                    pool.indirect_dma_start(
                                        out=rows[:, :], out_offset=bass.IndirectOffsetOnAxis(ap=row_u[:, r:r + 1], axis=0),
                                        in_=stage[:, r, :], in_offset=None,
                                        bounds_check=bound, oob_is_err=False).then_inc(scattered[b], 16)
                        turns(pool, TURNS, body)
                        for b in range(4):
                            pool.wait_ge(scattered[b], 16 * U * FOLD * TURNS)
                        pool.sem_inc(list_done, 1)
                    gated(pool, program)

        def zero_cells(sp):
            for n in range(NB):
                of_block = adjacency[n << BLK:(n + 1) << BLK, :].rearrange("(p c) a -> p (c a)", p=P)
                sp.dma_start(of_block[:, 0:NB * P], zeros).then_inc(cells_zero, 16)
            sp.dma_start(adjacency[CELLS:CELLS + (1 + LANES) * P, :].rearrange("(p c) a -> p (c a)", p=P),
                         zeros[:, 0:1 + LANES]).then_inc(cells_zero, 16)
            cells_zeroed[0] = 16 * (NB + 1)

        place = Place(ARENA - NB * P)
        first = start_sort(0, src, dst, E1, C1, True, place, place([C1, 4]), after_loads=zero_cells)
        scatter_sorted(first, first.place, lambda eng: eng.If(eng.value_load(first.flag[0:1, 0:1], min_val=0, max_val=1) == 0),
                       brought_back=True)

        place = Place()
        place.at = first.place.at
        CC = -(-S1 // P)
        cols = first.cols
        src_f, key_f = place([C1]), place([C1])
        srcs = src_rows.rearrange("r e -> (r e)").rearrange("(p c) -> p c", p=P)
        keys = key_rows_dram.rearrange("r e -> (r e)").rearrange("(p c) -> p c", p=P)
        first_i, last_i = place([NB], i32), place([NB], i32)
        first_f, last_f, taken, ends, shared = (place([NB]) for _ in range(5))
        seen, seen2 = place([NB]), place([NB])
        chunk_no, blocks, rows_back, base = (place([CC]) for _ in range(4))
        most = place([1])
        row_u, block_i = place([CC], u32), place([CC], i32)
        assert place.at <= 2 * NB * D
        place.at = 2 * NB * D
        got = got_of_chunks = place([2 * CC, P])
        with stage_of() as block:
            split, listed, rooted, chunks_made, copied = (sem(n) for n in ("split", "listed", "rooted", "chunks_made", "copied"))
            fetched_rows, over, judged = sem("fetched_rows"), sem("over"), sem("judged")

            @block.tensor
            def _(pe):
                pe.wait_ge(over, 1)
                pe.matmul(psum[:, 0, 0:1], ones[:, :], most, start=True, stop=True).then_inc(judged, 1)

            @block.vector
            def _(dve):
                def do(ins):
                    dve_step.done(ins, dve)

                dve.tensor_copy(src_f, cols[:, :, 0:1].rearrange("p c a -> p (c a)"))
                dve.tensor_copy(key_f, cols[:, :, 1:2].rearrange("p c a -> p (c a)")).then_inc(split, 1)
                do(dve.tensor_scalar(dinv[:, :], counts[0][:, :], 1.0, None, ALU.add))
                dve.tensor_copy(small[:, 4, :], dinv[:, :]).then_inc(rooted, 1)
                do(dve.tensor_reduce(most, counts[0][:, :], AX.X, ALU.max))
                dve.tensor_scalar(most, most, float(DEGREE_MAX), None, ALU.is_gt).then_inc(over, 1)
                dve.wait_ge(judged, 1)
                dve.memset(largest[:, :], 0.0)
                do(dve.tensor_scalar(way[:, 0:1], psum[:, 0, 0:1], 0.0, float(BY_ROWS), ALU.is_gt, ALU.mult))
                do(dve.tensor_copy(first_i, block_start[0][:, :]))
                do(dve.tensor_scalar(first_i, first_i, 7, None, ALU.logical_shift_right))
                do(dve.tensor_copy(first_f, first_i))
                dve.memset(last_f[:, NB - 1:NB], float(E1 + P - 1))
                do(dve.tensor_scalar(last_f[:, 0:NB - 1], block_start[0][:, 1:NB], float(P - 1), None, ALU.add))
                do(dve.tensor_copy(last_i, last_f))
                do(dve.tensor_scalar(last_i, last_i, 7, None, ALU.logical_shift_right))
                do(dve.tensor_copy(last_f, last_i))
                do(dve.tensor_tensor(taken, last_f, first_f, ALU.subtract))
                do(dve.tensor_tensor_scan(ends, ones[:, 0:NB], taken, 0.0, ALU.mult, ALU.add))
                dve.memset(shared[:, NB - 1:NB], 0.0)
                do(dve.tensor_tensor(shared[:, 0:NB - 1], last_f[:, 0:NB - 1], first_f[:, 1:NB], ALU.subtract))
                do(dve.tensor_scalar(chunk_no, iota_row[:, 0:CC], float(P), iota_col[:, :], ALU.mult, ALU.add))
                for c in range(CC):
                    dve.tensor_scalar(seen, ends, chunk_no[:, c:c + 1], 0.0, ALU.is_le, ALU.add, accum_out=blocks[:, c:c + 1])
                    do(dve.scalar_tensor_tensor(seen2, ends, chunk_no[:, c:c + 1], shared, ALU.is_le, ALU.mult,
                                                accum_out=rows_back[:, c:c + 1]))
                do(dve.tensor_scalar(blocks, blocks, float(NB - 1), None, ALU.min))
                do(dve.tensor_copy(block_i, blocks))
                do(dve.tensor_tensor(rows_back, chunk_no, rows_back, ALU.subtract))
                dve.tensor_scalar(row_u, rows_back, float(C1 - 1), None, ALU.min).then_inc(chunks_made, 1)
                do(dve.tensor_scalar(base, blocks, float(P), None, ALU.mult))
                dve.wait_ge(rooted, 2)
                do(dve.reciprocal(dinv[:, :], small[:, 5, :]))
                dve.wait_ge(fetched_rows, 32 * CC)
                for c in range(CC):
                    last = dve.tensor_scalar(got[:, CC + c, :], got[:, CC + c, :], base[:, c:c + 1], None, ALU.subtract)
                do(last)

            @block.scalar
            def _(act):
                act.wait_ge(split, 1)
                act.dma_start(srcs, src_f).then_inc(listed, 16)
                act.dma_start(keys, key_f).then_inc(listed, 16)
                act.wait_ge(rooted, 1)
                act.activation(small[:, 5, :], small[:, 4, :], ACT.Sqrt).then_inc(rooted, 1)

            @block.sync
            def _(sp):
                sp.wait_ge(chunks_made, 1)
                with nc.allow_non_contiguous_dma("a few words"):
                    sp.dma_start(chunk_dram.rearrange("(c p) -> p c", p=P), block_i).then_inc(copied, 16)
                sp.wait_ge(copied, 16)

            @block.gpsimd
            def _(pool):
                pool.wait_ge(listed, 32)
                pool.wait_ge(chunks_made, 1)
                for i, table_ in enumerate((src_rows, key_rows_dram)):
                    for c in range(CC):
                        pool.indirect_dma_start(
                            out=got[:, i * CC + c, :], out_offset=None, in_=table_[:, :],
                            in_offset=bass.IndirectOffsetOnAxis(ap=row_u[:, c:c + 1], axis=0),
                            bounds_check=C1 - 1, oob_is_err=False).then_inc(fetched_rows, 16)
                pool.wait_ge(fetched_rows, 32 * CC)

        def when(eng, wanted, program):
            with eng.If(eng.value_load(way[0:1, 0:1], min_val=0, max_val=BY_ROWS) == wanted):
                program(eng)

        place = Place(2 * NB * D)
        GROUPS = -(-C1 // P)
        rows_in = place([2 * GROUPS, P])
        src_T, key_T = place([C1]), place([C1])
        code, part_a, part_b, key_i = (place([C1], i32) for _ in range(4))
        R4 = 4 * LANES
        stage = place([R4, 2])
        alike = place([LANES, P])
        alike2 = place([LANES, P])
        alike3 = place([LANES, P])
        total, earlier = place([R4]), place([R4])
        value = place([R4])
        leads = place([R4], i32)
        where, code_now = place([R4], i32), place([R4], i32)
        elsewhere = place([LANES], i32)
        with stage_of() as block:
            rows_loaded, col_made, col_used = sem("rows_loaded"), sem("col_made"), sem("col_used")
            elsewhere_set = sem("elsewhere_set")

            @block.sync
            def _(sp):
                for i, t in enumerate((src_rows, key_rows_dram)):
                    whole = C1 // P
                    sp.dma_start(rows_in[:, i * GROUPS:i * GROUPS + whole, :],
                                 t[0:whole * P, :].rearrange("(g p) e -> p g e", p=P)).then_inc(rows_loaded, 16)
                    if C1 % P:
                        sp.dma_start(rows_in[0:C1 % P, i * GROUPS + whole, :], t[whole * P:C1, :]).then_inc(rows_loaded, 16)

            @block.gpsimd
            def _(pool):
                pool.iota(elsewhere, pattern=[[P, LANES]], base=CELLS + P, channel_multiplier=1).then_inc(elsewhere_set, 1)
                pool.wait_ge(elsewhere_set, 1)

            @block.tensor
            def _(pe):
                pe.wait_ge(rows_loaded, 32 * (1 + (C1 % P > 0)))
                for n in range(2 * GROUPS):
                    m = min(P, C1 - (n % GROUPS) * P)
                    wait(pe, col_used, n - 7)
                    pe.transpose(psum[:, n % 8, 0:m], rows_in[0:m, n, :], ident[0:m, 0:m]).then_inc(col_made, 1)

            @block.vector
            def _(dve):
                def do(ins):
                    dve_step.done(ins, dve)

                for n in range(2 * GROUPS):
                    c = n % GROUPS
                    m = min(P, C1 - c * P)
                    dve.wait_ge(col_made, n + 1)
                    dve.tensor_copy((src_T, key_T)[n // GROUPS][:, c * P:c * P + m], psum[:, n % 8, 0:m]).then_inc(col_used, 1)
                dve.wait_ge(col_used, 2 * GROUPS)
                do(dve.tensor_copy(code, src_T))
                do(dve.tensor_scalar(key_i, key_T, float(NP), None, ALU.min))
                do(dve.tensor_scalar(part_a, code, P - 1, BLK - LO, ALU.bitwise_and, ALU.logical_shift_left))
                do(dve.tensor_scalar(part_b, code, LO, LO, ALU.logical_shift_right, ALU.logical_shift_left))
                do(dve.tensor_tensor(code, part_a, part_b, ALU.bitwise_or))
                do(dve.tensor_scalar(part_a, key_i, P - 1, None, ALU.bitwise_and))
                do(dve.tensor_scalar(part_b, key_i, LO, BLK, ALU.logical_shift_right, ALU.logical_shift_left))
                do(dve.tensor_tensor(code, code, part_a, ALU.bitwise_or))
                do(dve.tensor_tensor(code, code, part_b, ALU.bitwise_or))

        src_L, key_L, code_L = (t.rearrange("p (l r) -> p l r", r=LANE_ROWS) for t in (src_T, key_T, code))
        TURNS_A = LANE_ROWS // 4
        assert LANE_ROWS % 4 == 0
        with stage_of() as block:
            staged, rows_made, rows_used, ranked, passed, paced = (
                sem(n) for n in ("staged", "rows_made", "rows_used", "ranked", "passed", "paced"))
            lane = [sem(f"lane{u}") for u in range(LANES)]
            step = Steps(sem("step"))

            @block.scalar
            def _(act):
                def program(act):
                    def body(k):
                        for b in range(4):
                            j = 4 * k + b
                            wait(act, ranked, j - 3)
                            cut = slice(b * LANES, (b + 1) * LANES)
                            act.copy(stage[:, cut, 0:1], src_L[:, :, bass.ds(j, 1)])
                            act.copy(stage[:, cut, 1:2], key_L[:, :, bass.ds(j, 1)]).then_inc(staged, 1)
                    turns(act, TURNS_A, body)
                when(act, BY_BF16, program)

            @block.tensor
            def _(pe):
                def program(pe):
                    def body(k):
                        for b in range(4):
                            j = 4 * k + b
                            pe.wait_ge(staged, j + 1)
                            wait(pe, rows_used, j - 1)
                            for u in range(LANES):
                                for i in range(2):
                                    at = (u % 2 * 2 + i) * P
                                    last = pe.matmul(psum[:, (b % 2) * 4 + u // 2, at:at + P],
                                                     stage[:, b * LANES + u, i:i + 1].to_broadcast([P, P]), ident[:, :],
                                                     start=True, stop=True)
                            last.then_inc(rows_made, 1)
                    turns(pe, TURNS_A, body)
                when(pe, BY_BF16, program)

            @block.vector
            def _(dve):
                def program(dve):
                    def body(k):
                        for b in range(4):
                            j = 4 * k + b
                            cut = slice(b * LANES, (b + 1) * LANES)
                            dve.wait_ge(rows_made, j + 1)
                            for u in range(LANES):
                                at = (u % 2 * 2) * P
                                last = dve.tensor_scalar(alike[:, u, :], psum[:, (b % 2) * 4 + u // 2, at:at + P],
                                                         stage[:, b * LANES + u, 0:1], None, ALU.is_equal)
                            step.done(last, dve)
                            for u in range(LANES):
                                at = (u % 2 * 2 + 1) * P
                                last = dve.scalar_tensor_tensor(alike2[:, u, :], psum[:, (b % 2) * 4 + u // 2, at:at + P],
                                                                stage[:, b * LANES + u, 1:2], alike[:, u, :],
                                                                ALU.is_equal, ALU.mult,
                                                                accum_out=total[:, b * LANES + u:b * LANES + u + 1])
                            last.then_inc(rows_used, 1)
                            dve.wait_ge(rows_used, j + 1)
                            for u in range(LANES):
                                last = dve.scalar_tensor_tensor(alike3[:, u, :], alike2[:, u, :], 1.0, before[:, P:2 * P],
                                                                ALU.mult, ALU.mult,
                                                                accum_out=earlier[:, b * LANES + u:b * LANES + u + 1])
                            step.done(last, dve)
                            wait(dve, passed, j - 2)
                            dve.tensor_scalar(where[:, cut], elsewhere, 0, None, ALU.bitwise_or)
                            dve.tensor_scalar(code_now[:, cut], code_L[:, :, bass.ds(j, 1)].rearrange("p l a -> p (l a)"), 0, None,
                                              ALU.bitwise_or)
                            step.done(dve.tensor_scalar(leads[:, cut], earlier[:, cut], 0.0, None, ALU.is_equal), dve)
                            dve.scalar_tensor_tensor(value[:, cut], earlier[:, cut], 0.0, total[:, cut], ALU.is_equal, ALU.mult)
                            dve.copy_predicated(where[:, cut], leads[:, cut], code_now[:, cut]).then_inc(ranked, 1)
                    turns(dve, TURNS_A, body, [step], [12])
                when(dve, BY_BF16, program)

            @block.gpsimd
            def _(pool):
                def program(pool):
                    pool.wait_ge(cells_zero, cells_zeroed[0])
                    bound = pool.to_reg(CELLS + (1 + LANES) * P - 1)

                    def body(k):
                        for b in range(4):
                            j = 4 * k + b
                            pool.wait_ge(ranked, j + 1)
                            for part in range(2):
                                group = range(part * LANES // 2, (part + 1) * LANES // 2)
                                for u in group:
                                    wait(pool, lane[u], j * 16)
                                pool.sem_inc(paced, 1)
                                for u in group:
                                    r = b * LANES + u
                                    pool.indirect_dma_start(
                                        out=adjacency[:, :],
                                        out_offset=bass.IndirectOffsetOnAxis(ap=where[:, r:r + 1].bitcast(u32), axis=0),
                                        in_=value[:, r:r + 1], in_offset=None, bounds_check=bound, oob_is_err=True,
                                        compute_op=ALU.add).then_inc(lane[u], 16)
                            pool.sem_inc(passed, 1)
                    turns(pool, TURNS_A, body)
                    for u in range(LANES):
                        pool.wait_ge(lane[u], 16 * LANE_ROWS)
                when(pool, BY_BF16, program)

        place = Place()
        x_sb = place([NB, D])
        acc = place([NB, D])
        cells = place([2 * NB, P])
        W_sb = place([KD, D])
        bias = place([D])
        src_u_at = place.at
        src_u = place([S1], u32)
        dst_lo = place([S1])
        chunk_row = place([S1], i32)
        SO = 7
        second_cols = ARENA - 1024 - 4 * C2
        assert place.at <= second_cols
        place.at = ARENA - 1024
        stats = place([NB, 6])
        mv = place([NB, 2])
        rstd = place([NB])
        flat = cells.rearrange("p r d -> p (r d)")
        fetched = flat[:, 0:RING * D].rearrange("p (r d) -> p r d", d=D)
        hot = flat[:, RING * D:RING * (D + P)].rearrange("p (r d) -> p r d", d=P)
        idx = flat[:, RING * (D + P):RING * (D + P) + RING].bitcast(u32)
        lo_stage = flat[:, RING * (D + P) + RING:RING * (D + P) + 2 * RING]
        o_ring = flat[:, 0:SO * D].rearrange("p (u d) -> p u d", d=D)
        oT_ring = flat[:, SO * D:2 * SO * D].rearrange("p (u k c) -> p u k c", k=KD, c=P)
        got = got_of_chunks
        table_v = table.rearrange("(b p) f -> p b f", p=P)
        psum_T = psum[:, 0:4, 0:D].rearrange("p b (k c) -> p b k c", k=KD)
        psum_M = psum[:, 4:8, 0:D]

        def in_pairs(eng, count, one, steps=(), per=()):
            def body(k):
                for s_ in range(2):
                    one(2 * k + s_, s_, k)
            turns(eng, count // 2, body, steps, per)
            if count % 2:
                one(count - 1, 0, count // 2)

        def norm_stats(tag, before_it=None):
            with stage_of() as block:
                var_ready, root_ready = sem(f"var_ready{tag}"), sem(f"root_ready{tag}")

                @block.vector
                def _(dve):
                    if before_it:
                        before_it(dve)
                    for n in range(NB):
                        last = dve.bn_stats(stats[:, n, :], x_sb[:, n, :])
                    dve_step.done(last, dve)
                    for n in range(NB):
                        last = dve.bn_aggr(mv[:, n, :], stats[:, n, :])
                    dve_step.done(last, dve)
                    dve.tensor_scalar(rstd, mv[:, :, 1:2].rearrange("p n a -> p (n a)"), EPS, None, ALU.add).then_inc(var_ready, 1)
                    dve.wait_ge(root_ready, 1)
                    dve_step.done(dve.reciprocal(rstd, rstd), dve)

                @block.scalar
                def _(act):
                    act.wait_ge(var_ready, 1)
                    act.activation(rstd, rstd, ACT.Sqrt).then_inc(root_ready, 1)

        def project(tag, rows_of_block, width, finish, transposed_too=None, weights=None):
            with stage_of() as block:
                rows_ready, turned, T_ready, multiplied, ended, left, sent = (
                    sem(f"{n}{tag}") for n in ("rows_ready", "turned", "T_ready", "multiplied", "ended", "left", "sent"))
                t_out = sem(f"t_out{tag}")

                @block.vector
                def _(dve):
                    def body(k):
                        for u in range(SO):
                            wait(dve, turned, k * SO + (u + 1 - SO))
                            rows_of_block(dve, k * SO + u, o_ring[:, u, :]).then_inc(rows_ready, 1)
                    turns(dve, G7, body)

                @block.tensor
                def _(pe):
                    pe.wait_ge(loads, loaded[0])

                    def body(k):
                        for u in range(SO):
                            pe.wait_ge(rows_ready, k * SO + (u + 1))
                            wait(pe, T_ready, k * SO + max(u - 3, 0))
                            for c in range(KD):
                                last = pe.transpose(psum_T[:, u % 4, c, :], o_ring[:, u, c * P:(c + 1) * P], ident[:, :])
                            last.then_inc(turned, 1)
                        for u in range(SO):
                            pe.wait_ge(T_ready, k * SO + (u + 1))
                            wait(pe, ended, k * SO + max(u - 3, 0))
                            for c in range(KD):
                                last = pe.matmul(psum_M[:, u % 4, 0:width], oT_ring[:, u, c, :], weights[:, c, 0:width],
                                                 start=c == 0, stop=c == KD - 1)
                            last.then_inc(multiplied, 1)
                    turns(pe, G7, body)

                @block.scalar
                def _(act):
                    def body(k):
                        for u in range(SO):
                            act.wait_ge(turned, k * SO + (u + 1))
                            wait(act, multiplied, k * SO + (u + 1 - SO))
                            if transposed_too is not None:
                                wait(act, t_out, k * 16)
                            act.copy(oT_ring[:, u, :, :], psum_T[:, u % 4, :, :]).then_inc(T_ready, 1)
                        for u in range(SO):
                            act.wait_ge(multiplied, k * SO + (u + 1))
                            finish(act, k * SO + u, psum_M[:, u % 4, 0:width]).then_inc(ended, 1)
                    turns(act, G7, body)

                @block.sync
                def _(sp):
                    paced = sem(f"paced{tag}")

                    def body(k):
                        if transposed_too is None:
                            sp.wait_ge(ended, k * SO + SO)
                            sp.sem_inc(paced, 1)
                            sp.dma_start(table_v[:, bass.ds(k * SO, SO), :], acc[:, bass.ds(k * SO, SO), :]).then_inc(left, 16)
                        else:
                            sp.wait_ge(T_ready, k * SO + SO)
                            sp.sem_inc(paced, 1)
                            view = transposed_too[:, :, bass.ds(k * (SO * P), SO * P)]
                            for c in range(KD):
                                sp.dma_start(view[:, c, :].rearrange("p (u n) -> p u n", n=P), oT_ring[:, :, c, :]).then_inc(
                                    t_out if c == KD - 1 else left, 16)
                            sp.wait_ge(left, 16 * (k + 1))
                            sp.wait_ge(t_out, 16 * (k + 1))
                            sp.sem_inc(paced, 1)
                    turns(sp, G7, body)
                    sp.wait_ge(left, 16 * G7)

        with stage_of() as block:
            zeroed, col_made, col_used = sem("zeroed"), sem("col_made"), sem("col_used")

            @block.sync
            def _(sp):
                load(sp, chunk_row[0:1, :], chunk_dram[0:S1].rearrange("(a c) -> a c", a=1))
                sp.wait_ge(zeroed, 1)
                nf = N // P
                load(sp, x_sb[:, 0:nf, :], x[0:nf * P, :].rearrange("(b p) f -> p b f", p=P))
                load(sp, x_sb[0:N - nf * P, nf, :], x[nf * P:N, :])

            want = loaded[0]

            @block.tensor
            def _(pe):
                for n in range(2 * CC):
                    wait(pe, col_used, n - 7)
                    pe.transpose(psum[:, n % 8, 0:P], got[:, n, :], ident[:, :]).then_inc(col_made, 1)

            @block.vector
            def _(dve):
                dve.memset(x_sb[:, NB - 1, :], 0.0).then_inc(zeroed, 1)
                for n in range(2 * CC):
                    c = n % CC
                    m = min(P, S1 - c * P)
                    dve.wait_ge(col_made, n + 1)
                    to = (src_u, dst_lo)[n // CC]
                    dve.tensor_copy(to[:, c * P:c * P + m], psum[:, n % 8, 0:m]).then_inc(col_used, 1)
                dve.wait_ge(loads, want)

        norm_stats("a")

        def normed(dve, n, to):
            return dve.tensor_scalar(to, x_sb[:, bass.ds(n, 1), :].rearrange("p a f -> p (a f)"),
                                     mv[:, bass.ds(n, 1), 0:1].rearrange("p a f -> p (a f)"), rstd[:, bass.ds(n, 1)],
                                     ALU.subtract, ALU.mult)

        def conv_out(dve, n, to):
            return dve.scalar_tensor_tensor(to, x_sb[:, bass.ds(n, 1), :].rearrange("p a f -> p (a f)"),
                                            dinv[:, bass.ds(n, 1)], bias, ALU.mult, ALU.add)

        def scaled(act, n, got):
            return act.activation(acc[:, bass.ds(n, 1), :].rearrange("p a f -> p (a f)"), got, ACT.Copy,
                                  scale=dinv[:, bass.ds(n, 1)])

        def load_layer(layer):
            with stage_of() as block:
                @block.sync
                def _(sp):
                    load(sp, W_sb, gW[layer].rearrange("(k p) n -> p k n", p=P))
                    if layer:
                        load(sp, bias, gb[layer - 1].partition_broadcast(P))
                    sp.wait_ge(loads, loaded[0])

        def add_neighbours(layer):
            with stage_of() as block:
                names = ("idx_ready", "lo_ready", "hot_ready", "multiplied", "added")
                idx_ready, lo_ready, hot_ready, multiplied, added = (sem(f"c{layer}_{n}") for n in names)
                copied_acc = sem("copied_acc")
                arrived = [sem(f"c{layer}_arrived{b}") for b in range(2)]
                slots = psum[:, :, 0:D]
                TURNS = S1 // RING

                @block.scalar
                def _(act):
                    def program(act):
                        def body(k):
                            for b in range(2):
                                half = slice(b * U, b * U + U)
                                wait(act, arrived[b], k * (16 * U))
                                act.copy(idx[:, half], src_u[:, bass.ds(k * RING + b * U, U)]).then_inc(idx_ready, 1)
                                wait(act, hot_ready, (2 * k + b - 1) * U)
                                act.copy(lo_stage[:, half], dst_lo[:, bass.ds(k * RING + b * U, U)]).then_inc(lo_ready, 1)
                        turns(act, TURNS, body)
                    when(act, BY_ROWS, program)

                @block.gpsimd
                def _(pool):
                    def program(pool):
                        paced = sem("paced")
                        bound = pool.to_reg(NP - 1)

                        def body(k):
                            for b in range(2):
                                pool.wait_ge(idx_ready, 2 * k + b + 1)
                                wait(pool, multiplied, (2 * k + b - 1) * U)
                                pool.sem_inc(paced, 1)
                                for r in range(b * U, b * U + U):
                                    pool.indirect_dma_start(
                                        out=fetched[:, r, :], out_offset=None, in_=table[:, :],
                                        in_offset=bass.IndirectOffsetOnAxis(ap=idx[:, r:r + 1], axis=0),
                                        bounds_check=bound, oob_is_err=False).then_inc(arrived[b], 16)
                        turns(pool, TURNS, body)
                    when(pool, BY_ROWS, program)

                @block.vector
                def _(dve):
                    def program(dve):
                        dve.tensor_copy(x_sb, acc).then_inc(copied_acc, 1)
                        dve.wait_ge(copied_acc, 1)
                        reg = [dve.alloc_register(f"blk{layer}_{u}") for u in range(U)]

                        def body(k):
                            for b in range(2):
                                dve.wait_ge(lo_ready, 2 * k + b + 1)
                                wait(dve, multiplied, (2 * k + b - 1) * U)
                                for r in range(b * U, b * U + U):
                                    dve.tensor_scalar(hot[:, r, :], iota_row[:, :], lo_stage[:, r:r + 1], None, ALU.is_equal).then_inc(hot_ready, 1)
                                dve.load(reg, chunk_row[0:1, bass.ds(k * RING + b * U, U)])
                                for u in range(U):
                                    n = k * RING + (b * U + u)
                                    where = bass.ds(dve.snap(reg[u], min_val=0, max_val=NB - 1), 1)
                                    to = x_sb[:, where, :].rearrange("p a f -> p (a f)")
                                    dve.wait_ge(multiplied, n + 1)
                                    wait(dve, added, n)
                                    dve.tensor_tensor(to, to, slots[:, u, :], ALU.add).then_inc(added, 1)
                        turns(dve, TURNS, body)
                        dve.wait_ge(added, S1)
                    when(dve, BY_ROWS, program)

                @block.tensor
                def _(pe):
                    def program(pe):
                        def body(k):
                            for b in range(2):
                                pe.wait_ge(arrived[b], (k + 1) * (16 * U))
                                for u in range(U):
                                    n = k * RING + (b * U + u)
                                    pe.wait_ge(hot_ready, n + 1)
                                    wait(pe, added, n - U + 1)
                                    pe.matmul(slots[:, u, :], hot[:, b * U + u, :], fetched[:, b * U + u, :], start=True, stop=True).then_inc(multiplied, 1)
                        turns(pe, TURNS, body)
                    when(pe, BY_ROWS, program)
        def sum_blocks(pe, blocks, cells_in, cells_used, summed_up):
            for n in blocks:
                products_of(pe, n, n % 2, n // 2, 6, cells_in, cells_used, summed_up)

        def products_of(pe, n, s_, k, bank, cells_in, cells_used, summed_up):
            pe.wait_ge(cells_in[s_], (k + 1) * 16)
            wait(pe, summed_up, n - 1)
            for c in range(NB):
                last = pe.matmul(psum[:, bank + s_, 0:D], cells[:, s_ * NB + c, :], acc[:, c, :], start=c == 0, stop=c == NB - 1)
            last.then_inc(cells_used, 1)

        def add_block(dve, n, bank, cells_used, summed_up):
            dve.wait_ge(cells_used, n + 1)
            at = bass.ds(n, 1)
            dve.tensor_tensor(x_sb[:, at, :].rearrange("p a f -> p (a f)"), acc[:, at, :].rearrange("p a f -> p (a f)"),
                              psum[:, bank, 0:D], ALU.add).then_inc(summed_up, 1)

        def add_by_matrix():
            with stage_of() as block:
                cells_used, summed_up, paced = sem("cells_used"), sem("summed_up"), sem("paced")
                cells_in = [sem(f"cells_in{i}") for i in range(2)]

                @block.sync
                def _(sp):
                    when(sp, BY_FLOAT, lambda sp: load_cells(sp, cells_used, cells_in, paced))

                @block.tensor
                def _(pe):
                    def program(pe):
                        in_pairs(pe, NB, lambda n, s_, k: products_of(pe, n, s_, k, 0, cells_in, cells_used, summed_up))
                    when(pe, BY_FLOAT, program)

                @block.vector
                def _(dve):
                    def program(dve):
                        in_pairs(dve, NB, lambda n, s_, k: add_block(dve, n, s_, cells_used, summed_up))
                        dve.wait_ge(summed_up, NB)
                    when(dve, BY_FLOAT, program)

        parts = [arena[:, at:at + NB * D // 2].bitcast(bf16).rearrange("p (n d) -> p n d", d=D)
                 for at in (0, NB * D // 2, 2 * NB * D)]
        cells_bf = arena[:, 2 * NB * D + NB * D // 2:3 * NB * D].bitcast(bf16).rearrange("p (c d) -> p c d", d=P)

        def add_by_bf16_matrix():
            GB = NB // 7
            place = Place(second_cols)
            place.at = src_u_at
            rest = [place([GB, D]) for _ in range(2)]
            with stage_of() as block:
                cells_used, summed_up, paced = sem("cells_used"), sem("summed_up"), sem("paced")
                cells_in = [sem(f"cells_in{i}") for i in range(2)]
                first_made, rest_made, second_made, third_made, back = (
                    sem(n) for n in ("first_made", "rest_made", "second_made", "third_made", "back"))

                def group(t, g):
                    return t[:, g * GB:(g + 1) * GB, :]

                @block.sync
                def _(sp):
                    def program(sp):
                        def one(n, s_, k):
                            wait(sp, cells_used, n - 1)
                            sp.sem_inc(paced, 1)
                            sp.dma_start(cells_bf[:, s_ * NB:(s_ + 1) * NB, :].rearrange("p c d -> p (c d)"),
                                         adjacency_bf.rearrange("b p c -> p b c")[:, bass.ds(n, 1), :].rearrange("p b c -> p (b c)")
                                         ).then_inc(cells_in[s_], 16)
                        in_pairs(sp, NB, one)
                    when(sp, BY_BF16, program)

                @block.scalar
                def _(act):
                    def program(act):
                        for g in range(7):
                            act.copy(group(parts[0], g), group(acc, g)).then_inc(first_made, 1)
                        for g in range(7):
                            act.wait_ge(rest_made, g + 1)
                            act.copy(group(parts[1], g), rest[g % 2]).then_inc(second_made, 1)
                        act.wait_ge(summed_up, NB)
                        act.copy(x_sb[:, NB // 2:NB, :], acc[:, NB // 2:NB, :]).then_inc(back, 1)
                        act.wait_ge(back, 2)
                    when(act, BY_BF16, program)

                @block.vector
                def _(dve):
                    def program(dve):
                        def make_rest(g):
                            dve.wait_ge(first_made, g + 1)
                            dve.tensor_tensor(rest[g % 2], group(acc, g), group(parts[0], g), ALU.subtract).then_inc(rest_made, 1)

                        make_rest(0)
                        for g in range(7):
                            if g < 6:
                                wait(dve, third_made, g)
                                make_rest(g + 1)
                            dve.wait_ge(second_made, g + 1)
                            dve.tensor_tensor(group(parts[2], g), rest[g % 2], group(parts[1], g), ALU.subtract).then_inc(third_made, 1)

                        def one(n, s_, k):
                            dve.wait_ge(cells_used, n + 1)
                            to = acc[:, bass.ds(n, 1), :].rearrange("p a f -> p (a f)")
                            dve.tensor_tensor(to, to, psum[:, s_, 0:D], ALU.add).then_inc(summed_up, 1)
                        in_pairs(dve, NB, one)
                        dve.wait_ge(summed_up, NB)
                        dve.tensor_copy(x_sb[:, 0:NB // 2, :], acc[:, 0:NB // 2, :]).then_inc(back, 1)
                        dve.wait_ge(back, 2)
                    when(dve, BY_BF16, program)

                @block.tensor
                def _(pe):
                    def program(pe):
                        def one(n, s_, k):
                            pe.wait_ge(cells_in[s_], (k + 1) * 16)
                            wait(pe, summed_up, n - 1)
                            for c in range(NB):
                                if isinstance(n, int) and n == 0 and c % GB == 0:
                                    pe.wait_ge(third_made, c // GB + 1)
                                for i, part in enumerate(parts):
                                    last = pe.matmul(psum[:, s_, 0:D], cells_bf[:, s_ * NB + c, :], part[:, c, :],
                                                     start=c == 0 and i == 0, stop=c == NB - 1 and i == 2)
                            last.then_inc(cells_used, 1)
                        in_pairs(pe, NB, one)
                    when(pe, BY_BF16, program)

        def choose_way():
            place = Place()
            place.at = ARENA - 1024
            most, too_many = place([1]), place([1])
            with stage_of() as block:
                over, judged = sem("over"), sem("judged")

                @block.tensor
                def _(pe):
                    pe.wait_ge(over, 1)
                    pe.matmul(psum[:, 0, 0:1], ones[:, :], too_many, start=True, stop=True).then_inc(judged, 1)

                @block.vector
                def _(dve):
                    dve_step.done(dve.tensor_reduce(most, largest[:, :], AX.X, ALU.max), dve)
                    dve.tensor_scalar(too_many, most, float(COUNT_MAX), None, ALU.is_gt).then_inc(over, 1)
                    dve.wait_ge(judged, 1)
                    dve_step.done(dve.tensor_scalar(most, psum[:, 0, 0:1], 0.0, float(BY_FLOAT), ALU.is_gt, ALU.mult), dve)
                    dve_step.done(dve.tensor_tensor(way[:, 0:1], way[:, 0:1], most, ALU.add), dve)

        place = Place(3 * NB * D)
        place.at = 2 * NB * D
        at_end = Place()
        at_end.at = second_cols
        second = start_sort(1, edges[0], edges[1], E2, C2, False, place, at_end([C2, 4]))
        with stage_of() as block:
            filled = sem("filled")

            @block.sync
            def _(sp):
                fill_list(sp, second, filled)

        def rank_place():
            place = Place(second_cols)
            place.at = src_u_at
            return place

        def where_way(wanted):
            return lambda eng: eng.If(eng.value_load(way[0:1, 0:1], min_val=0, max_val=BY_ROWS) == wanted)

        for layer in range(3):
            load_layer(layer)
            project(f"_l{layer}", conv_out if layer else normed, D, scaled, weights=W_sb)
            add_neighbours(layer)
            if layer == 0:
                scatter_sorted(second, rank_place(), where_way(BY_BF16), beside=True)
                choose_way()
            else:
                add_by_matrix()
                add_by_bf16_matrix()
        scatter_sorted(second, rank_place(), where_way(BY_ROWS))

        place = Place()
        place.at = src_u_at
        Wg = place([KD, HE])
        att = place([2, HE])
        last_bias = place([D])
        with stage_of() as block:
            stored = sem("x1_stored")
            x1_ready = sem("x1_ready")

            @block.sync
            def _(sp):
                nf = N // P
                load(sp, acc[:, 0:nf, :], x[0:nf * P, :].rearrange("(b p) f -> p b f", p=P))
                load(sp, acc[0:N - nf * P, nf, :], x[nf * P:N, :])
                load(sp, last_bias, gb[2].partition_broadcast(P))
                load(sp, Wg, W_gat.rearrange("(k p) n -> p k n", p=P))
                load(sp, att[:, 0, :], att_src.rearrange("h e -> (h e)").partition_broadcast(P))
                load(sp, att[:, 1, :], att_dst.rearrange("h e -> (h e)").partition_broadcast(P))
                sp.wait_ge(x1_ready, 1)
                sp.dma_start(x1_dram.rearrange("(b p) f -> p b f", p=P), x_sb).then_inc(stored, 16)
                sp.wait_ge(stored, 16)
                sp.wait_ge(loads, loaded[0])

            want = loaded[0]

            @block.vector
            def _(dve):
                dve.wait_ge(loads, want)
                for n in range(NB):
                    last = dve.scalar_tensor_tensor(x_sb[:, n, :], x_sb[:, n, :], dinv[:, n:n + 1], last_bias, ALU.mult, ALU.add)
                dve_step.done(last, dve)
                dve.tensor_tensor(x_sb, x_sb, acc, ALU.add).then_inc(x1_ready, 1)
                dve.wait_ge(x1_ready, 1)

        norm_stats("b")

        def features(act, n, got):
            return act.copy(node_feat[:, bass.ds(n, 1), 0:HE].rearrange("p a f -> p (a f)"), got)

        project("_gat", normed, HE, features, transposed_too=xT_dram, weights=Wg)

        place = Place()
        packed = place([NB, TW])
        prod = place([NB, HE])
        with stage_of() as block:
            stored, packed_ready = sem("table2_stored"), sem("packed_ready")

            @block.vector
            def _(dve):
                dve_step.done(dve.memset(packed, 0.0), dve)
                for s in range(2):
                    dve_step.done(dve.tensor_tensor(prod, node_feat[:, :, 0:HE],
                                                    att[:, s:s + 1, :].to_broadcast([P, NB, HE]), ALU.mult), dve)
                    dve_step.done(dve.tensor_reduce(node_feat[:, :, HE + H * s:HE + H * s + H],
                                                    prod.rearrange("p n (h e) -> p n h e", h=H), AX.X, ALU.add), dve)
                dve.tensor_copy(packed[:, :, 0:24], node_feat[:, :, :]).then_inc(packed_ready, 1)

            @block.sync
            def _(sp):
                sp.wait_ge(packed_ready, 1)
                sp.dma_start(table2.rearrange("(b p) f -> p b f", p=P), packed).then_inc(stored, 16)
                sp.wait_ge(stored, 16)

        place = Place()
        EW = HE + H
        edge = place([S2, EW])
        same = place([S2])
        apart = place([S2])
        idx2_all = place([S2 + RING], u32)
        fetched2 = place([RING, TW])
        idx2 = place([RING], u32)
        node_max = place([NB, H])
        node_pay = place([NB, 2 * H])
        node_sum = place([NB, EW])
        first_row, last_row = place([NB], u32), place([NB], u32)
        node_tmp = place([NB, H])
        node_tmp2 = place([NB, H])
        node_big = place([NB, HE])
        carry_rows = place([4, P])
        end_cols = place([2, 24])
        nt1, nt2 = place([NB]), place([NB])
        vecs = place([3, HE])
        all_same = place([1])
        shared_from = place.at
        far = place([S2, 2 * H])
        score = place([S2, H])
        maxed = place([S2, H])

        with stage_of() as block:
            rec_in, rec_used, vec_in = sem("rec2_in"), sem("rec2_used"), sem("vec_in")
            spread0 = sem("spread_zeroed")
            rv = sorted2[1:P * S2 + 1, :].rearrange("(p c) f -> p c f", c=S2)
            rprev = sorted2[0:P * S2, :].rearrange("(p c) f -> p c f", c=S2)
            recv = far.rearrange("p c f -> p (c f)")[:, 0:S2 * 4].rearrange("p (c f) -> p c f", f=4)

            @block.sync
            def _(sp):
                sp.dma_start(recv, rv).then_inc(rec_in, 16)
                sp.wait_ge(rec_used, 1)
                sp.dma_start(recv, rprev).then_inc(rec_in, 16)
                for i, v in enumerate((b_gat, ln_g, ln_b)):
                    sp.dma_start(vecs[:, i, :], v.partition_broadcast(P)).then_inc(vec_in, 16)
                sp.wait_ge(vec_in, 48)
                sp.wait_ge(rec_used, 2)
                sp.dma_start(spread.rearrange("(p c) f -> p c f", c=S2), far).then_inc(spread0, 16)
                sp.wait_ge(spread0, 16)

            @block.vector
            def _(dve):
                dve.memset(node_max, -BIG)
                dve.memset(node_sum, 0.0)
                dve.wait_ge(rec_in, 16)
                dve.memset(idx2_all[:, S2:S2 + RING], 0)
                dve.tensor_copy(idx2_all[:, 0:S2], recv[:, :, 0:1].rearrange("p c a -> p (c a)"))
                dve.tensor_copy(same, recv[:, :, 1:2].rearrange("p c a -> p (c a)")).then_inc(rec_used, 1)
                dve.wait_ge(rec_in, 32)
                dve_step.done(dve.tensor_tensor(same, same, recv[:, :, 1:2].rearrange("p c a -> p (c a)"), ALU.is_equal), dve)
                dve.memset(far, 0.0).then_inc(rec_used, 1)
                dve_step.done(dve.tensor_scalar(apart, same, 1.0, BIG, ALU.subtract, ALU.mult), dve)
                dve_step.done(dve.tensor_reduce(all_same, same, AX.X, ALU.min), dve)
                dve_step.done(dve.tensor_scalar(nt1, counts[1][:, :], 0.0, SKIP, ALU.is_equal, ALU.mult), dve)
                dve_step.done(dve.tensor_tensor(nt2, nt1, starts[1][:, :], ALU.add), dve)
                dve.tensor_copy(first_row, nt2)
                dve_step.done(dve.tensor_tensor(nt1, nt2, counts[1][:, :], ALU.add), dve)
                dve_step.done(dve.tensor_scalar(last_row, nt1, 1.0, None, ALU.subtract), dve)

        mlp = Place()
        mlp.at = shared_from
        GN = SO * P
        HN = GN // 2
        HT, YT = 2 * FC, SO
        PAIRS = G7 // 2
        assert G7 % 2 == 1
        W1_sb = mlp([NE * KD, F])
        W2_sb = mlp([NE * FC, D])
        b1_sb = mlp([NE, FC])
        b2_sb = mlp([NE, D])
        xT = mlp([2 * KD, GN])
        hh = mlp([2 * FC, GN])
        y_ring = mlp([YT, D])
        psum_H = psum[:, 0:4, 0:HN]
        psum_Y = psum[:, 4:8, 0:D]

        def groups(eng, one, steps=(), per=()):
            def body(k):
                for s in range(2):
                    one(2 * k + s, s, k)
            turns(eng, PAIRS, body, steps, per)
            one(G7 - 1, 0, PAIRS)

        with stage_of() as block:
            idx_ready, copied2 = sem("idx_ready"), sem("copied")
            arrived2 = [sem(f"arrived{b}") for b in range(2)]
            w_in, hid, gelud, y_made, y_taken, up_done = (sem(n) for n in ("w_in", "hid", "gelud", "y_made", "y_taken", "up_done"))
            x_in = [sem(f"x_in{i}") for i in range(2)]
            y_out = [sem(f"y_out{u}") for u in range(YT)]
            paced, sp_paced = sem("paced"), sem("sp_paced")

            @block.gpsimd
            def _(pool):
                bound = pool.to_reg(NP - 1)

                def body(k):
                    for b in range(2):
                        pool.wait_ge(idx_ready, 2 * k + b + 1)
                        wait(pool, copied2, 2 * k + b - 1)
                        pool.sem_inc(paced, 1)
                        for r in range(b * U, b * U + U):
                            pool.indirect_dma_start(
                                out=fetched2[:, r, :], out_offset=None, in_=table2[:, :],
                                in_offset=bass.IndirectOffsetOnAxis(ap=idx2[:, r:r + 1], axis=0),
                                bounds_check=bound, oob_is_err=False).then_inc(arrived2[b], 16)
                turns(pool, S2 // RING, body)

            @block.vector
            def _(dve):
                dve.tensor_copy(idx2[:, 0:U], idx2_all[:, 0:U]).then_inc(idx_ready, 1)
                dve.tensor_copy(idx2[:, U:RING], idx2_all[:, U:RING]).then_inc(idx_ready, 1)

                def body(k):
                    for b in range(2):
                        half = slice(b * U, b * U + U)
                        dve.wait_ge(arrived2[b], (k + 1) * (16 * U))
                        dve.tensor_copy(idx2[:, half], idx2_all[:, bass.ds(k * RING + (RING + b * U), U)]).then_inc(idx_ready, 1)
                        dve.tensor_copy(edge[:, bass.ds(k * RING + b * U, U), :], fetched2[:, half, 0:EW]).then_inc(copied2, 1)
                turns(dve, S2 // RING, body)
                dve.wait_ge(copied2, 2 * (S2 // RING))

            @block.sync
            def _(sp):
                sp.dma_start(W1_sb, W1.rearrange("e (k p) f -> p (e k) f", p=P)).then_inc(w_in, 16)
                sp.dma_start(W2_sb, W2.rearrange("e (c p) d -> p (e c) d", p=P)).then_inc(w_in, 16)
                with nc.allow_non_contiguous_dma("biases, one word a row"):
                    for e in range(NE):
                        sp.dma_start(b1_sb[:, e, :], b1[e].rearrange("(c p) -> p c", p=P)).then_inc(w_in, 16)
                sp.dma_start(b2_sb[0:1, :, :], b2.rearrange("(a e) d -> a e d", a=1)).then_inc(w_in, 16)

                def fetch(t, s):
                    wait(sp, up_done, t - 1)
                    sp.sem_inc(sp_paced, 1)
                    sp.dma_start(xT[:, s * KD:(s + 1) * KD, :], xT_dram[:, :, bass.ds(t * GN, GN)]).then_inc(x_in[s], 16)

                fetch(0, 0)

                def one(t, s, k):
                    if not (isinstance(t, int) and t == G7 - 1):
                        fetch(t + 1, 1 - s)
                    for e in range(NE):
                        for u in range(YT):
                            sp.wait_ge(y_taken, t * (NE * YT) + (e * YT + u + 1))
                            sp.sem_inc(sp_paced, 1)
                            sp.dma_start(y_dram[e, bass.ds(t * GN + u * P, P), :], y_ring[:, u, :]).then_inc(y_out[u], 16)
                groups(sp, one)
                for u in range(YT):
                    sp.wait_ge(y_out[u], 16 * G7 * NE)

            @block.tensor
            def _(pe):
                pe.wait_ge(w_in, 16 * (3 + NE))

                def up(t, s, k, e):
                    if e == 0:
                        pe.wait_ge(x_in[s], (k + 1) * 16)
                    for i in range(HT):
                        fc, half = i // 2, i % 2
                        wait(pe, gelud, t * (NE * HT) + (e * HT + i - 3))
                        for c in range(KD):
                            last = pe.matmul(psum_H[:, i % 4, :], W1_sb[:, e * KD + c, fc * P:(fc + 1) * P],
                                             xT[:, s * KD + c, half * HN:(half + 1) * HN], start=c == 0, stop=c == KD - 1)
                        last.then_inc(hid, 1)

                def down(t, s, k, e):
                    pe.wait_ge(gelud, t * (NE * HT) + (e + 1) * HT)
                    for u in range(YT):
                        wait(pe, y_taken, t * (NE * YT) + (e * YT + max(u - 3, 0)))
                        for fc in range(FC):
                            pe.matmul(psum_Y[:, u % 4, :], hh[:, (e % 2) * FC + fc, u * P:(u + 1) * P], W2_sb[:, e * FC + fc, :],
                                      start=fc == 0, stop=False)
                        last = pe.matmul(psum_Y[:, u % 4, :], ones[0:1, :], b2_sb[0:1, e, :], start=False, stop=True)
                        last.then_inc(y_made, 1)

                def one(t, s, k):
                    up(t, s, k, 0)
                    for e in range(NE):
                        if e + 1 < NE:
                            up(t, s, k, e + 1)
                        down(t, s, k, e)
                    pe.sem_inc(up_done, 1)
                groups(pe, one)

            @block.scalar
            def _(act):
                act.wait_ge(w_in, 16 * (3 + NE))

                def gelu(t, e):
                    wait(act, y_made, t * (NE * YT) + (e - 1) * YT)
                    for i in range(HT):
                        fc, half = i // 2, i % 2
                        act.wait_ge(hid, t * (NE * HT) + (e * HT + i + 1))
                        act.activation(hh[:, (e % 2) * FC + fc, half * HN:(half + 1) * HN], psum_H[:, i % 4, :], ACT.Gelu,
                                       bias=b1_sb[:, e, fc:fc + 1]).then_inc(gelud, 1)

                def one(t, s, k):
                    gelu(t, 0)
                    for e in range(NE):
                        if e + 1 < NE:
                            gelu(t, e + 1)
                        for u in range(YT):
                            wait(act, y_out[u], t * (16 * NE) + 16 * e)
                            act.wait_ge(y_made, t * (NE * YT) + (e * YT + u + 1))
                            act.copy(y_ring[:, u, :], psum_Y[:, u % 4, :]).then_inc(y_taken, 1)
                groups(act, one)

        def segment_scan(tag, width, data, result, gate, op0, neutral):
            with stage_of() as block:
                scanned, turned, combined, back = (sem(f"{n}{tag}") for n in ("scanned", "turned", "combined", "back"))
                ends, gates_ = end_cols[:, 0, 0:width], end_cols[:, 1, 0:width]
                T1, T2 = psum[0:width, 0, 0:P], psum[0:width, 1, 0:P]
                R1, R2, R3, R4 = (carry_rows[0:width, i, :] for i in range(4))
                TB = psum[:, 2, 0:width]

                @block.vector
                def _(dve):
                    for f in range(width):
                        last = dve.tensor_tensor_scan(result(f), gate, data(f), neutral, op0[0], op0[1])
                    dve_step.done(last, dve)
                    for f in range(width):
                        dve.tensor_copy(ends[:, f:f + 1], result(f)[:, S2 - 1:S2])
                        if neutral == 0.0:
                            last = dve.tensor_copy(gates_[:, f:f + 1], all_same)
                        else:
                            last = dve.tensor_scalar(gates_[:, f:f + 1], all_same, 1.0, BIG, ALU.subtract, ALU.mult)
                    last.then_inc(scanned, 1)
                    dve.wait_ge(turned, 1)
                    dve.tensor_copy(R1, T1)
                    dve_step.done(dve.tensor_copy(R2, T2), dve)
                    dve_step.done(dve.tensor_tensor_scan(R3, R2, R1, neutral, op0[0], op0[1]), dve)
                    dve_step.done(dve.memset(R4, neutral), dve)
                    dve.tensor_copy(R4[:, 1:P], R3[:, 0:P - 1]).then_inc(combined, 1)
                    dve.wait_ge(back, 1)
                    dve_step.done(dve.tensor_copy(ends, TB), dve)
                    for f in range(width):
                        last = dve.tensor_tensor_scan(result(f), gate, data(f), ends[:, f:f + 1], op0[0], op0[1])
                    dve_step.done(last, dve)

                @block.tensor
                def _(pe):
                    pe.wait_ge(scanned, 1)
                    pe.transpose(T1, ends, ident[:, :])
                    pe.transpose(T2, gates_, ident[:, :]).then_inc(turned, 1)
                    pe.wait_ge(combined, 1)
                    pe.transpose(TB, R4, ident[0:width, 0:width]).then_inc(back, 1)

        def column(t, f):
            return t[:, :, f:f + 1].rearrange("p c a -> p (c a)")

        def node_rows(tag, tensor, to, rows, scatter):
            with stage_of() as block:
                moved = sem(f"node_moved{tag}")

                @block.gpsimd
                def _(pool):
                    bound = pool.to_reg(P * S2 - 1)
                    for n in range(NB):
                        off = bass.IndirectOffsetOnAxis(ap=rows[:, n:n + 1], axis=0)
                        if scatter:
                            pool.indirect_dma_start(out=tensor[:, :], out_offset=off, in_=to[:, n, :], in_offset=None,
                                                    bounds_check=bound, oob_is_err=False).then_inc(moved, 16)
                        else:
                            pool.indirect_dma_start(out=to[:, n, :], out_offset=None, in_=tensor[:, :], in_offset=off,
                                                    bounds_check=bound, oob_is_err=False).then_inc(moved, 16)
                    pool.wait_ge(moved, 16 * NB)

        def move(tag, to, of):
            with stage_of() as block:
                moved = sem(f"moved{tag}")

                @block.sync
                def _(sp):
                    sp.dma_start(to, of).then_inc(moved, 16)
                    sp.wait_ge(moved, 16)

        segment_scan("_max", H, lambda f: column(edge, HE + f), lambda f: column(maxed, f), apart, (ALU.add, ALU.max), -BIG)
        move("_max", maxes.rearrange("(p c) f -> p c f", c=S2), maxed)
        node_rows("_max", maxes, node_max, last_row, False)

        with stage_of() as block:
            @block.vector
            def _(dve):
                a_src, a_dst = node_feat[:, :, HE:HE + H], node_feat[:, :, HE + H:HE + 2 * H]
                dve.tensor_copy(node_pay[:, :, 0:H], a_dst)
                dve_step.done(dve.tensor_tensor(node_max, node_max, a_src, ALU.max), dve)
                dve_step.done(dve.tensor_tensor(node_tmp, node_max, a_dst, ALU.add), dve)
                dve_step.done(dve.scalar_tensor_tensor(node_pay[:, :, H:2 * H], node_tmp, 0.2, node_tmp, ALU.mult, ALU.max), dve)
        node_rows("_pay", spread, node_pay, first_row, True)
        move("_pay", far, spread.rearrange("(p c) f -> p c f", c=S2))

        segment_scan("_far0", H, lambda f: column(far, f), lambda f: column(score, f), same, (ALU.mult, ALU.add), 0.0)
        segment_scan("_far1", H, lambda f: column(far, H + f), lambda f: column(maxed, f), same, (ALU.mult, ALU.add), 0.0)

        with stage_of() as block:
            raw_ready, exp_ready = sem("raw_ready"), sem("exp_ready")

            @block.vector
            def _(dve):
                a_src = edge[:, :, HE:HE + H]
                dve_step.done(dve.tensor_tensor(score, score, a_src, ALU.add), dve)
                dve_step.done(dve.scalar_tensor_tensor(far[:, :, 0:H], score, 0.2, score, ALU.mult, ALU.max), dve)
                dve.tensor_tensor(score, far[:, :, 0:H], maxed, ALU.subtract).then_inc(raw_ready, 1)
                dve.wait_ge(exp_ready, 1)
                for h in range(H):
                    part_ = edge[:, :, h * NE:(h + 1) * NE]
                    dve.tensor_tensor(part_, part_, score[:, :, h:h + 1].to_broadcast([P, S2, NE]), ALU.mult)
                dve_step.done(dve.tensor_copy(edge[:, :, HE:HE + H], score), dve)

            @block.scalar
            def _(act):
                act.wait_ge(raw_ready, 1)
                act.activation(score, score, ACT.Exp).then_inc(exp_ready, 1)


        for part_no, (f0, f1) in enumerate(((0, 8), (8, 16), (16, 20))):
            w = f1 - f0
            tgt = far if w == 8 else score
            segment_scan(f"_sum{part_no}", w, lambda f, f0=f0: column(edge, f0 + f), lambda f, tgt=tgt: column(tgt, f),
                         same, (ALU.mult, ALU.add), 0.0)
            with stage_of() as block:
                @block.vector
                def _(dve, f0=f0, f1=f1, tgt=tgt, w=w):
                    dve_step.done(dve.tensor_copy(edge[:, :, f0:f1], tgt[:, :, 0:w]), dve)
        move("_sum", sums.rearrange("(p c) f -> p c f", c=S2), edge)
        node_rows("_sum", sums, node_sum, last_row, False)

        with stage_of() as block:
            s_raw, s_exp, s_var, s_root = sem("s_raw"), sem("s_exp"), sem("s_var"), sem("s_root")
            a_src, a_dst = node_feat[:, :, HE:HE + H], node_feat[:, :, HE + H:HE + 2 * H]
            agg = node_sum[:, :, 0:HE]
            sc = node_tmp2

            @block.vector
            def _(dve):
                def do(ins):
                    dve_step.done(ins, dve)

                do(dve.tensor_tensor(node_tmp, a_src, a_dst, ALU.add))
                do(dve.scalar_tensor_tensor(node_tmp2, node_tmp, 0.2, node_tmp, ALU.mult, ALU.max))
                dve.tensor_tensor(node_tmp, node_tmp2, node_pay[:, :, H:2 * H], ALU.subtract).then_inc(s_raw, 1)
                dve.wait_ge(s_exp, 1)
                for h in range(H):
                    last = dve.tensor_tensor(node_big[:, :, h * NE:(h + 1) * NE], node_feat[:, :, h * NE:(h + 1) * NE],
                                             node_tmp[:, :, h:h + 1].to_broadcast([P, NB, NE]), ALU.mult)
                do(last)
                do(dve.tensor_tensor(agg, agg, node_big, ALU.add))
                do(dve.tensor_tensor(node_tmp2, node_sum[:, :, HE:EW], node_tmp, ALU.add))
                do(dve.tensor_scalar(node_tmp2, node_tmp2, 1e-16, None, ALU.add))
                do(dve.reciprocal(node_tmp, node_tmp2))
                for h in range(H):
                    last = dve.tensor_tensor(agg[:, :, h * NE:(h + 1) * NE], agg[:, :, h * NE:(h + 1) * NE],
                                             node_tmp[:, :, h:h + 1].to_broadcast([P, NB, NE]), ALU.mult)
                do(last)
                do(dve.tensor_tensor(agg, agg, vecs[:, 0:1, :].to_broadcast([P, NB, HE]), ALU.add))
                do(dve.tensor_reduce(nt1, agg, AX.X, ALU.add))
                do(dve.tensor_scalar(nt1, nt1, 1.0 / HE, None, ALU.mult))
                do(dve.tensor_tensor(agg, agg, nt1.rearrange("p (n a) -> p n a", a=1).to_broadcast([P, NB, HE]), ALU.subtract))
                do(dve.tensor_tensor(node_big, agg, agg, ALU.mult))
                do(dve.tensor_reduce(nt1, node_big, AX.X, ALU.add))
                dve.tensor_scalar(nt1, nt1, 1.0 / HE, EPS, ALU.mult, ALU.add).then_inc(s_var, 1)
                dve.wait_ge(s_root, 1)
                do(dve.reciprocal(nt2, nt1))
                do(dve.tensor_tensor(agg, agg, nt2.rearrange("p (n a) -> p n a", a=1).to_broadcast([P, NB, HE]), ALU.mult))
                do(dve.tensor_tensor(agg, agg, vecs[:, 1:2, :].to_broadcast([P, NB, HE]), ALU.mult))
                do(dve.tensor_tensor(agg, agg, vecs[:, 2:3, :].to_broadcast([P, NB, HE]), ALU.add))
                do(dve.tensor_reduce(sc, agg.rearrange("p n (h e) -> p n e h", h=H), AX.X, ALU.add))
                do(dve.tensor_scalar(sc, sc, 1.0 / H, None, ALU.mult))
                place_ = node_pay[:, :, 0:NE]
                do(dve.memset(place_, 0.0))
                for e in range(NE):
                    for o in range(NE):
                        if o != e:
                            do(dve.tensor_tensor(node_tmp[:, :, 0:1], sc[:, :, o:o + 1], sc[:, :, e:e + 1],
                                                 ALU.is_ge if o < e else ALU.is_gt))
                            do(dve.tensor_tensor(place_[:, :, e:e + 1], place_[:, :, e:e + 1], node_tmp[:, :, 0:1], ALU.add))
                do(dve.tensor_scalar(place_, place_, 1.5, None, ALU.is_lt))
                do(dve.tensor_reduce(nt1, sc, AX.X, ALU.max))
                dve.tensor_tensor(sc, sc, nt1.rearrange("p (n a) -> p n a", a=1).to_broadcast([P, NB, NE]), ALU.subtract).then_inc(s_raw, 1)
                dve.wait_ge(s_exp, 2)
                do(dve.tensor_tensor(gates[:, :, :], sc, place_, ALU.mult))
                do(dve.tensor_reduce(nt1, gates[:, :, :], AX.X, ALU.add))
                do(dve.reciprocal(nt2, nt1))
                do(dve.tensor_tensor(gates[:, :, :], gates[:, :, :], nt2.rearrange("p (n a) -> p n a", a=1).to_broadcast([P, NB, NE]), ALU.mult))

            @block.scalar
            def _(act):
                act.wait_ge(s_raw, 1)
                act.activation(node_tmp, node_tmp, ACT.Exp).then_inc(s_exp, 1)
                act.wait_ge(s_var, 1)
                act.activation(nt1, nt1, ACT.Sqrt).then_inc(s_root, 1)
                act.wait_ge(s_raw, 2)
                act.activation(sc, sc, ACT.Exp).then_inc(s_exp, 1)

        place = Place()
        ya = place([2 * SO, D])
        ye = place([2 * NE * SO, D])
        gate_ring = place([2 * SO, NE])
        out_v = out[0:(NB - 1) * P, :].rearrange("(b p) f -> p b f", p=P)
        x1_v = x1_dram.rearrange("(b p) f -> p b f", p=P)
        with stage_of() as block:
            added, paced = sem("added"), sem("paced")
            y_in, y_out = ([sem(f"{n}{i}") for i in range(2)] for n in ("y_in", "y_out"))
            A = NE * SO
            PARTS = 1 + NE

            @block.sync
            def _(sp):
                def fetch(t, s, k):
                    wait(sp, y_out[s], k * 16)
                    sp.sem_inc(paced, 1)
                    sp.dma_start(ya[:, s * SO:(s + 1) * SO, :], x1_v[:, bass.ds(t * SO, SO), :]).then_inc(y_in[s], 16)
                    for e in range(NE):
                        sp.dma_start(ye[:, (s * NE + e) * SO:(s * NE + e + 1) * SO, :],
                                     y_dram[e].rearrange("(b p) f -> p b f", p=P)[:, bass.ds(t * SO, SO), :]).then_inc(y_in[s], 16)

                def store(t, s, k):
                    sp.wait_ge(added, (t + 1) * A)
                    sp.sem_inc(paced, 1)
                    sp.dma_start(out_v[:, bass.ds(t * SO, SO), :], ya[:, s * SO:(s + 1) * SO, :]).then_inc(y_out[s], 16)

                def body(k, last):
                    store(2 * k, 0, k)
                    fetch(2 * k + 2, 0, k + 1)
                    store(2 * k + 1, 1, k)
                    if not last:
                        fetch(2 * k + 3, 1, k + 1)
                fetch(0, 0, 0)
                fetch(1, 1, 0)
                turns_ahead(sp, PAIRS, body)
                sp.wait_ge(added, G7 * A)
                sp.dma_start(out_v[:, (G7 - 1) * SO:NB - 1, :], ya[:, 0:SO - 1, :]).then_inc(y_out[0], 16)
                sp.dma_start(out[(NB - 1) * P:N, :], ya[0:N - (NB - 1) * P, SO - 1, :]).then_inc(y_out[1], 16)
                for s in range(2):
                    sp.wait_ge(y_out[s], 16 * (PAIRS + 1))

            @block.vector
            def _(dve):
                def one(t, s, k):
                    dve.wait_ge(y_in[s], (k + 1) * (16 * PARTS))
                    cut = slice(s * SO, (s + 1) * SO)
                    dve_step.done(dve.tensor_copy(gate_ring[:, cut, :], gates[:, bass.ds(t * SO, SO), :]), dve)
                    for e in range(NE):
                        for u in range(SO):
                            wait(dve, added, t * A + (e * SO + u - (SO - 1)))
                            to = ya[:, s * SO + u, :]
                            dve.scalar_tensor_tensor(to, ye[:, (s * NE + e) * SO + u, :], gate_ring[:, s * SO + u, e:e + 1], to,
                                                     ALU.mult, ALU.add).then_inc(added, 1)
                groups(dve, one, [dve_step], [2])


_INS = ['x', 'src', 'dst', 'L0_gnn_W1', 'L0_gnn_b1', 'L0_gnn_W2', 'L0_gnn_b2', 'L0_gnn_W3', 'L0_gnn_b3',
        'L0_ffn_W_gat', 'L0_ffn_att_src', 'L0_ffn_att_dst', 'L0_ffn_b_gat', 'L0_ffn_ln_gamma', 'L0_ffn_ln_beta',
        'L0_ffn_W1', 'L0_ffn_b1', 'L0_ffn_W2', 'L0_ffn_b2', 'L0_ffn_edge_index']


def build(nc, a, out):
    gnn_moe_kernel(nc, a['x'], a['src'], a['dst'],
                   [a[f'L0_gnn_W{i}'] for i in (1, 2, 3)], [a[f'L0_gnn_b{i}'] for i in (1, 2, 3)],
                   a['L0_ffn_W_gat'], a['L0_ffn_att_src'], a['L0_ffn_att_dst'], a['L0_ffn_b_gat'],
                   a['L0_ffn_ln_gamma'], a['L0_ffn_ln_beta'], a['L0_ffn_W1'], a['L0_ffn_b1'],
                   a['L0_ffn_W2'], a['L0_ffn_b2'], a['L0_ffn_edge_index'], out)


def kernel(**inputs):
    import numpy as _np
    import concourse.bacc as _bacc
    from concourse import mybir as _mybir
    from concourse.bass_utils import run_bass_kernel_spmd as _run

    nc = _bacc.Bacc("TRN2", target_bir_lowering=False, num_devices=1)
    arrays, args = {}, {}
    for name in _INS:
        a = _np.ascontiguousarray(inputs[name])
        arrays[f"in_{name}_dram"] = a
        args[name] = nc.dram_tensor(f"in_{name}_dram", a.shape, _mybir.dt.from_np(a.dtype), kind="ExternalInput").ap()
    out = nc.dram_tensor("out_0_dram", inputs['x'].shape, _mybir.dt.float32, kind="ExternalOutput").ap()
    build(nc, args, out)
    r = _run(nc, [arrays], core_ids=[0])
    return r.results[0]["out_0_dram"]
```
